# Optimizing a Trainium2 kernel written in Bass

```python
import numpy as np
import jax
import jax.numpy as jnp

def _softmax(x, axis=-1):
    return jax.nn.softmax(x, axis=axis)

def _gelu(x):
    return jax.nn.gelu(x, approximate=True)

def _silu(x):
    return jax.nn.silu(x)

def _sigmoid(x):
    return jax.nn.sigmoid(x)

def _layernorm(x, axis=-1, eps=1e-05):
    m = jnp.mean(x, axis=axis, keepdims=True)
    v = jnp.var(x, axis=axis, keepdims=True)
    return (x - m) / jnp.sqrt(v + eps)

def _scatter_add(tgt, idx, src, axis=0):
    return tgt.at[idx].add(src)

def _segment_sum(src, seg, n):
    return jax.ops.segment_sum(src, seg, n)
kernel_name = 'mk_xattn_ffn_d4_seqx_r8_79115f'

def setup_inputs(seed: int=0):
    np.random.seed(seed)
    _w = jnp.asarray

    def _rec_inputs():
        import jax
        import jax.numpy as jnp
        _rk = jax.random.key(seed)
        x = 7.22e-05 + 1 * jax.random.normal(jax.random.fold_in(_rk, 1), (4, 512, 128), jnp.float32)
        _lenS = 512 - jax.random.randint(jax.random.fold_in(_rk, 7), (4,), 0, max(1, 512 // 4) + 1, jnp.int32)
        _lenS2 = 154 - jax.random.randint(jax.random.fold_in(_rk, 8), (4,), 0, max(1, 154 // 4) + 1, jnp.int32)
        _ctx_1024P = jax.random.normal(jax.random.fold_in(_rk, 11), (4, 16, 128), jnp.float32)
        _ctx_1024c = jax.random.dirichlet(jax.random.fold_in(_rk, 511), 0.3 * jnp.ones((16,), jnp.float32), (4, 154))
        _ctx_1024t = jnp.einsum('bsk,bkd->bsd', _ctx_1024c, _ctx_1024P)
        _ctx_1024t = _ctx_1024t * jax.lax.rsqrt(jnp.mean(jnp.square(_ctx_1024t)) + 1e-12) * 0.953939
        ctx_1024 = -0.000514642 + 1.00011 * (_ctx_1024t + 0.3 * jax.random.normal(jax.random.fold_in(_rk, 611), (4, 154, 128), jnp.float32))
        _validS = jnp.arange(512)[None, :] < _lenS[:, None]
        _validS2 = jnp.arange(154)[None, :] < _lenS2[:, None]
        _causal = jnp.tril(jnp.ones((512, 512), dtype=bool))
        mask_Bx1xSxS2_if1 = jnp.where(jnp.ones((4, 1, 512, 154), dtype=bool), 1, 0).astype(jnp.int32)
        return (x, ctx_1024, mask_Bx1xSxS2_if1)
    x, ctx_1024, mask_Bx1xSxS2_if1 = _rec_inputs()

    def _L0_xattn_setup():
        import jax, jax.numpy as jnp
        import numpy as np
        B, L_ENC, L_DEC, D = (16, 64, 128, 128)
        key = jax.random.key(seed)
        k1, k2, k3, k4, k5, k6 = jax.random.split(key, 6)
        encoder_hc = jax.random.normal(k1, (B, L_ENC, D), dtype=jnp.float32)
        decoder_hq = jax.random.normal(k2, (B, L_DEC, D), dtype=jnp.float32)
        w_sim = jax.random.normal(k3, (3 * D,), dtype=jnp.float32) * 0.02
        b_sim = jax.random.normal(k4, (1,), dtype=jnp.float32) * 0.02
        W_qv = jax.random.normal(k5, (4 * D, D), dtype=jnp.float32) * 0.02
        b_qv = jax.random.normal(k6, (D,), dtype=jnp.float32) * 0.02
        return {'encoder_hc': encoder_hc, 'decoder_hq': decoder_hq, 'w_sim': w_sim, 'b_sim': b_sim, 'W_qv': W_qv, 'b_qv': b_qv}
    _L0_xattn_all = _L0_xattn_setup()
    _L0_xattn_in = {k: v for k, v in _L0_xattn_all.items() if k in ('w_sim', 'b_sim', 'W_qv', 'b_qv')}
    del _L0_xattn_all

    def _L0_ffn_setup():
        import jax, jax.numpy as jnp
        import numpy as np
        NUM_EXPERTS = 8
        TOP_K = 2
        D_MODEL = 128
        D_HID = 512
        BATCH, SEQ = (2, 256)
        key = jax.random.key(seed)
        ks = jax.random.split(key, 5)
        s = 0.02
        return {'x': jax.random.normal(ks[0], (BATCH, SEQ, D_MODEL), dtype=jnp.float32), 'Wg': jax.random.normal(ks[1], (D_MODEL, NUM_EXPERTS), dtype=jnp.float32) * s, 'bg': jnp.zeros((NUM_EXPERTS,), dtype=jnp.float32), 'W0': jax.random.normal(ks[2], (NUM_EXPERTS, D_MODEL, D_HID), dtype=jnp.float32) * s, 'b0': jnp.zeros((NUM_EXPERTS, D_HID), dtype=jnp.float32), 'W1': jax.random.normal(ks[3], (NUM_EXPERTS, D_MODEL, D_HID), dtype=jnp.float32) * s, 'b1': jnp.zeros((NUM_EXPERTS, D_HID), dtype=jnp.float32), 'W2': jax.random.normal(ks[4], (NUM_EXPERTS, D_HID, D_MODEL), dtype=jnp.float32) * s, 'b2': jnp.zeros((NUM_EXPERTS, D_MODEL), dtype=jnp.float32)}
    _L0_ffn_all = _L0_ffn_setup()
    _L0_ffn_in = {k: v for k, v in _L0_ffn_all.items() if k in ('Wg', 'bg', 'W0', 'b0', 'W1', 'b1', 'W2', 'b2')}
    del _L0_ffn_all

    def _L1_xattn_setup():
        import jax, jax.numpy as jnp
        import numpy as np
        HEADS = 16
        key = jax.random.key(seed)
        ks = jax.random.split(key, 8)
        N, S, E = (2, 256, 128)
        D = E // HEADS
        return {'values': jax.random.normal(ks[0], (N, S, E), jnp.float32), 'keys': jax.random.normal(ks[1], (N, S, E), jnp.float32), 'queries': jax.random.normal(ks[2], (N, S, E), jnp.float32), 'mask': jnp.ones((N, 1, S, S), jnp.int32), 'Wv': jax.random.normal(ks[3], (D, D), jnp.float32) * D ** (-0.5), 'Wk': jax.random.normal(ks[4], (D, D), jnp.float32) * D ** (-0.5), 'Wq': jax.random.normal(ks[5], (D, D), jnp.float32) * D ** (-0.5), 'Wo': jax.random.normal(ks[6], (E, E), jnp.float32) * E ** (-0.5), 'bo': jnp.zeros((E,), jnp.float32)}
    _L1_xattn_all = _L1_xattn_setup()
    _L1_xattn_in = {k: v for k, v in _L1_xattn_all.items() if k in ('Wv', 'Wk', 'Wq', 'Wo', 'bo')}
    del _L1_xattn_all

    def _L1_ffn_setup():
        import jax, jax.numpy as jnp
        import numpy as np
        CAPACITY_FACTOR = 1.25
        key = jax.random.key(seed)
        k1, k2, k3, k4 = jax.random.split(key, 4)
        B, T, D, F, E = (4, 512, 128, 512, 8)
        s = 0.02
        return {'x': jax.random.normal(k1, (B, T, D), dtype=jnp.float32), 'wg': jax.random.normal(k2, (D, E), dtype=jnp.float32) * s, 'W1': jax.random.normal(k3, (E, D, F), dtype=jnp.float32) * s, 'b1': jnp.zeros((E, F), dtype=jnp.float32), 'W2': jax.random.normal(k4, (E, F, D), dtype=jnp.float32) * s, 'b2': jnp.zeros((E, D), dtype=jnp.float32)}
    _L1_ffn_all = _L1_ffn_setup()
    _L1_ffn_in = {k: v for k, v in _L1_ffn_all.items() if k in ('wg', 'W1', 'b1', 'W2', 'b2')}
    del _L1_ffn_all

    def _L2_xattn_setup():
        import jax, jax.numpy as jnp
        import numpy as np
        DIM = 128
        NUM_HEADS = 16
        DIM_HEAD = 64
        INNER = NUM_HEADS * DIM_HEAD
        SCALE = DIM_HEAD ** (-0.5)

        def _layernorm(x, gamma, beta, eps=1e-05):
            mu = jnp.mean(x, axis=-1, keepdims=True)
            var = jnp.mean(jnp.square(x - mu), axis=-1, keepdims=True)
            return (x - mu) * jax.lax.rsqrt(var + eps) * gamma + beta
        key = jax.random.key(seed)
        ks = jax.random.split(key, 8)
        B, SQ, SK = (2, 256, 512)
        x = jax.random.normal(ks[0], (B, SQ, DIM), dtype=jnp.float32)
        context = jax.random.normal(ks[1], (B, SK, DIM), dtype=jnp.float32)
        ln_gamma = jnp.ones((DIM,), jnp.float32)
        ln_beta = jnp.zeros((DIM,), jnp.float32)
        w_q = jax.random.normal(ks[2], (DIM, INNER), dtype=jnp.float32) / np.sqrt(DIM)
        w_kv = jax.random.normal(ks[3], (DIM, 2 * INNER), dtype=jnp.float32) / np.sqrt(DIM)
        w_out = jax.random.normal(ks[4], (INNER, DIM), dtype=jnp.float32) / np.sqrt(INNER)
        b_out = jnp.zeros((DIM,), jnp.float32)
        gate = jnp.array([0.5], jnp.float32)
        return {'x': x, 'context': context, 'ln_gamma': ln_gamma, 'ln_beta': ln_beta, 'w_q': w_q, 'w_kv': w_kv, 'w_out': w_out, 'b_out': b_out, 'gate': gate}
    _L2_xattn_all = _L2_xattn_setup()
    _L2_xattn_in = {k: v for k, v in _L2_xattn_all.items() if k in ('ln_gamma', 'ln_beta', 'w_q', 'w_kv', 'w_out', 'b_out', 'gate')}
    del _L2_xattn_all

    def _L2_ffn_setup():
        import jax, jax.numpy as jnp
        import numpy as np
        TOP_K = 2
        key = jax.random.key(seed)
        k1, k2, k3, k4 = jax.random.split(key, 4)
        B, S, d, f, E = (4, 512, 128, 256, 8)
        x = jax.random.normal(k1, (B, S, d), dtype=jnp.float32)
        wg = jax.random.normal(k2, (d, E), dtype=jnp.float32) * 0.02
        w1 = jax.random.normal(k3, (E, d, f), dtype=jnp.float32) * 0.02
        w2 = jax.random.normal(k4, (E, f, d), dtype=jnp.float32) * 0.02
        return {'x': x, 'wg': wg, 'w1': w1, 'w2': w2}
    _L2_ffn_all = _L2_ffn_setup()
    _L2_ffn_in = {k: v for k, v in _L2_ffn_all.items() if k in ('wg', 'w1', 'w2')}
    del _L2_ffn_all

    def _L3_xattn_setup():
        import jax, jax.numpy as jnp
        import numpy as np
        HIDDEN = 128
        HEADS = 16
        HEAD_DIM = 64
        key = jax.random.key(seed)
        ks = jax.random.split(key, 7)
        B, Q, K = (2, 256, 512)
        s = 1.0 / np.sqrt(HIDDEN)
        return {'query': jax.random.normal(ks[0], (B, Q, HIDDEN), dtype=jnp.float32), 'key': jax.random.normal(ks[1], (B, K, HIDDEN), dtype=jnp.float32), 'value': jax.random.normal(ks[2], (B, K, HIDDEN), dtype=jnp.float32), 'w_q': jax.random.normal(ks[3], (HIDDEN, HEADS * HEAD_DIM), dtype=jnp.float32) * s, 'w_k': jax.random.normal(ks[4], (HIDDEN, HEADS * HEAD_DIM), dtype=jnp.float32) * s, 'w_v': jax.random.normal(ks[5], (HIDDEN, HEADS * HEAD_DIM), dtype=jnp.float32) * s, 'w_o': jax.random.normal(ks[6], (HEADS * HEAD_DIM, HIDDEN), dtype=jnp.float32) * s}
    _L3_xattn_all = _L3_xattn_setup()
    _L3_xattn_in = {k: v for k, v in _L3_xattn_all.items() if k in ('w_q', 'w_k', 'w_v', 'w_o')}
    del _L3_xattn_all

    def _L3_ffn_setup():
        import jax, jax.numpy as jnp
        import numpy as np
        N_EMBD = 128
        NUM_EXPERTS = 8
        TOP_K = 2
        D_FF = 4 * N_EMBD
        B, S = (4, 256)
        key = jax.random.key(seed)
        ks = jax.random.split(key, 7)
        scale = lambda fan_in: 1.0 / np.sqrt(fan_in)
        x = jax.random.normal(ks[0], (B, S, N_EMBD), dtype=jnp.float32)
        W_router = jax.random.normal(ks[1], (N_EMBD, NUM_EXPERTS), dtype=jnp.float32) * scale(N_EMBD)
        b_router = jnp.zeros((NUM_EXPERTS,), dtype=jnp.float32)
        W1 = jax.random.normal(ks[2], (NUM_EXPERTS, N_EMBD, D_FF), dtype=jnp.float32) * scale(N_EMBD)
        b1 = jnp.zeros((NUM_EXPERTS, D_FF), dtype=jnp.float32)
        W2 = jax.random.normal(ks[3], (NUM_EXPERTS, D_FF, N_EMBD), dtype=jnp.float32) * scale(D_FF)
        b2 = jnpp = jnp.zeros((NUM_EXPERTS, N_EMBD), dtype=jnp.float32)
        return {'x': x, 'W_router': W_router, 'b_router': b_router, 'W1': W1, 'b1': b1, 'W2': W2, 'b2': b2}
    _L3_ffn_all = _L3_ffn_setup()
    _L3_ffn_in = {k: v for k, v in _L3_ffn_all.items() if k in ('W_router', 'b_router', 'W1', 'b1', 'W2', 'b2')}
    del _L3_ffn_all
    return {'x': x, 'ctx_1024': ctx_1024, 'mask_Bx1xSxS2_if1': mask_Bx1xSxS2_if1, 'L0_xattn_w_sim': _L0_xattn_in['w_sim'], 'L0_xattn_b_sim': _L0_xattn_in['b_sim'], 'L0_xattn_W_qv': _L0_xattn_in['W_qv'], 'L0_xattn_b_qv': _L0_xattn_in['b_qv'], 'L0_ffn_Wg': _L0_ffn_in['Wg'], 'L0_ffn_bg': _L0_ffn_in['bg'], 'L0_ffn_W0': _L0_ffn_in['W0'], 'L0_ffn_b0': _L0_ffn_in['b0'], 'L0_ffn_W1': _L0_ffn_in['W1'], 'L0_ffn_b1': _L0_ffn_in['b1'], 'L0_ffn_W2': _L0_ffn_in['W2'], 'L0_ffn_b2': _L0_ffn_in['b2'], 'L1_xattn_Wv': _L1_xattn_in['Wv'], 'L1_xattn_Wk': _L1_xattn_in['Wk'], 'L1_xattn_Wq': _L1_xattn_in['Wq'], 'L1_xattn_Wo': _L1_xattn_in['Wo'], 'L1_xattn_bo': _L1_xattn_in['bo'], 'L1_ffn_wg': _L1_ffn_in['wg'], 'L1_ffn_W1': _L1_ffn_in['W1'], 'L1_ffn_b1': _L1_ffn_in['b1'], 'L1_ffn_W2': _L1_ffn_in['W2'], 'L1_ffn_b2': _L1_ffn_in['b2'], 'L2_xattn_ln_gamma': _L2_xattn_in['ln_gamma'], 'L2_xattn_ln_beta': _L2_xattn_in['ln_beta'], 'L2_xattn_w_q': _L2_xattn_in['w_q'], 'L2_xattn_w_kv': _L2_xattn_in['w_kv'], 'L2_xattn_w_out': _L2_xattn_in['w_out'], 'L2_xattn_b_out': _L2_xattn_in['b_out'], 'L2_xattn_gate': _L2_xattn_in['gate'], 'L2_ffn_wg': _L2_ffn_in['wg'], 'L2_ffn_w1': _L2_ffn_in['w1'], 'L2_ffn_w2': _L2_ffn_in['w2'], 'L3_xattn_w_q': _L3_xattn_in['w_q'], 'L3_xattn_w_k': _L3_xattn_in['w_k'], 'L3_xattn_w_v': _L3_xattn_in['w_v'], 'L3_xattn_w_o': _L3_xattn_in['w_o'], 'L3_ffn_W_router': _L3_ffn_in['W_router'], 'L3_ffn_b_router': _L3_ffn_in['b_router'], 'L3_ffn_W1': _L3_ffn_in['W1'], 'L3_ffn_b1': _L3_ffn_in['b1'], 'L3_ffn_W2': _L3_ffn_in['W2'], 'L3_ffn_b2': _L3_ffn_in['b2']}

def reference(x, ctx_1024, mask_Bx1xSxS2_if1, L0_xattn_w_sim, L0_xattn_b_sim, L0_xattn_W_qv, L0_xattn_b_qv, L0_ffn_Wg, L0_ffn_bg, L0_ffn_W0, L0_ffn_b0, L0_ffn_W1, L0_ffn_b1, L0_ffn_W2, L0_ffn_b2, L1_xattn_Wv, L1_xattn_Wk, L1_xattn_Wq, L1_xattn_Wo, L1_xattn_bo, L1_ffn_wg, L1_ffn_W1, L1_ffn_b1, L1_ffn_W2, L1_ffn_b2, L2_xattn_ln_gamma, L2_xattn_ln_beta, L2_xattn_w_q, L2_xattn_w_kv, L2_xattn_w_out, L2_xattn_b_out, L2_xattn_gate, L2_ffn_wg, L2_ffn_w1, L2_ffn_w2, L3_xattn_w_q, L3_xattn_w_k, L3_xattn_w_v, L3_xattn_w_o, L3_ffn_W_router, L3_ffn_b_router, L3_ffn_W1, L3_ffn_b1, L3_ffn_W2, L3_ffn_b2):
    import jax
    import jax.numpy as jnp

    def _L0_xattn_ref(encoder_hc, decoder_hq, w_sim, b_sim, W_qv, b_qv):
        import jax, jax.numpy as jnp
        import numpy as np
        B, L_ENC, L_DEC, D = (16, 64, 128, 128)
        d = encoder_hc.shape[-1]
        w1, w2, w3 = (w_sim[:d], w_sim[d:2 * d], w_sim[2 * d:])
        Sim = (encoder_hc @ w1)[:, :, None] + (decoder_hq @ w2)[:, None, :] + jnp.einsum('bid,bjd->bij', encoder_hc * w3, decoder_hq) + b_sim[0]
        A = jax.nn.softmax(Sim, axis=2)
        hq_hat = jnp.einsum('bij,bjd->bid', A, decoder_hq)
        Batt = jax.nn.softmax(jnp.max(Sim, axis=2), axis=1)
        hc_bar = jnp.einsum('bi,bid->bd', Batt, encoder_hc)[:, None, :]
        hc_hat = jnp.broadcast_to(hc_bar, encoder_hc.shape)
        feats = jnp.concatenate([encoder_hc, hq_hat, encoder_hc * hq_hat, encoder_hc * hc_hat], axis=-1)
        hcq = feats @ W_qv + b_qv
        return hcq

    def _L0_ffn_ref(x, Wg, bg, W0, b0, W1, b1, W2, b2):
        import jax, jax.numpy as jnp
        import numpy as np
        NUM_EXPERTS = 8
        TOP_K = 2
        D_MODEL = 128
        D_HID = 512
        BATCH, SEQ = (2, 256)
        n, s, d = x.shape
        gate_logits = x @ Wg + bg
        top_vals, top_idx = jax.lax.top_k(gate_logits, TOP_K)
        w = jax.nn.softmax(top_vals, axis=-1)
        combine = jnp.sum(jax.nn.one_hot(top_idx, NUM_EXPERTS, dtype=x.dtype) * w[..., None], axis=-2)
        xf = x.reshape(n * s, d)
        h = jnp.einsum('td,edh->eth', xf, W0) + b0[:, None, :]
        g = jax.nn.silu(jnp.einsum('td,edh->eth', xf, W1) + b1[:, None, :])
        y = jnp.einsum('eth,ehd->etd', h * g, W2) + b2[:, None, :]
        out = jnp.einsum('te,etd->td', combine.reshape(n * s, NUM_EXPERTS), y)
        return out.reshape(n, s, d)

    def _L1_xattn_ref(values, keys, queries, mask, Wv, Wk, Wq, Wo, bo):
        import jax, jax.numpy as jnp
        import numpy as np
        HEADS = 16
        N, Sq, E = queries.shape
        H = HEADS
        D = E // H
        v = values.reshape(N, -1, H, D)
        k = keys.reshape(N, -1, H, D)
        q = queries.reshape(N, Sq, H, D)
        v = jnp.einsum('nlhd,od->nlho', v, Wv)
        k = jnp.einsum('nlhd,od->nlho', k, Wk)
        q = jnp.einsum('nqhd,od->nqho', q, Wq)
        energy = jnp.einsum('nqhd,nkhd->nhqk', q, k)
        energy = jnp.where(mask == 0, jnp.float32(-1e+20), energy)
        attn = jax.nn.softmax(energy * (1.0 / E ** 0.5), axis=3)
        out = jnp.einsum('nhqk,nkhd->nqhd', attn, v).reshape(N, Sq, E)
        return out @ Wo.T + bo

    def _L1_ffn_ref(x, wg, W1, b1, W2, b2):
        import jax, jax.numpy as jnp
        import numpy as np
        CAPACITY_FACTOR = 1.25
        B, T, D = x.shape
        E = wg.shape[1]
        N = B * T
        capacity = int(N / E * CAPACITY_FACTOR) + 1
        xf = x.reshape(N, D)
        logits = xf @ wg
        scores = jax.nn.softmax(logits, axis=-1)
        top1 = jnp.argmax(scores, axis=-1)
        combine_w = jnp.take_along_axis(scores, top1[:, None], axis=1)[:, 0]
        oh = jax.nn.one_hot(top1, E, dtype=jnp.int32)
        rank = jnp.take_along_axis(jnp.cumsum(oh, axis=0), top1[:, None], axis=1)[:, 0] - 1
        valid = rank < capacity
        trash = E * capacity
        slot = jnp.where(valid, top1 * capacity + rank, trash)
        buf = jnp.zeros((E * capacity + 1, D), dtype=x.dtype).at[slot].set(xf)
        eb = buf[:E * capacity].reshape(E, capacity, D)
        h = jax.nn.gelu(jnp.einsum('ecd,edf->ecf', eb, W1) + b1[:, None, :], approximate=False)
        y = jnp.einsum('ecf,efd->ecd', h, W2) + b2[:, None, :]
        yf = y.reshape(E * capacity, D)
        gathered = yf[jnp.minimum(slot, E * capacity - 1)]
        out_flat = jnp.where(valid[:, None], gathered, 0.0) * combine_w[:, None]
        return out_flat.reshape(B, T, D)

    def _L2_xattn_ref(x, context, ln_gamma, ln_beta, w_q, w_kv, w_out, b_out, gate):
        import jax, jax.numpy as jnp
        import numpy as np
        DIM = 128
        NUM_HEADS = 16
        DIM_HEAD = 64
        INNER = NUM_HEADS * DIM_HEAD
        SCALE = DIM_HEAD ** (-0.5)

        def _layernorm(x, gamma, beta, eps=1e-05):
            mu = jnp.mean(x, axis=-1, keepdims=True)
            var = jnp.mean(jnp.square(x - mu), axis=-1, keepdims=True)
            return (x - mu) * jax.lax.rsqrt(var + eps) * gamma + beta
        B, SQ, _ = x.shape
        SK = context.shape[1]
        xn = _layernorm(x, ln_gamma, ln_beta)
        q = (xn @ w_q).reshape(B, SQ, NUM_HEADS, DIM_HEAD)
        kv = context @ w_kv
        k, v = jnp.split(kv, 2, axis=-1)
        k = k.reshape(B, SK, NUM_HEADS, DIM_HEAD)
        v = v.reshape(B, SK, NUM_HEADS, DIM_HEAD)
        scores = jnp.einsum('bqhd,bkhd->bhqk', q * SCALE, k)
        attn = jax.nn.softmax(scores, axis=-1)
        out = jnp.einsum('bhqk,bkhd->bqhd', attn, v).reshape(B, SQ, INNER)
        out = out @ w_out + b_out
        return out * jnp.tanh(gate[0])

    def _L2_ffn_ref(x, wg, w1, w2):
        import jax, jax.numpy as jnp
        import numpy as np
        TOP_K = 2
        B, S, d = x.shape
        E = wg.shape[1]
        xt = x.reshape(-1, d)
        T = xt.shape[0]
        gate_logits = xt @ wg
        top_vals, top_idx = jax.lax.top_k(gate_logits, TOP_K)
        weights = jax.nn.softmax(top_vals.astype(jnp.float32), axis=-1).astype(x.dtype)
        combine = jnp.zeros((T, E), dtype=x.dtype).at[jnp.arange(T)[:, None], top_idx].add(weights)
        h = jax.nn.gelu(jnp.einsum('td,edf->etf', xt, w1), approximate=False)
        y = jnp.einsum('etf,efd->etd', h, w2)
        out = jnp.einsum('te,etd->td', combine, y)
        return out.reshape(B, S, d)

    def _L3_xattn_ref(query, key, value, w_q, w_k, w_v, w_o):
        import jax, jax.numpy as jnp
        import numpy as np
        HIDDEN = 128
        HEADS = 16
        HEAD_DIM = 64
        B, Q, _ = query.shape
        Kl = key.shape[1]
        scale = HEAD_DIM ** (-0.5)
        q = (query @ w_q).reshape(B, Q, HEADS, HEAD_DIM).transpose(0, 2, 1, 3)
        k = (key @ w_k).reshape(B, Kl, HEADS, HEAD_DIM).transpose(0, 2, 1, 3)
        v = (value @ w_v).reshape(B, Kl, HEADS, HEAD_DIM).transpose(0, 2, 1, 3)
        scores = jnp.einsum('bhqd,bhkd->bhqk', q, k) * scale
        attn = jax.nn.softmax(scores, axis=-1)
        out = jnp.einsum('bhqk,bhkd->bhqd', attn, v)
        out = out.transpose(0, 2, 1, 3).reshape(B, Q, HEADS * HEAD_DIM)
        return out @ w_o

    def _L3_ffn_ref(x, W_router, b_router, W1, b1, W2, b2):
        import jax, jax.numpy as jnp
        import numpy as np
        N_EMBD = 128
        NUM_EXPERTS = 8
        TOP_K = 2
        D_FF = 4 * N_EMBD
        B, S = (4, 256)
        Bv, Sv, D = x.shape
        flat_x = x.reshape(-1, D)
        T = flat_x.shape[0]
        logits = flat_x @ W_router + b_router
        top_vals, top_idx = jax.lax.top_k(logits, TOP_K)
        neg_inf = jnp.full_like(logits, -jnp.inf)
        sparse_logits = neg_inf.at[jnp.arange(T)[:, None], top_idx].set(top_vals)
        router_weights = jax.nn.softmax(sparse_logits, axis=-1)
        final_output = jnp.zeros_like(flat_x)
        for e in range(NUM_EXPERTS):
            expert_mask = jnp.any(top_idx == e, axis=-1)
            h = jax.nn.relu(flat_x @ W1[e] + b1[e])
            y = h @ W2[e] + b2[e]
            w = router_weights[:, e] * expert_mask.astype(x.dtype)
            final_output = final_output + y * w[:, None]
        return final_output.reshape(Bv, Sv, D)
    x = x + _L0_xattn_ref(_layernorm(x, axis=-1), ctx_1024, L0_xattn_w_sim, L0_xattn_b_sim, L0_xattn_W_qv, L0_xattn_b_qv)
    x = x + _L0_ffn_ref(_layernorm(x, axis=-1), L0_ffn_Wg, L0_ffn_bg, L0_ffn_W0, L0_ffn_b0, L0_ffn_W1, L0_ffn_b1, L0_ffn_W2, L0_ffn_b2)
    x = x + _L1_xattn_ref(ctx_1024, ctx_1024, _layernorm(x, axis=-1), mask_Bx1xSxS2_if1, L1_xattn_Wv, L1_xattn_Wk, L1_xattn_Wq, L1_xattn_Wo, L1_xattn_bo)
    x = x + _L1_ffn_ref(_layernorm(x, axis=-1), L1_ffn_wg, L1_ffn_W1, L1_ffn_b1, L1_ffn_W2, L1_ffn_b2)
    x = x + _L2_xattn_ref(_layernorm(x, axis=-1), ctx_1024, L2_xattn_ln_gamma, L2_xattn_ln_beta, L2_xattn_w_q, L2_xattn_w_kv, L2_xattn_w_out, L2_xattn_b_out, L2_xattn_gate)
    x = x + _L2_ffn_ref(_layernorm(x, axis=-1), L2_ffn_wg, L2_ffn_w1, L2_ffn_w2)
    x = x + _L3_xattn_ref(_layernorm(x, axis=-1), ctx_1024, ctx_1024, L3_xattn_w_q, L3_xattn_w_k, L3_xattn_w_v, L3_xattn_w_o)
    x = x + _L3_ffn_ref(_layernorm(x, axis=-1), L3_ffn_W_router, L3_ffn_b_router, L3_ffn_W1, L3_ffn_b1, L3_ffn_W2, L3_ffn_b2)
    return x

_drawn_inputs = setup_inputs


def setup_inputs(seed=0):
    import zlib

    import numpy as np

    out = dict(_drawn_inputs(seed))
    spreads = {'L0_ffn_bg': (0.0, 0.297),
     'L0_ffn_b0': (0.0, 0.746),
     'L0_ffn_b1': (0.0, 0.8),
     'L0_ffn_b2': (0.0, 0.1),
     'L1_xattn_bo': (0.0, 0.1),
     'L1_ffn_b1': (0.0, 0.706),
     'L1_ffn_b2': (0.0, 0.44),
     'L2_xattn_ln_gamma': (1.0, 0.6),
     'L2_xattn_ln_beta': (0.0, 0.652),
     'L2_xattn_b_out': (0.0, 0.316),
     'L3_ffn_b_router': (0.0, 0.294),
     'L3_ffn_b1': (0.0, 0.299),
     'L3_ffn_b2': (0.0, 0.334)}
    factors = {'L0_xattn_w_sim': 2.811,
     'L0_ffn_W0': 5.435,
     'L0_ffn_W1': 5.781,
     'L0_ffn_W2': 4.892,
     'L1_ffn_wg': 3.396,
     'L1_ffn_W1': 5.088,
     'L1_ffn_W2': 4.817,
     'L2_ffn_wg': 2.973,
     'L2_ffn_w1': 2.674}
    for name, (base, spread) in spreads.items():
        noise = np.random.default_rng([zlib.crc32(name.encode()), seed]).standard_normal(out[name].shape)
        drawn = base * np.exp(spread * noise) if base else spread * noise
        out[name] = jnp.asarray(drawn.astype(out[name].dtype))
    for name, factor in factors.items():
        out[name] = (out[name] * factor).astype(out[name].dtype)
    return out
```

```python
import concourse.bass as bass
from concourse import mybir
from contextlib import ExitStack


def xattn_moe_stack(nc, t, out):
    F32, F32R, BF16 = mybir.dt.float32, mybir.dt.float32r, mybir.dt.bfloat16
    U32, I32 = mybir.dt.uint32, mybir.dt.int32
    ALU, ACT, AX = mybir.AluOpType, mybir.ActivationFunctionType, mybir.AxisListType

    B, S, D = t["x"].shape
    SK = t["ctx_1024"].shape[1]
    P = 128
    TB = S // P
    NT = B * TB
    KC = 2
    CK = SK // KC
    E = t["L0_ffn_Wg"].shape[1]
    HEADS = 16
    EPS = 1e-5
    CAPACITY = int(B * S / E * 1.25) + 1
    NEG = -1e20
    LO = 32
    NLN = 9

    FFN = [
        dict(w1="L0_ffn_W1", w0="L0_ffn_W0", w2="L0_ffn_W2", wg="L0_ffn_Wg", bg="L0_ffn_bg", b2="L0_ffn_b2", act=ACT.Silu),
        dict(w1="L1_ffn_W1", w0=None, w2="L1_ffn_W2", wg="L1_ffn_wg", bg=None, b2="L1_ffn_b2", act=ACT.Gelu),
        dict(w1="L2_ffn_w1", w0=None, w2="L2_ffn_w2", wg="L2_ffn_wg", bg=None, b2=None, act=ACT.Gelu),
        dict(w1="L3_ffn_W1", w0=None, w2="L3_ffn_W2", wg="L3_ffn_W_router", bg="L3_ffn_b_router", b2="L3_ffn_b2", act=ACT.Relu),
    ]
    for f in FFN:
        f["nc"] = t[f["w1"]].shape[2] // P
    KB = [l * E * B for l in range(5)]
    AB = [sum(f["nc"] for f in FFN[:l]) * E * B for l in range(5)]
    WB = [sum(3 if f["w0"] else 2 for f in FFN[:l]) * 16 * (E // 2) for l in range(5)]

    ATT = [None, dict(hg=4, dh=8, scale=D ** -0.5), dict(hg=2, dh=64, scale=64 ** -0.5), dict(hg=2, dh=64, scale=64 ** -0.5)]
    for a in ATT[1:]:
        a["ng"] = HEADS // a["hg"]
        a["rows"] = P // a["hg"]
        a["nh"] = a["hg"] // 2
    GB = [0, 0, 4, 12, 20]
    UB = [0, 0] + [B * HEADS * l for l in (1, 2, 3)]
    MB = [0, 0, 4 * 16, 4 * 16 + 8 * 8, 4 * 16 + 16 * 8]

    def wait(eng, sem, value):
        if not isinstance(value, int) or value > 0:
            eng.wait_ge(sem, value)

    def one(i):
        return slice(i, i + 1) if isinstance(i, int) else bass.ds(i, 1)

    with ExitStack() as ctx:
        def sb(name, shape, dt=F32):
            return ctx.enter_context(nc.sbuf_tensor(name, shape, dt))

        def sem(name):
            return ctx.enter_context(nc.semaphore(name))

        x_tok = sb("x_tok", [P, NT, D])
        xn_tok = sb("xn_tok", [P, NT, D])
        xnT = sb("xnT", [P, B * S])
        acc = sb("acc", [P, B * S])
        ln_sq = sb("ln_sq", [P, TB, D])
        ln_s = sb("ln_s", [P, NT])
        ln_v = sb("ln_v", [P, NT])
        ln_r = sb("ln_r", [P, NT])
        mhalf = sb("mhalf", [P, NT])
        ident = sb("ident", [P, P])
        ones = sb("ones", [P, P])
        tri = sb("tri", [P, P])
        iota8 = sb("iota8", [P, E])
        ident_bf = sb("ident_bf", [P, P], BF16)
        sel_all = sb("sel_all", [LO + E, E, P], F32R)
        sel_slot = [sb(f"sel_slot{u}", [LO + E, P], F32R) for u in range(2)]
        selh_src = sb("selh_src", [4, 4, CK])
        selh = sb("selh", [4, 4, CK], F32R)
        ctx_tok = sb("ctx_tok", [CK, B * KC, D])
        ctxT = sb("ctxT", [P, B * SK])
        mask_f = sb("mask_f", [P, SK])
        mask_bf = sb("mask_bf", [P, NT, SK], BF16)
        maskT = sb("maskT", [CK, KC, B * S], BF16)
        row_any = sb("row_any", [P, NT])
        row_neg = sb("row_neg", [P, NT])
        w_sim = sb("w_sim", [P, 3])
        b_sim = sb("b_sim", [P, 1])
        b_qv = sb("b_qv", [P, 1])
        bo1 = sb("bo1", [P, 1])
        gamma = sb("gamma", [P, 1])
        beta = sb("beta", [P, 1])
        bo2 = sb("bo2", [P, 1])
        gate = sb("gate", [P, 1])
        tgate = sb("tgate", [P, 1])
        bias_rows = sb("bias_rows", [P, P])
        biasT = sb("biasT", [P, P])
        b1_slot = [sb(f"b1_slot{u}", [P, 4]) for u in range(2)]
        b0_slot = [sb(f"b0_slot{u}", [P, 4]) for u in range(2)]
        w_qv = sb("w_qv", [P, 4, D])
        keys0 = sb("keys0", [P, B * SK])
        w2rep = sb("w2rep", [P, P])
        cj = sb("cj", [CK, B * KC])
        mx0 = sb("mx0", [P, NT])
        mx0b = sb("mx0b", [P, NT])
        nm0 = sb("nm0", [1, B * S], F32R)
        bmax = sb("bmax", [1, B])
        nbmax = sb("nbmax", [P, B])
        eb = sb("eb", [P, NT])
        hc_r = sb("hc_r", [P, B])
        hc = sb("hc", [P, B])
        mask_room = mask_bf[:, :, :].rearrange("p n s -> p (n s)").bitcast(F32)
        hqT, xhq = mask_room[:, 0:S], mask_room[:, S:2 * S]
        xhc = sb("xhc", [P, S])
        wP = [sb(f"wP{n}", [P, 4 * P]) for n in range(3)]
        woP = sb("woP", [P, 4, P])
        wq_s = sb("wq_s", [P, P])
        wk_s = sb("wk_s", [P, P])
        wv_s = sb("wv_s", [P, P])
        wo_s = sb("wo_s", [P, P])
        q_r = sb("q_r", [P, B * S], F32R)
        kz = {4: sb("kz4", [P, 4, B * SK]), 2: sb("kz2", [P, 2, B * SK])}
        kz_r = {4: sb("kz4_r", [P, 4, B * SK], F32R), 2: sb("kz2_r", [P, 2, B * SK], F32R)}
        v_room = sb("v_room", [P, B * KC, P])
        v = v_room[0:CK, :, :]
        mx = sb("mx", [P, B, TB, 4])
        nm = sb("nm", [4, B * S], F32R)
        prob_room = [sb(f"prob{n}", [P, KC, S]) for n in range(2)]
        prob = [r[0:CK, :, :] for r in prob_room]
        rsum = sb("rsum", [P, S])
        oT = sb("oT", [P, S])
        wg = sb("wg", [P, 4, E])
        bg = sb("bg", [P, 2, E])
        b2 = sb("b2", [E, 3, D])
        lg = sb("lg", [P, NT, E])
        m8 = sb("m8", [P, NT, 8])
        ix8 = sb("ix8", [P, NT, 8], U32)
        ixf = sb("ixf", [P, NT, 2])
        oh = sb("oh", [P, 2, NT, E])
        dexp = sb("dexp", [P, NT, E])
        r_d = sb("r_d", [P, NT])
        r_e = sb("r_e", [P, NT])
        r_s = sb("r_s", [P, NT])
        r_w = sb("r_w", [P, 2, NT])
        cum = [sb(f"cum{n}", [P, NT, E]) for n in range(2)]
        comb = sb("comb", [P, NT, E])
        comb2 = sb("comb2", [P, NT, E])
        cTf = xn_tok[0:E, :, :].rearrange("p n d -> p (n d)")
        cT = sb("cT", [LO + E, B * S], F32R)
        w1_s = [sb(f"w1_s{u}", [P, 4 * P]) for u in range(2)]
        w0_s = [v_room[:, 4 * u:4 * u + 4, :].rearrange("p c f -> p (c f)") for u in range(2)]
        w2_s = [sb(f"w2_s{u}", [P, 4, D]) for u in range(2)]
        h_room = sb("h_room", [P, 2 * 4 * S])
        hT = [h_room[:, n * 4 * S:(n + 1) * 4 * S].rearrange("p (c s) -> p c s", c=4) for n in range(2)]
        q = h_room[:, 0:B * S]
        mask_i = h_room[:, 0:NT * SK].bitcast(I32).rearrange("p (n s) -> p n s", n=NT)
        gS = prob_room[0]
        wrep = sb("wrep", [P, 2, S])
        sel_src = wrep[0:LO + E, :, :].rearrange("p a s -> p (a s)").rearrange("p (e c) -> p e c", e=E)
        yw = rsum

        ps = ctx.enter_context(nc.psum_tensor("ps", [P, 8, 512], F32))

        in_x = sem("in_x")
        in_ctx = sem("in_ctx")
        in_vec = sem("in_vec")
        in_mask = sem("in_mask")
        in_ffn = sem("in_ffn")
        in_l1 = sem("in_l1")
        zeroed = sem("zeroed")
        const_g = sem("const_g")
        const_v = sem("const_v")
        vec = sem("vec")
        ctxT_ps = sem("ctxT_ps"); ctxT_ok = sem("ctxT_ok")
        bias_ps = sem("bias_ps"); bias_ok = sem("bias_ok")
        mb_ok = sem("mb_ok"); mt_ps = sem("mt_ps"); mt_ok = sem("mt_ok")
        gate_ok = sem("gate_ok")
        ln_var = sem("ln_var"); ln_rstd = sem("ln_rstd"); ln_ok = sem("ln_ok")
        xT_ps = sem("xT_ps"); xT_ok = sem("xT_ok")
        x_new = sem("x_new"); accT_ps = sem("accT_ps")
        z_pre = sem("z_pre"); z_cps = sem("z_cps"); z_c = sem("z_c")
        z_sc = sem("z_sc"); z_mx = sem("z_mx"); z_mT = sem("z_mT"); z_nm = sem("z_nm"); z_bm = sem("z_bm")
        z_bps = sem("z_bps"); z_nb = sem("z_nb"); z_eb = sem("z_eb"); z_hps = sem("z_hps"); z_hc = sem("z_hc")
        z_s = sem("z_s"); z_p = sem("z_p"); z_o = sem("z_o"); z_f = sem("z_f"); z_y = sem("z_y"); z_acc = sem("z_acc")
        a_w = sem("a_w"); a_wo = sem("a_wo")
        a_qps = sem("a_qps"); a_q = sem("a_q"); a_qr = sem("a_qr")
        a_kps = sem("a_kps"); a_k = sem("a_k"); a_kr = sem("a_kr")
        a_vps = sem("a_vps"); a_v = sem("a_v")
        a_mps = sem("a_mps"); a_m = sem("a_m"); a_nps = sem("a_nps"); a_n = sem("a_n")
        a_s = sem("a_s"); a_p = sem("a_p"); a_pv = sem("a_pv"); a_o = sem("a_o")
        a_y = sem("a_y"); a_acc = sem("a_acc"); a_zero = sem("a_zero"); a_fin = sem("a_fin")
        f_lg = sem("f_lg"); f_d = sem("f_d"); f_e = sem("f_e"); f_oh = sem("f_oh"); f_rank = sem("f_rank")
        f_comb = sem("f_comb"); f_cps = sem("f_cps"); f_cf = sem("f_cf"); f_c = sem("f_c")
        f_ips = sem("f_ips"); f_init = sem("f_init")
        f_w = [sem("f_w0"), sem("f_w1")]
        f_sel = sem("f_sel"); f_wps = sem("f_wps"); f_wr = sem("f_wr")
        f_h = sem("f_h"); f_a = sem("f_a"); f_hd = sem("f_hd"); f_y = sem("f_y"); f_yd = sem("f_yd")
        a_rs = sem("a_rs"); f_init2 = sem("f_init2"); f_ym = sem("f_ym")
        out_sem = sem("out_sem")

        block = ctx.enter_context(nc.Block())

        def bsl(b):
            return slice(b * S, (b + 1) * S)

        def tiles(b):
            return slice(b * TB, (b + 1) * TB)

        x_d = t["x"].rearrange("b (n p) d -> b p n d", p=P)
        out_d = out.rearrange("b (n p) d -> b p n d", p=P)

        def col(name):
            return t[name].rearrange("(p a) -> p a", a=1)

        @block.sync
        def _(sp):
            for b in range(B):
                sp.dma_start(x_tok[:, tiles(b), :], x_d[b]).then_inc(in_x, 16)
            sp.dma_start(w_sim[:, :], t["L0_xattn_w_sim"].rearrange("(a p) -> p a", a=3), allow_slow_non_contiguous=True).then_inc(in_vec, 16)
            sp.dma_start(b_sim[:, :], t["L0_xattn_b_sim"].rearrange("(p a) -> p a", a=1).broadcast_to([P, 1])).then_inc(in_vec, 16)
            sp.dma_start(b_qv[:, :], col("L0_xattn_b_qv")).then_inc(in_vec, 16)
            sp.dma_start(bo1[:, :], col("L1_xattn_bo")).then_inc(in_vec, 16)
            sp.dma_start(gamma[:, :], col("L2_xattn_ln_gamma")).then_inc(in_vec, 16)
            sp.dma_start(beta[:, :], col("L2_xattn_ln_beta")).then_inc(in_vec, 16)
            sp.dma_start(bo2[:, :], col("L2_xattn_b_out")).then_inc(in_vec, 16)
            sp.dma_start(gate[:, :], t["L2_xattn_gate"].rearrange("(p a) -> p a", a=1).broadcast_to([P, 1])).then_inc(in_vec, 16)
            sp.dma_start(w_qv[:, :, :], t["L0_xattn_W_qv"].rearrange("(k p) d -> p k d", p=P)).then_inc(in_vec, 16)
            for l, f in enumerate(FFN):
                sp.dma_start(wg[:, l, :], t[f["wg"]]).then_inc(in_ffn, 16)
            for n, f in enumerate((FFN[0], FFN[3])):
                sp.dma_start(bg[:, n, :], t[f["bg"]].rearrange("(a e) -> a e", a=1).broadcast_to([P, E])).then_inc(in_ffn, 16)
            for n, l in enumerate((0, 1, 3)):
                sp.dma_start(b2[:, n, :], t[FFN[l]["b2"]]).then_inc(in_ffn, 16)
            for n, name in enumerate(("L0_ffn_b1", "L0_ffn_b0", "L1_ffn_b1", "L3_ffn_b1")):
                sp.dma_start(bias_rows[32 * n:32 * n + 32, :], t[name].rearrange("e (c p) -> (e c) p", p=P)).then_inc(in_ffn, 16)
            sp.dma_start(mask_i[:, :, :], t["mask_Bx1xSxS2_if1"].rearrange("b a (n p) s -> p (b a n) s", p=P)).then_inc(in_mask, 16)
            dh, rows = ATT[1]["dh"], ATT[1]["rows"]
            wait(sp, zeroed, 1)
            for n, name in enumerate(("L1_xattn_Wq", "L1_xattn_Wk", "L1_xattn_Wv")):
                for h in range(HEADS):
                    sp.dma_start(wP[n][dh * h:dh * h + dh, rows * h:rows * h + dh], t[name].rearrange("o d -> d o"), allow_slow_non_contiguous=True).then_inc(in_l1, 16)
            for j in range(4):
                for g in range(4):
                    h = 4 * g + j
                    sp.dma_start(woP[rows * j:rows * j + dh, g, :],
                                 t["L1_xattn_Wo"][:, dh * h:dh * h + dh].rearrange("e d -> d e"), allow_slow_non_contiguous=True).then_inc(in_l1, 16)

            def load_expert(f, u, e):
                n = f["nc"]
                for name, dst in (("w1", w1_s[u]), ("w0", w0_s[u])):
                    if f[name]:
                        sp.dma_start(dst[:, 0:n * P].rearrange("p (a f) -> p a f", a=1),
                                     t[f[name]].rearrange("e p f -> p e f")[:, one(e), :]).then_inc(f_w[u], 16)
                sp.dma_start(w2_s[u][:, 0:n, :].rearrange("p (a c) d -> p a c d", a=1),
                             t[f["w2"]].rearrange("e (c p) d -> p e c d", p=P)[:, one(e), :, :]).then_inc(f_w[u], 16)

            for l, f in enumerate(FFN[:NL_FFN]):
                wait(sp, f_y, KB[l])
                load_expert(f, 0, 0)
                load_expert(f, 1, 1)
                with sp.Fori(0, E // 2 - 1) as i:
                    for u in range(2):
                        sp.wait_ge(f_y, i * (2 * B) + (KB[l] + B * (u + 1)))
                        load_expert(f, u, i * 2 + (2 + u))
            for b in range(B):
                sp.wait_ge(x_new, B * (N_SUB - 1) + b + 1)
                sp.dma_start(out_d[b], x_tok[:, tiles(b), :]).then_inc(out_sem, 16)
            sp.wait_ge(out_sem, 16 * B)

        @block.gpsimd
        def _(pool):
            for n in range(3):
                pool.memset(wP[n][:, :], 0.0)
            pool.memset(woP[:, :, :], 0.0).then_inc(zeroed, 1)
            pool.dma_start(ctx_tok[:, :, :], t["ctx_1024"].rearrange("b (c p) d -> p (b c) d", p=CK)).then_inc(in_ctx, 16)
            pool.memset(ident[:, :], 0.0).then_inc(const_g, 1)
            pool.memset(tri[:, :], 1.0).then_inc(const_g, 1)
            pool.memset(sel_src[:, :, :], 0.0).then_inc(const_g, 1)
            pool.memset(selh_src[:, :, :], 0.0).then_inc(const_g, 1)
            pool.memset(ones[:, :], 1.0)
            pool.memset(mhalf[:, :], -0.5)
            pool.iota(iota8[:, :], [[1, E]], base=0, channel_multiplier=0, allow_small_or_imprecise_dtypes=True)
            pool.wait_ge(const_g, 4)
            pool.affine_select(out=ident[:, :], in_=ident[:, :], compare_op=ALU.not_equal, fill=1.0, base=0,
                               pattern=[[-1, P]], channel_multiplier=1)
            pool.affine_select(out=tri[:, :], in_=tri[:, :], compare_op=ALU.is_ge, fill=0.0, base=0,
                               pattern=[[1, P]], channel_multiplier=-1)
            pool.affine_select(out=selh_src[:, :, :], in_=selh_src[:, :, :], compare_op=ALU.not_equal, fill=1.0, base=0,
                               pattern=[[-1, 4], [0, CK]], channel_multiplier=1)
            pool.affine_select(out=sel_src[:, :, :], in_=sel_src[:, :, :], compare_op=ALU.not_equal, fill=1.0, base=0,
                               pattern=[[-1, E], [0, P]], channel_multiplier=1).then_inc(const_g, 1)
            pool.wait_ge(const_g, 5)
            pool.affine_select(out=sel_src[:, :, :], in_=sel_src[:, :, :], compare_op=ALU.not_equal, fill=1.0, base=-LO,
                               pattern=[[-1, E], [0, P]], channel_multiplier=1).then_inc(const_g, 1)
            for hg in (4, 2):
                pool.memset(kz[hg][:, :, :], 0.0)
            pool.memset(acc[:, :], 0.0).then_inc(const_g, 1)

            def rstd(j):
                for b in range(B):
                    pool.wait_ge(ln_var, B * j + b + 1)
                    pool.tensor_tensor(ln_r[:, tiles(b)], ln_v[:, tiles(b)], mhalf[:, tiles(b)], ALU.pow).then_inc(ln_rstd, 1)

            def group_weights(l):
                a, G = ATT[l], GB[l]
                if l == 1:
                    pool.wait_ge(in_l1, 16 * (3 * HEADS + 16))
                    src = [w[:, :].rearrange("p (g c) -> p g c", g=4) for w in wP] + [woP[:, :, :]]
                elif l == 2:
                    kv = t["L2_xattn_w_kv"].rearrange("p (m g c) -> m p g c", m=2, c=P)
                    src = [t["L2_xattn_w_q"].rearrange("p (g c) -> p g c", c=P), kv[0], kv[1],
                           t["L2_xattn_w_out"].rearrange("(g p) e -> p g e", p=P)]
                else:
                    src = [t[f"L3_xattn_w_{m}"].rearrange("p (g c) -> p g c", c=P) for m in "qkv"] + \
                          [t["L3_xattn_w_o"].rearrange("(g p) e -> p g e", p=P)]

                def load(g):
                    wait(pool, a_vps, g * 2 + 2 * G)
                    for dst, s in zip((wq_s, wk_s, wv_s), src):
                        pool.dma_start(dst[:, :].rearrange("p (a c) -> p a c", a=1), s[:, one(g), :]).then_inc(a_w, 16)
                    wait(pool, a_y, g * B + B * G)
                    pool.dma_start(wo_s[:, :].rearrange("p (a c) -> p a c", a=1), src[3][:, one(g), :]).then_inc(a_wo, 16)
                return load

            j = 0
            for s in range(N_SUB):
                l = s // 2
                if s % 2 == 0 and l:
                    load = group_weights(l)
                    load(0)
                rstd(j)
                j += 1
                if s == 4:
                    rstd(j)
                    j += 1
                if s % 2 == 0 and l:
                    with pool.Fori(1, ATT[l]["ng"]) as g:
                        load(g)

        @block.scalar
        def _(act):
            def copy_(out_, in_, sem_, **kw):
                return act.activation(out_, in_, ACT.Identity, **kw).then_inc(sem_, 1)

            for m in range(2):
                act.wait_ge(ctxT_ps, m + 1)
                copy_(ctxT[:, m * 2 * SK:(m + 1) * 2 * SK], ps[:, m, 0:2 * SK], ctxT_ok)
            act.wait_ge(bias_ps, 1)
            copy_(biasT[:, :], ps[:, 2, 0:P], bias_ok)
            act.wait_ge(in_vec, 16 * 9)
            act.activation(tgate[:, :], gate[:, :], ACT.Tanh).then_inc(gate_ok, 1)
            def mask_copies():
                for n in range(B * KC):
                    act.wait_ge(mt_ps, n + 1)
                    b, c = n // KC, n % KC
                    copy_(maskT[:, c, bsl(b)], ps[0:CK, 4 + n % 2, :], mt_ok)

            def xT(s):
                for b in range(B):
                    act.wait_ge(xT_ps, B * s + b + 1)
                    if s == 4:
                        act.activation(xnT[:, bsl(b)], ps[:, b, :], ACT.Identity, bias=beta[:, 0:1], scale=gamma[:, 0:1]).then_inc(xT_ok, 1)
                    else:
                        copy_(xnT[:, bsl(b)], ps[:, b, :], xT_ok)

            def attention0():
                act.wait_ge(z_cps, 1)
                copy_(cj[:, :], ps[0:CK, 4, 0:B * KC], z_c, bias=b_sim[0:CK, 0:1])
                for b in range(B):
                    act.wait_ge(z_mT, b + 1)
                    act.activation(nm0[:, bsl(b)], ps[0:1, 6, :], ACT.Copy, scale=-1.0).then_inc(z_nm, 1)
                    act.wait_ge(z_bps, b + 1)
                    act.activation(nbmax[:, b:b + 1], ps[:, 7, 0:1], ACT.Copy, scale=-1.0).then_inc(z_nb, 1)
                    act.wait_ge(z_nb, b + 1)
                    act.activation(eb[:, tiles(b)], mx0b[:, tiles(b)], ACT.Exp, bias=nbmax[:, b:b + 1]).then_inc(z_eb, 1)
                act.wait_ge(z_c, 1)
                for b in range(B):
                    act.wait_ge(z_s, b + 1)
                    if b >= 2:
                        act.wait_ge(z_o, b - 1)
                    for c in range(KC):
                        n = b * KC + c
                        act.activation(prob[b % 2][:, c, :], ps[0:CK, 2 * (b % 2) + c, :], ACT.Exp, bias=cj[:, n:n + 1]).then_inc(z_p, 1)
                    if b >= 1:
                        y_out(b - 1)
                y_out(B - 1)

            def y_out(b):
                act.wait_ge(z_y, b + 1)
                copy_(acc[:, bsl(b)], ps[:, 7, :], z_acc, bias=b_qv[:, 0:1])

            def attention(l):
                a = ATT[l]
                hg, rows, NU = a["hg"], a["rows"], B * a["hg"]
                with act.Fori(0, a["ng"]) as g:
                    for b in range(B):
                        act.wait_ge(a_qps, g * B + (B * GB[l] + b + 1))
                        copy_(q[:, bsl(b)], ps[:, b, :], a_q)
                    for m in range(2):
                        act.wait_ge(a_kps, g * 2 + (2 * GB[l] + m + 1))
                        for j in range(hg):
                            r = slice(rows * j, rows * j + rows)
                            last = act.activation(kz[hg][r, j, m * 2 * SK:(m + 1) * 2 * SK], ps[r, 4 + m, 0:2 * SK], ACT.Identity)
                        last.then_inc(a_k, 1)
                    for m in range(2):
                        act.wait_ge(a_vps, g * 2 + (2 * GB[l] + m + 1))
                        copy_(v[:, 4 * m:4 * m + 4, :], ps[0:CK, 6 + m, :].rearrange("p (n c) -> p n c", n=4), a_v)
                    for b in range(B):
                        act.wait_ge(a_nps, g * B + (B * GB[l] + b + 1))
                        act.activation(nm[0:hg, bsl(b)], ps[0:hg, 6, :], ACT.Copy, scale=-1.0).then_inc(a_n, 1)
                    for u in range(NU):
                        act.wait_ge(a_s, g * NU + (UB[l] + u + 1))
                        wait(act, a_pv, g * NU + (UB[l] + max(u - 1, 0)))
                        act.activation(prob[u % 2][:, :, :], ps[0:CK, 2 * (u % 2):2 * (u % 2) + 2, :], ACT.Exp, scale=a["scale"]).then_inc(a_p, 1)

            def ffn(l):
                f = FFN[l]
                n = f["nc"]
                act.wait_ge(f_d, l + 1)
                if l == 1:
                    act.activation(dexp[:, :, :], dexp[:, :, :], ACT.Exp).then_inc(f_e, 1)
                else:
                    act.activation(r_e[:, :], r_d[:, :], ACT.Exp).then_inc(f_e, 1)
                for b in range(B):
                    act.wait_ge(f_cps, B * l + b + 1)
                    copy_(cTf[:, bsl(b)], ps[0:E, 6 + b % 2, :], f_cf)
                if f["b2"]:
                    for b in range(B):
                        act.wait_ge(f_ips, B * IB[l] + b + 1)
                        copy_(acc[:, bsl(b)], ps[:, 4 + b % 2, :], f_init)
                act.preload_act_table(f["act"])
                with act.Fori(0, E // 2) as i:
                    for k in range(2 * B):
                        u, K = k // B, KB[l] + k
                        act.wait_ge(f_wps, i * (2 * B) + (K + 1))
                        wait(act, f_yd, i * (2 * B) + (K if k == 0 else K - 1))
                        copy_(wrep[:, k % 2, :], ps[:, 6 + k % 2, :], f_wr)
                        for c in range(n):
                            A = AB[l] + n * k + c
                            act.wait_ge(f_h, i * (2 * B * n) + (A + 1))
                            if f["w0"]:
                                wait(act, f_hd, i * (2 * B * n) + (A - c if k == 0 and c < 2 else A - 1))
                                dst, src = gS[:, c % 2, :], ps[:, c % 2, :]
                            else:
                                dst, src = hT[k % 2][:, c, :], ps[:, c, :]
                            if l == 2:
                                act.activation(dst, src, f["act"]).then_inc(f_a, 1)
                            else:
                                act.activation(dst, src, f["act"], bias=b1_slot[u][:, c:c + 1]).then_inc(f_a, 1)

            for s in range(N_SUB):
                if s == 1:
                    mask_copies()
                xT(s)
                if s % 2:
                    ffn(s // 2)
                elif s == 0:
                    attention0()
                else:
                    attention(s // 2)

        @block.vector
        def _(dve):
            step = [0]

            def link(ins):
                step[0] += 1
                ins.then_inc(vec, 1)
                dve.wait_ge(vec, step[0])

            dve.wait_ge(const_g, 7)
            dve.tensor_copy(sel_all[:, :, :], sel_src[:, :, :])
            dve.tensor_copy(selh[:, :, :], selh_src[:, :, :])
            dve.tensor_copy(ident_bf[:, :], ident[:, :])
            for hg in (4, 2):
                dve.tensor_copy(kz_r[hg][:, :, :], kz[hg][:, :, :])
            link(dve.tensor_copy(cT[:, :], acc[0:LO + E, :]))
            dve.wait_ge(in_vec, 16 * 9)
            link(dve.tensor_scalar(w2rep[:, :], ones[:, :], w_sim[:, 1:2], None, ALU.mult))
            dve.sem_inc(const_v, 1)
            for b in range(B):
                dve.wait_ge(in_x, 16 * B)

            def layer_norm(j, src, scaled=False):
                for b in range(B):
                    tb = tiles(b)
                    if b == 0 and j == 0:
                        pass
                    link(dve.tensor_reduce(ln_s[:, tb], src[:, tb, :], AX.X, ALU.add))
                    link(dve.tensor_scalar(ln_s[:, tb], ln_s[:, tb], -1.0 / D, None, ALU.mult))
                    mean = ln_s[:, tb].rearrange("p (n a) -> p n a", a=1).broadcast_to([P, TB, D])
                    link(dve.tensor_tensor(xn_tok[:, tb, :], src[:, tb, :], mean, ALU.add))
                    link(dve.tensor_tensor(ln_sq[:, :, :], xn_tok[:, tb, :], xn_tok[:, tb, :], ALU.mult))
                    link(dve.tensor_reduce(ln_v[:, tb], ln_sq[:, :, :], AX.X, ALU.add))
                    dve.tensor_scalar(ln_v[:, tb], ln_v[:, tb], 1.0 / D, EPS, ALU.mult, ALU.add).then_inc(ln_var, 1)
                    dve.wait_ge(ln_rstd, B * j + b + 1)
                    if scaled:
                        link(dve.tensor_tensor(ln_r[:, tb], ln_r[:, tb], row_any[:, tb], ALU.mult))
                    r = ln_r[:, tb].rearrange("p (n a) -> p n a", a=1).broadcast_to([P, TB, D])
                    dve.tensor_tensor(xn_tok[:, tb, :], xn_tok[:, tb, :], r, ALU.mult).then_inc(ln_ok, 1)
                    dve.wait_ge(ln_ok, B * j + b + 1)

            def finish(s):
                for b in range(B):
                    dve.wait_ge(accT_ps, B * s + b + 1)
                    dve.tensor_tensor(x_tok[:, tiles(b), :], x_tok[:, tiles(b), :],
                                      ps[:, 6 + b % 2, :].rearrange("p (n d) -> p n d", n=TB), ALU.add).then_inc(x_new, 1)
                    dve.wait_ge(x_new, B * s + b + 1)

            def mask_bias():
                dve.wait_ge(in_mask, 16)
                for n in range(NT):
                    link(dve.tensor_scalar(mask_f[:, :], mask_i[:, n, :], 0.0, None, ALU.not_equal))
                    link(dve.tensor_reduce(row_any[:, n:n + 1], mask_f[:, :], AX.X, ALU.max))
                    link(dve.tensor_scalar(row_neg[:, n:n + 1], row_any[:, n:n + 1], -NEG, None, ALU.mult))
                    dve.tensor_scalar(mask_bf[:, n, :], mask_f[:, :], 1.0, row_neg[:, n:n + 1], ALU.subtract, ALU.mult).then_inc(mb_ok, 1)
                    dve.wait_ge(mb_ok, n + 1)

            def attention0():
                dve.wait_ge(ctxT_ok, 2)
                dve.tensor_scalar(keys0[:, :], ctxT[:, :], w_sim[:, 2:3], w_sim[:, 0:1], ALU.mult, ALU.add).then_inc(z_pre, 1)
                for b in range(B):
                    dve.wait_ge(z_sc, b + 1)
                    link(dve.tensor_reduce(mx0[:, tiles(b)], ps[:, 0:TB, 0:SK], AX.X, ALU.max))
                    dve.tensor_scalar(mx0b[:, tiles(b)], mx0[:, tiles(b)], b_sim[:, 0:1], None, ALU.add).then_inc(z_mx, 1)
                    dve.wait_ge(z_nm, b + 1)
                    dve.tensor_reduce(bmax[:, b:b + 1], ps[0:1, 6, :], AX.X, ALU.max).then_inc(z_bm, 1)
                    dve.wait_ge(z_hps, b + 1)
                    link(dve.reciprocal(hc_r[:, b:b + 1], ps[:, 7, 2:3]))
                    dve.tensor_tensor(hc[:, b:b + 1], ps[:, 7, 4:5], hc_r[:, b:b + 1], ALU.mult).then_inc(z_hc, 1)
                dve.wait_ge(z_hc, B)
                for b in range(B):
                    dve.wait_ge(z_o, b + 1)
                    wait(dve, z_y, b)
                    link(dve.reciprocal(rsum[:, :], ps[:, 5, :]))
                    link(dve.tensor_tensor(hqT, ps[:, 4, :], rsum[:, :], ALU.mult))
                    dve.tensor_tensor(xhq, hqT, xnT[:, bsl(b)], ALU.mult)
                    dve.tensor_scalar(xhc[:, :], xnT[:, bsl(b)], hc[:, b:b + 1], None, ALU.mult).then_inc(z_f, 1)

            def attention(l):
                a = ATT[l]
                hg, NU, NM = a["hg"], B * a["hg"], B * a["nh"] * 2
                dve.memset(acc[:, :], 0.0).then_inc(a_zero, 1)
                dve.wait_ge(a_zero, l)
                with dve.Fori(0, a["ng"]) as g:
                    for b in range(B):
                        dve.wait_ge(a_q, g * B + (B * GB[l] + b + 1))
                        dve.tensor_copy(q_r[:, bsl(b)], q[:, bsl(b)]).then_inc(a_qr, 1)
                    for m in range(2):
                        dve.wait_ge(a_k, g * 2 + (2 * GB[l] + m + 1))
                        dve.tensor_copy(kz_r[hg][:, :, m * 2 * SK:(m + 1) * 2 * SK], kz[hg][:, :, m * 2 * SK:(m + 1) * 2 * SK]).then_inc(a_kr, 1)
                    n = 0
                    for b in range(B):
                        for h in range(a["nh"]):
                            for w in range(2):
                                dve.wait_ge(a_mps, g * NM + (MB[l] + n + 1))
                                bk = 2 * (n % 2)
                                dve.tensor_reduce(mx[:, b, 2 * w:2 * w + 2, 2 * h:2 * h + 2],
                                                  ps[:, bk:bk + 2, 0:2 * SK].rearrange("p k (h s) -> p k h s", h=2),
                                                  AX.X, ALU.max).then_inc(a_m, 1)
                                n += 1
                    for b in range(B):
                        dve.wait_ge(a_pv, g * NU + (UB[l] + hg * (b + 1)))
                        link_o(dve.reciprocal(rsum[:, :], ps[:, 5, :]), g * B + (B * GB[l] + b + 1))
                        dve.tensor_tensor(oT[:, :], ps[:, 4, :], rsum[:, :], ALU.mult).then_inc(a_o, 1)
                        dve.wait_ge(a_y, g * B + (B * GB[l] + b + 1))
                        if_prev = g * B + (B * GB[l] + b)
                        wait(dve, a_acc, if_prev)
                        dve.tensor_tensor(acc[:, bsl(b)], acc[:, bsl(b)], ps[:, 7, :], ALU.add).then_inc(a_acc, 1)
                dve.wait_ge(a_acc, B * (GB[l] + a["ng"]))
                for b in range(B):
                    if l == 1:
                        dve.tensor_scalar(acc[:, bsl(b)], acc[:, bsl(b)], bo1[:, 0:1], None, ALU.add).then_inc(a_fin, 1)
                    elif l == 2:
                        dve.wait_ge(gate_ok, 1)
                        dve.tensor_scalar(acc[:, bsl(b)], acc[:, bsl(b)], bo2[:, 0:1], tgate[:, 0:1], ALU.add, ALU.mult).then_inc(a_fin, 1)

            def link_o(ins, value):
                ins.then_inc(a_rs, 1)
                dve.wait_ge(a_rs, value)

            def wide(ap):
                return ap.rearrange("p (n a) -> p n a", a=1).broadcast_to([P, NT, E])

            def routing(l):
                f = FFN[l]
                dve.wait_ge(f_lg, l + 1)
                logits = ps[:, 5, 0:NT * E].rearrange("p (n e) -> p n e", e=E)
                if f["bg"]:
                    row = bg[:, {0: 0, 3: 1}[l]:{0: 0, 3: 1}[l] + 1, :].broadcast_to([P, NT, E])
                    link(dve.tensor_tensor(lg[:, :, :], logits, row, ALU.add))
                else:
                    link(dve.tensor_copy(lg[:, :, :], logits))
                for n in range(NT):
                    ins = dve.max(m8[:, n, :], lg[:, n, :])
                link(ins)
                for n in range(NT):
                    ins = dve.max_index(ix8[:, n, :], m8[:, n, :], lg[:, n, :])
                link(ins)
                link(dve.tensor_copy(ixf[:, :, :], ix8[:, :, 0:2]))
                ex = iota8[:, :].rearrange("p (a e) -> p a e", a=1).broadcast_to([P, NT, E])
                for k in range(1 if l == 1 else 2):
                    link(dve.tensor_tensor(oh[:, k, :, :], ex, ixf[:, :, k:k + 1].broadcast_to([P, NT, E]), ALU.is_equal))
                if l == 1:
                    dve.tensor_tensor(dexp[:, :, :], lg[:, :, :], m8[:, :, 0:1].broadcast_to([P, NT, E]), ALU.subtract).then_inc(f_d, 1)
                    link(dve.memset(cum[0][:, 0:1, :], 0.0))
                    link(dve.tensor_copy(cum[0][:, 1:NT, :], oh[:, 0, 0:NT - 1, :]))
                    k, d = 0, 1
                    while d < NT:
                        dve.tensor_copy(cum[1 - k][:, 0:d, :], cum[k][:, 0:d, :])
                        link(dve.tensor_tensor(cum[1 - k][:, d:NT, :], cum[k][:, d:NT, :], cum[k][:, 0:NT - d, :], ALU.add))
                        k, d = 1 - k, 2 * d
                    dve.sem_inc(f_oh, 1)
                    dve.wait_ge(f_e, l + 1)
                    link(dve.tensor_reduce(r_s[:, :], dexp[:, :, :], AX.X, ALU.add))
                    link(dve.reciprocal(r_w[:, 0, :], r_s[:, :]))
                    dve.wait_ge(f_rank, 1)
                    link(dve.tensor_scalar(comb2[:, :, :], ps[:, 6, 0:NT * E].rearrange("p (n e) -> p n e", e=E),
                                           float(CAPACITY), None, ALU.is_le))
                    link(dve.tensor_tensor(comb2[:, :, :], comb2[:, :, :], oh[:, 0, :, :], ALU.mult))
                    dve.tensor_tensor(comb[:, :, :], comb2[:, :, :], wide(r_w[:, 0, :]), ALU.mult).then_inc(f_comb, 1)
                else:
                    dve.tensor_tensor(r_d[:, :].rearrange("p (n a) -> p n a", a=1), m8[:, :, 1:2], m8[:, :, 0:1], ALU.subtract).then_inc(f_d, 1)
                    dve.wait_ge(f_e, l + 1)
                    link(dve.tensor_scalar(r_s[:, :], r_e[:, :], 1.0, None, ALU.add))
                    link(dve.reciprocal(r_w[:, 0, :], r_s[:, :]))
                    link(dve.tensor_tensor(r_w[:, 1, :], r_w[:, 0, :], r_e[:, :], ALU.mult))
                    link(dve.tensor_tensor(comb[:, :, :], oh[:, 0, :, :], wide(r_w[:, 0, :]), ALU.mult))
                    link(dve.tensor_tensor(comb2[:, :, :], oh[:, 1, :, :], wide(r_w[:, 1, :]), ALU.mult))
                    dve.tensor_tensor(comb[:, :, :], comb[:, :, :], comb2[:, :, :], ALU.add).then_inc(f_comb, 1)
                if not f["b2"]:
                    dve.memset(acc[:, :], 0.0).then_inc(f_init2, 1)
                for b in range(B):
                    dve.wait_ge(f_cf, B * l + b + 1)
                    link(dve.tensor_copy(cT[0:E, bsl(b)], cTf[:, bsl(b)]))
                    dve.tensor_tensor(cT[LO:LO + E, bsl(b)], cTf[:, bsl(b)], cT[0:E, bsl(b)].bitcast(F32), ALU.subtract).then_inc(f_c, 1)

            def ffn(l):
                f = FFN[l]
                n = f["nc"]
                routing(l)
                if f["b2"]:
                    dve.wait_ge(f_init, B * IB[l] + B)
                else:
                    dve.wait_ge(f_init2, 1)
                with dve.Fori(0, E // 2) as i:
                    for u in range(2):
                        for slot, base in ((b1_slot[u], {0: 0, 1: 64, 2: None, 3: 96}[l]), (b0_slot[u], 32 if f["w0"] else None)):
                            if base is not None:
                                dve.tensor_copy(slot[:, :].rearrange("p (a c) -> p a c", a=1),
                                                biasT[:, base:base + E * n].rearrange("p (e c) -> p e c", c=n)[:, bass.ds(i * 2 + u, 1), :])
                        dve.tensor_copy(sel_slot[u][:, :].rearrange("p (a c) -> p a c", a=1),
                                        sel_all[:, bass.ds(i * 2 + u, 1), :]).then_inc(f_sel, 1)

                    dve.wait_ge(f_sel, i * 2 + (E * l + 2))

                    def y_acc(k):
                        K = KB[l] + k
                        dve.wait_ge(f_y, i * (2 * B) + (K + 1))
                        dve.wait_ge(f_wr, i * (2 * B) + (K + 1))
                        dve.tensor_tensor(yw[:, :], ps[:, 4 + k % 2, :], wrep[:, k % 2, :], ALU.mult).then_inc(f_ym, 1)
                        dve.wait_ge(f_ym, i * (2 * B) + (K + 1))
                        dve.tensor_tensor(acc[:, bsl(k % B)], acc[:, bsl(k % B)], yw[:, :], ALU.add).then_inc(f_yd, 1)
                        dve.wait_ge(f_yd, i * (2 * B) + (K + 1))

                    for k in range(2 * B):
                        if f["w0"]:
                            for c in range(n):
                                A = AB[l] + n * k + c
                                dve.wait_ge(f_a, i * (2 * B * n) + (A + 1))
                                bias = b0_slot[k // B][:, c:c + 1]
                                dve.scalar_tensor_tensor(out=hT[k % 2][:, c, :], in0=ps[:, 2 + c % 2, :], scalar=bias,
                                                         in1=gS[:, c % 2, :], op0=ALU.add, op1=ALU.mult).then_inc(f_hd, 1)
                        if k:
                            y_acc(k - 1)
                    y_acc(2 * B - 1)

            j = 0
            for s in range(N_SUB):
                if s == 1:
                    mask_bias()
                layer_norm(j, x_tok, scaled=(s == 2))
                j += 1
                if s == 4:
                    layer_norm(j, xn_tok)
                    j += 1
                if s % 2:
                    ffn(s // 2)
                elif s == 0:
                    attention0()
                else:
                    attention(s // 2)
                finish(s)

        @block.tensor
        def _(pe):
            mm = pe.matmul
            pe.wait_ge(const_g, 7)
            pe.wait_ge(in_ctx, 16)
            for m in range(2):
                for n in range(4):
                    last = pe.transpose(ps[:, m, n * CK:(n + 1) * CK], ctx_tok[:, 4 * m + n, :], ident[0:CK, 0:CK])
                last.then_inc(ctxT_ps, 1)
            pe.wait_ge(in_ffn, 16 * 13)
            pe.transpose(ps[:, 2, 0:P], bias_rows[:, :], ident[:, :]).then_inc(bias_ps, 1)

            def mask_transposes():
                pe.wait_ge(mb_ok, NT)
                for n in range(B * KC):
                    b, c = n // KC, n % KC
                    if n >= 2:
                        pe.wait_ge(mt_ok, n - 1)
                    for k in range(TB):
                        last = mm(ps[0:CK, 4 + n % 2, k * P:(k + 1) * P], mask_bf[:, b * TB + k, c * CK:(c + 1) * CK], ident_bf[:, :], start=True, stop=True)
                    last.then_inc(mt_ps, 1)

            def xT(s):
                for b in range(B):
                    pe.wait_ge(ln_ok, B * (s + (1 if s >= 4 else 0)) + b + 1)
                    if b == 0 and s:
                        pe.wait_ge(xT_ok, B * s)
                    if s == 0:
                        pe.wait_ge(ctxT_ok, 2)
                        pe.wait_ge(bias_ok, 1)
                    for k in range(TB):
                        last = pe.transpose(ps[:, b, k * P:(k + 1) * P], xn_tok[:, b * TB + k, :], ident[:, :])
                    last.then_inc(xT_ps, 1)

            def finish(s, sem_, base):
                for b in range(B):
                    pe.wait_ge(sem_, base + (b + 1 if s % 2 else B))
                    if b >= 2:
                        pe.wait_ge(x_new, B * s + b - 1)
                    for k in range(TB):
                        last = pe.transpose(ps[:, 6 + b % 2, k * P:(k + 1) * P], acc[:, b * S + k * P:b * S + (k + 1) * P], ident[:, :])
                    last.then_inc(accT_ps, 1)

            def attention0():
                pe.wait_ge(z_pre, 1)
                pe.wait_ge(const_v, 1)
                for n in range(B * KC):
                    last = mm(ps[0:CK, 4, n:n + 1], ctxT[:, n * CK:(n + 1) * CK], w_sim[:, 1:2], start=True, stop=True)
                last.then_inc(z_cps, 1)
                for b in range(B):
                    keys = slice(b * SK, (b + 1) * SK)
                    pe.wait_ge(xT_ok, B)
                    wait(pe, z_mx, b)
                    for k in range(TB):
                        mm(ps[:, k, 0:SK], xnT[:, b * S + k * P:b * S + (k + 1) * P], keys0[:, keys], start=True, stop=False)
                        last = mm(ps[:, k, 0:SK], w2rep[:, :], ctxT[:, keys], start=False, stop=True)
                    last.then_inc(z_sc, 1)
                    pe.wait_ge(z_mx, b + 1)
                    wait(pe, z_bm, b)
                    for k in range(TB):
                        last = pe.transpose(ps[0:1, 6, k * P:(k + 1) * P], mx0b[:, b * TB + k:b * TB + k + 1], ident[:, :])
                    last.then_inc(z_mT, 1)
                    pe.wait_ge(z_bm, b + 1)
                    wait(pe, z_hc, b)
                    mm(ps[:, 7, 0:1], ones[0:1, :], bmax[:, b:b + 1], start=True, stop=True).then_inc(z_bps, 1)
                    pe.wait_ge(z_eb, b + 1)
                    for k in range(TB):
                        mm(ps[:, 7, 2:3], ones[:, :], eb[:, b * TB + k:b * TB + k + 1], start=(k == 0), stop=(k == TB - 1))
                    for k in range(TB):
                        last = mm(ps[:, 7, 4:5], xn_tok[:, b * TB + k, :], eb[:, b * TB + k:b * TB + k + 1], start=(k == 0), stop=(k == TB - 1))
                    last.then_inc(z_hps, 1)
                pe.wait_ge(z_nm, B)
                pe.wait_ge(z_c, 1)
                pe.wait_ge(z_hc, B)

                def scores(b):
                    if b >= 2:
                        pe.wait_ge(z_p, KC * (b - 1))
                    for c in range(KC):
                        n = b * KC + c
                        bank = ps[0:CK, 2 * (b % 2) + c, :]
                        mm(bank, keys0[:, n * CK:(n + 1) * CK], xnT[:, bsl(b)], start=True, stop=False)
                        last = mm(bank, selh[0:1, 0, :], nm0[:, bsl(b)], start=False, stop=True)
                    last.then_inc(z_s, 1)

                scores(0)
                for b in range(B):
                    if b + 1 < B:
                        scores(b + 1)
                    pe.wait_ge(z_p, KC * (b + 1))
                    wait(pe, z_f, b)
                    for c in range(KC):
                        mm(ps[:, 4, :], ctx_tok[:, b * KC + c, :], prob[b % 2][:, c, :], start=(c == 0), stop=(c == KC - 1))
                    for c in range(KC):
                        last = mm(ps[:, 5, :], ones[0:CK, :], prob[b % 2][:, c, :], start=(c == 0), stop=(c == KC - 1))
                    last.then_inc(z_o, 1)
                    pe.wait_ge(z_f, b + 1)
                    wait(pe, z_acc, b)
                    for k, feat in enumerate((xnT[:, bsl(b)], hqT, xhq, xhc[:, :])):
                        last = mm(ps[:, 7, :], w_qv[:, k, :], feat, start=(k == 0), stop=(k == 3))
                    last.then_inc(z_y, 1)

            def attention(l):
                a = ATT[l]
                hg, rows, nh = a["hg"], a["rows"], a["nh"]
                NU, NM, G = B * hg, B * nh * 2, GB[l]
                pe.wait_ge(xT_ok, B * (2 * l + 1))
                if l == 1:
                    pe.wait_ge(mt_ok, B * KC)
                with pe.Fori(0, a["ng"]) as g:
                    pe.wait_ge(a_w, g * 48 + 48 * (G + 1))
                    wait(pe, a_p, g * NU + UB[l])
                    for b in range(B):
                        mm(ps[:, b, :], wq_s[:, :], xnT[:, bsl(b)], start=True, stop=True).then_inc(a_qps, 1)
                    wait(pe, a_o, g * B + B * G)
                    for m in range(2):
                        mm(ps[:, 4 + m, 0:2 * SK], wk_s[:, :], ctxT[:, m * 2 * SK:(m + 1) * 2 * SK], start=True, stop=True).then_inc(a_kps, 1)
                    wait(pe, a_acc, g * B + B * G)
                    wait(pe, a_n, g * B + B * G)
                    for m in range(2):
                        for n in range(4):
                            last = mm(ps[0:CK, 6 + m, n * P:(n + 1) * P], ctxT[:, (4 * m + n) * CK:(4 * m + n + 1) * CK], wv_s[:, :], start=True, stop=True)
                        last.then_inc(a_vps, 1)
                    pe.wait_ge(a_qr, g * B + (B * G + B))
                    pe.wait_ge(a_kr, g * 2 + (2 * G + 2))
                    n = 0
                    for b in range(B):
                        for h in range(nh):
                            for w in range(2):
                                if n >= 2:
                                    pe.wait_ge(a_m, g * NM + (MB[l] + n - 1))
                                for k in range(2):
                                    tile = b * TB + 2 * w + k
                                    bank = ps[:, 2 * (n % 2) + k, 0:2 * SK]
                                    last = mm(bank.rearrange("p (h s) -> p h s", h=2), q_r[:, tile * P:(tile + 1) * P],
                                              kz_r[hg][:, 2 * h:2 * h + 2, b * SK:(b + 1) * SK], start=True, stop=(l != 1))
                                    if l == 1:
                                        last = mm(bank.rearrange("p (h s) -> p h s", h=2), ident_bf[:, :],
                                                  mask_bf[:, tile:tile + 1, :].broadcast_to([P, 2, SK]), start=False, stop=True)
                                last.then_inc(a_mps, 1)
                                n += 1
                    pe.wait_ge(a_m, g * NM + (MB[l] + NM))
                    pe.wait_ge(a_v, g * 2 + (2 * G + 2))
                    for b in range(B):
                        if b:
                            pe.wait_ge(a_n, g * B + (B * G + b))
                        for k in range(TB):
                            last = pe.transpose(ps[0:hg, 6, k * P:(k + 1) * P], mx[:, b, k, 0:hg], ident[:, :])
                        last.then_inc(a_nps, 1)

                    def scores(u):
                        b, j = u // hg, u % hg
                        if u >= 2:
                            pe.wait_ge(a_p, g * NU + (UB[l] + u - 1))
                        pe.wait_ge(a_n, g * B + (B * G + b + 1))
                        for c in range(KC):
                            n = b * KC + c
                            bank = ps[0:CK, 2 * (u % 2) + c, :]
                            mm(bank, kz[hg][:, j, n * CK:(n + 1) * CK], q[:, bsl(b)], start=True, stop=False)
                            if l == 1:
                                mm(bank, ident_bf[0:CK, 0:CK], maskT[:, c, bsl(b)], start=False, stop=False)
                            last = mm(bank, selh[0:hg, j, :], nm[0:hg, bsl(b)], start=False, stop=True)
                        last.then_inc(a_s, 1)

                    def values(u):
                        b, j = u // hg, u % hg
                        r = slice(rows * j, rows * j + rows)
                        pe.wait_ge(a_p, g * NU + (UB[l] + u + 1))
                        if j == 0:
                            wait(pe, a_o, g * B + (B * G + b))
                        for c in range(KC):
                            mm(ps[r, 4, :], v[:, b * KC + c, r], prob[u % 2][:, c, :], start=(c == 0), stop=(c == KC - 1))
                        for c in range(KC):
                            last = mm(ps[r, 5, :], ones[0:CK, 0:rows], prob[u % 2][:, c, :], start=(c == 0), stop=(c == KC - 1))
                        last.then_inc(a_pv, 1)

                    def project(b):
                        pe.wait_ge(a_o, g * B + (B * G + b + 1))
                        pe.wait_ge(a_wo, g * 16 + 16 * (G + 1))
                        wait(pe, a_acc, g * B + (B * G + b))
                        mm(ps[:, 7, :], wo_s[:, :], oT[:, :], start=True, stop=True).then_inc(a_y, 1)

                    for u in range(NU):
                        scores(u)
                        if u:
                            values(u - 1)
                        if u > hg and u % hg == 1:
                            project(u // hg - 1)
                    values(NU - 1)
                    project(B - 1)

            def ffn(l):
                f = FFN[l]
                n = f["nc"]
                pe.wait_ge(xT_ok, B * (2 * l + 2))
                for k in range(NT):
                    last = mm(ps[:, 5, k * E:(k + 1) * E], xnT[:, k * P:(k + 1) * P], wg[:, l, :], start=True, stop=True)
                last.then_inc(f_lg, 1)
                if l == 1:
                    pe.wait_ge(f_oh, 1)
                    pe.wait_ge(x_new, B * (2 * l + 1))
                    mm(ps[:, 6, 0:NT * E], tri[:, :], oh[:, 0, :, :], start=True, stop=False)
                    mm(ps[:, 6, 0:NT * E], ones[:, :], cum[0][:, :, :], start=False, stop=True).then_inc(f_rank, 1)
                pe.wait_ge(f_comb, l + 1)
                for b in range(B):
                    if b >= 2:
                        pe.wait_ge(f_cf, B * l + b - 1)
                    for k in range(TB):
                        last = pe.transpose(ps[0:E, 6 + b % 2, k * P:(k + 1) * P], comb[:, b * TB + k, :], ident[:, :])
                    last.then_inc(f_cps, 1)
                if f["b2"]:
                    for b in range(B):
                        pe.wait_ge(f_cf, B * l + b + 1)
                        if b >= 2:
                            pe.wait_ge(f_init, B * IB[l] + b - 1)
                        mm(ps[:, 4 + b % 2, :], b2[:, IB[l], :], cTf[:, bsl(b)], start=True, stop=True).then_inc(f_ips, 1)
                    pe.wait_ge(f_init, B * IB[l] + B)
                pe.wait_ge(f_cf, B * l + B)
                pe.wait_ge(f_c, B * l + B)
                with pe.Fori(0, E // 2) as i:
                    def hidden(k):
                        u, b, K = k // B, k % B, KB[l] + k
                        if b == 0:
                            pe.wait_ge(f_sel, i * 2 + (E * l + u + 1))
                            nd = 3 if f["w0"] else 2
                            pe.wait_ge(f_w[u], i * (16 * nd) + (WB[l] + 16 * nd))
                        wait(pe, f_wr, i * (2 * B) + (K if k == 0 else K - 1))
                        mm(ps[:, 6 + k % 2, :], sel_slot[u][:, :], cT[:, bsl(b)], start=True, stop=True).then_inc(f_wps, 1)
                        for c in range(n):
                            A = AB[l] + n * k + c
                            cs = slice(c * P, (c + 1) * P)
                            if f["w0"]:
                                back = A - c if k == 0 and c < 2 else A - 1
                                wait(pe, f_a, i * (2 * B * n) + back)
                                mm(ps[:, c % 2, :], w1_s[u][:, cs], xnT[:, bsl(b)], start=True, stop=True)
                                wait(pe, f_hd, i * (2 * B * n) + back)
                                mm(ps[:, 2 + c % 2, :], w0_s[u][:, cs], xnT[:, bsl(b)], start=True, stop=True).then_inc(f_h, 1)
                            else:
                                wait(pe, f_a, i * (2 * B * n) + (A - c if k == 0 else A - n + 1))
                                mm(ps[:, c, :], w1_s[u][:, cs], xnT[:, bsl(b)], start=True, stop=True).then_inc(f_h, 1)

                    def down(k):
                        u, K = k // B, KB[l] + k
                        wait(pe, f_yd, i * (2 * B) + (K if k == 0 else K - 1))
                        for c in range(n):
                            A = AB[l] + n * k + c
                            pe.wait_ge(f_hd if f["w0"] else f_a, i * (2 * B * n) + (A + 1))
                            last = mm(ps[:, 4 + k % 2, :], w2_s[u][:, c, :], hT[k % 2][:, c, :], start=(c == 0), stop=(c == n - 1))
                        last.then_inc(f_y, 1)

                    for k in range(2 * B):
                        hidden(k)
                        if k:
                            down(k - 1)
                    down(2 * B - 1)

            for s in range(N_SUB):
                l = s // 2
                xT(s)
                if s % 2:
                    ffn(l)
                    finish(s, f_yd, KB[l + 1] - B)
                elif s == 0:
                    attention0()
                    mask_done = True
                    finish(0, z_acc, 0)
                    if N_SUB > 1:
                        mask_transposes()
                else:
                    attention(l)
                    finish(s, *((a_fin, B * (l - 1)) if l < 3 else (a_acc, B * (GB[l] + ATT[l]["ng"]) - B)))


NL_FFN = 4
N_SUB = 8
IB = {0: 0, 1: 1, 3: 2}


def kernel(**inputs):
    import numpy as _np
    import concourse.bacc as _bacc
    from concourse.bass_utils import run_bass_kernel_spmd as _run

    nc = _bacc.Bacc("TRN2", target_bir_lowering=False, num_devices=1)
    arrays, args = {}, {}
    for name, value in inputs.items():
        a = _np.ascontiguousarray(value)
        arrays[f"in_{name}"] = a
        args[name] = nc.dram_tensor(f"in_{name}", a.shape, mybir.dt.from_np(a.dtype), kind="ExternalInput").ap()
    shape = arrays["in_x"].shape
    out = nc.dram_tensor("out_0", shape, mybir.dt.float32, kind="ExternalOutput").ap()
    xattn_moe_stack(nc, args, out)
    r = _run(nc, [arrays], core_ids=[0])
    return r.results[0]["out_0"]
```

```python
import concourse.bass as bass
from concourse import mybir
from contextlib import ExitStack


def xattn_moe_stack(nc, t, out):
    F32, F32R, BF16 = mybir.dt.float32, mybir.dt.float32r, mybir.dt.bfloat16
    U32, I32 = mybir.dt.uint32, mybir.dt.int32
    ALU, ACT, AX = mybir.AluOpType, mybir.ActivationFunctionType, mybir.AxisListType

    B, S, D = t["x"].shape
    SK = t["ctx_1024"].shape[1]
    P = 128
    TB = S // P
    NT = B * TB
    KC = 2
    CK = SK // KC
    E = t["L0_ffn_Wg"].shape[1]
    HEADS = 16
    EPS = 1e-5
    CAPACITY = int(B * S / E * 1.25) + 1
    NEG = -1e20
    NPT = 4
    LO = 32
    NLN = 9

    FFN = [
        dict(w1="L0_ffn_W1", w0="L0_ffn_W0", w2="L0_ffn_W2", wg="L0_ffn_Wg", bg="L0_ffn_bg", b2="L0_ffn_b2", act=ACT.Silu),
        dict(w1="L1_ffn_W1", w0=None, w2="L1_ffn_W2", wg="L1_ffn_wg", bg=None, b2="L1_ffn_b2", act=ACT.Gelu),
        dict(w1="L2_ffn_w1", w0=None, w2="L2_ffn_w2", wg="L2_ffn_wg", bg=None, b2=None, act=ACT.Gelu),
        dict(w1="L3_ffn_W1", w0=None, w2="L3_ffn_W2", wg="L3_ffn_W_router", bg="L3_ffn_b_router", b2="L3_ffn_b2", act=ACT.Relu),
    ]
    for f in FFN:
        f["nc"] = t[f["w1"]].shape[2] // P
    KB = [1 + l * E * B for l in range(5)]
    AB = [1 + sum(f["nc"] for f in FFN[:l]) * E * B for l in range(5)]
    WB = [sum(3 if f["w0"] else 2 for f in FFN[:l]) * 16 * (E // 2) for l in range(5)]

    ATT = [None, dict(hg=4, dh=8, scale=D ** -0.5), dict(hg=2, dh=64, scale=64 ** -0.5), dict(hg=2, dh=64, scale=64 ** -0.5)]
    for a in ATT[1:]:
        a["ng"] = HEADS // a["hg"]
        a["rows"] = P // a["hg"]
        a["nh"] = a["hg"] // 2
        a["nj"] = 1 if a["hg"] == 4 else 2
        a["jobs"] = [(kind, j, n) for kind, n in (("q", 0), ("k", 0), ("q", 1), ("q", 2), ("q", 3), ("k", 1))
                     for j in range(a["nj"])] + [("v", 0, 0), ("v", 0, 1)]

    def before(count):
        out_, n = [0, 1], 1
        for a in ATT[1:]:
            n += count(a) * a["ng"]
            out_.append(n)
        return out_

    GB = before(lambda a: 1)
    OB = before(lambda a: B)
    PB = before(lambda a: B * a["nh"])
    MB = before(lambda a: B * TB * a["nh"])
    JB = before(lambda a: len(a["jobs"]))
    AW = [0, 0] + [16 * n for n in (4 * 3, 4 * 3 + 8 * 5)]
    HB = before(lambda a: len(a["jobs"]) - 2)

    def wait(eng, sem, value):
        if not isinstance(value, int) or value > 0:
            eng.wait_ge(sem, value)

    def at(g, k, c):
        return g[0] * k + (g[1] * k + c)

    def one(i):
        return slice(i, i + 1) if isinstance(i, int) else bass.ds(i, 1)

    with ExitStack() as ctx:
        def sb(name, shape, dt=F32):
            return ctx.enter_context(nc.sbuf_tensor(name, shape, dt))

        def sb_two(name, shape):
            offset = -(-nc.sbuf_base // 32) * 32
            room = sb(name, shape)
            return room, nc.alloc_sbuf_tensor_at(name + "_r", shape, F32R, offset=offset)

        def sem(name):
            return ctx.enter_context(nc.semaphore(name))

        x_tok = sb("x_tok", [P, NT, D])
        xn_tok = sb("xn_tok", [P, NT, D])
        xnT = sb("xnT", [P, B * S])
        acc = sb("acc", [P, B * S])
        ln_room, ln_room_r = sb_two("ln_room", [P, TB * D])
        ln_sq = ln_room[:, :].rearrange("p (n d) -> p n d", n=TB)
        ln_s = sb("ln_s", [P, NT])
        ln_v = sb("ln_v", [P, NT])
        ln_r = sb("ln_r", [P, NT])
        mhalf = sb("mhalf", [P, NT])
        ident = sb("ident", [P, P])
        ones = sb("ones", [P, P])
        tri = sb("tri", [P, P])
        iota8 = sb("iota8", [P, E])
        ident_bf = sb("ident_bf", [P, P], BF16)
        sel_all = sb("sel_all", [LO + E, E + 1, P], F32R)
        sel_slot = [sb(f"sel_slot{u}", [LO + E, P], F32R) for u in range(2)]
        rep_i = sb("rep_i", [P, 3], I32)
        neg_lo = sb("neg_lo", [P, 3])
        ones_r = sb("ones_r", [1, CK], F32R)
        ctx_tok = sb("ctx_tok", [CK, B * KC, D])
        ctxT = sb("ctxT", [P, B * SK])
        mask_f = sb("mask_f", [P, SK])
        mask_bf = sb("mask_bf", [P, NT, SK], BF16)
        row_any = sb("row_any", [P, NT])
        row_neg = sb("row_neg", [P, NT])
        w_sim = sb("w_sim", [P, 3])
        b_sim = sb("b_sim", [P, 1])
        b_qv = sb("b_qv", [P, 1])
        bo1 = sb("bo1", [P, 1])
        gamma = sb("gamma", [P, 1])
        beta = sb("beta", [P, 1])
        bo2 = sb("bo2", [P, 1])
        gate = sb("gate", [P, 1])
        tgate = sb("tgate", [P, 1])
        bias_rows = sb("bias_rows", [P, P])
        biasT = sb("biasT", [P, P + 4])
        b1_slot = [sb(f"b1_slot{u}", [P, 4]) for u in range(2)]
        b0_slot = [sb(f"b0_slot{u}", [P, 4]) for u in range(2)]
        w_qv = sb("w_qv", [P, 4, D])
        keys0 = sb("keys0", [P, B * SK])
        w2rep = sb("w2rep", [P, P])
        cj = sb("cj", [CK, B * KC])
        mx0 = sb("mx0", [P, NT])
        mx0b = sb("mx0b", [P, NT])
        nm0 = sb("nm0", [1, B * S], F32R)
        bmax = sb("bmax", [1, B])
        nbmax = sb("nbmax", [P, B])
        eb = sb("eb", [P, NT])
        hc_r = sb("hc_r", [P, B])
        hc = sb("hc", [P, B])
        mask_room = mask_bf[:, :, :].rearrange("p n s -> p (n s)").bitcast(F32)
        hqT, xhq = mask_room[:, 0:S], mask_room[:, S:2 * S]
        xhc = sb("xhc", [P, S])
        wP = [sb(f"wP{n}", [P, 4 * P]) for n in range(3)]
        woP = sb("woP", [P, 4, P])
        wq_s = sb("wq_s", [P, 2, 2, 64])
        wk_s = sb("wk_s", [P, 2, 2, 64])
        wv_s = sb("wv_s", [P, P])
        wo_s = sb("wo_s", [P, P])
        q_s = sb("q_s", [P, 2, B * S], F32R)
        q_h = sb("q_h", [P, 2, S], F32R)
        kz_h = sb("kz_h", [P, 2 * SK], F32R)
        kz = sb("kz", [P, 4, B * SK], F32R)
        k_hi = sb("k_hi", [P, 2, B * SK], F32R)
        k_lo = sb("k_lo", [P, 2, B * SK], F32R)
        v_room, v_room_r = sb_two("v_room", [P, B * KC * P])
        v = v_room[0:CK, :].rearrange("p (n c) -> p n c", c=P)
        nmx = sb("nmx", [P, NPT, 2])
        sm = sb("sm", [P, NPT, 2])
        rc = sb("rc", [P, NPT, 2])
        h_room, h_room_r = sb_two("h_room", [P, 2 * 4 * S])
        p_room, p_room_r = sb_two("p_room", [P, 4 * KC * S])
        prob = [r[0:CK, n * KC * S:(n + 1) * KC * S].rearrange("p (c s) -> p c s", c=KC) for r in (p_room, h_room) for n in range(4)]
        rsum = sb("rsum", [P, S])
        oT = sb("oT", [P, S])
        wg = sb("wg", [P, 4, E])
        bg = sb("bg", [P, 2, E])
        b2 = sb("b2", [E, 3, D])
        lg = sb("lg", [P, NT, E])
        m8 = sb("m8", [P, NT, 8])
        ix8 = sb("ix8", [P, NT, 8], U32)
        ixf = sb("ixf", [P, NT, 2])
        oh = sb("oh", [P, 2, NT, E])
        dexp = sb("dexp", [P, NT, E])
        r_d = sb("r_d", [P, NT])
        r_e = sb("r_e", [P, NT])
        r_s = sb("r_s", [P, NT])
        r_w = sb("r_w", [P, 2, NT])
        cum = [sb(f"cum{n}", [P, NT, E]) for n in range(2)]
        comb = sb("comb", [P, NT, E])
        comb2 = sb("comb2", [P, NT, E])
        cTf = xn_tok[0:E, :, :].rearrange("p n d -> p (n d)")
        cT = sb("cT", [LO + E, B * S], F32R)
        w1_s = [sb(f"w1_s{u}", [P, 4 * P]) for u in range(2)]
        w0_s = [v_room[:, 0:4 * P], keys0[:, 0:4 * P]]
        w2_s = [sb(f"w2_s{u}", [P, 4, D]) for u in range(2)]
        x_hi, x_lo = q_s[:, 0, :], q_s[:, 1, :]
        kz_flat = kz[:, :, :].rearrange("p j s -> p (j s)")
        k_flat = [k[:, :, :].rearrange("p j s -> p (j s)") for k in (k_hi, k_lo)]
        w1_p = [[kz_flat[:, (2 * u + n) * 4 * P:(2 * u + n + 1) * 4 * P] for n in range(2)] for u in range(2)]
        w0_p = [[q_h[:, 0, :], v_room_r[:, 4 * P:8 * P]], [q_h[:, 1, :], ln_room_r[:, :]]]
        w2_p = [[k[:, u * 4 * P:(u + 1) * 4 * P] for k in k_flat] for u in range(2)]
        h_p = [[r[:, n * 4 * S:(n + 1) * 4 * S].rearrange("p (c s) -> p c s", c=4) for r in (h_room_r, p_room_r)] for n in range(2)]
        mask_i = h_room[:, 0:NT * SK].bitcast(I32).rearrange("p (n s) -> p n s", n=NT)
        gS = [xhc, oT]
        h_f = sb("h_f", [P, 2, S])
        sel_src = h_f[0:LO + E, :, :].rearrange("p a s -> p (a s)").rearrange("p (e c) -> p e c", e=E)
        yw = rsum
        h_flat = h_f[:, :, :].rearrange("p u s -> p (u s)")
        pt = [w.rearrange("p (h s) -> p h s", h=2) for w in [h_flat[:, 2 * SK * u:2 * SK * (u + 1)] for u in range(3)] + [rsum[:, 0:2 * SK]]]

        ps = ctx.enter_context(nc.psum_tensor("ps", [P, 8, 512], F32))

        in_x = sem("in_x")
        in_ctx = sem("in_ctx")
        in_vec = sem("in_vec")
        in_mask = sem("in_mask")
        in_ffn = sem("in_ffn")
        in_l1 = sem("in_l1")
        zeroed = sem("zeroed")
        const_g = sem("const_g")
        const_v = sem("const_v")
        vec = sem("vec")
        ctxT_ps = sem("ctxT_ps"); ctxT_ok = sem("ctxT_ok")
        bias_ps = sem("bias_ps"); bias_ok = sem("bias_ok")
        mb_ok = sem("mb_ok")
        gate_ok = sem("gate_ok")
        ln_var = sem("ln_var"); ln_rstd = sem("ln_rstd"); ln_ok = sem("ln_ok")
        xT_ps = sem("xT_ps"); xT_ok = sem("xT_ok")
        x_new = sem("x_new"); accT_ps = sem("accT_ps")
        z_pre = sem("z_pre"); z_cps = sem("z_cps"); z_c = sem("z_c")
        z_sc = sem("z_sc"); z_mx = sem("z_mx"); z_mT = sem("z_mT"); z_nm = sem("z_nm"); z_bm = sem("z_bm")
        z_bps = sem("z_bps"); z_nb = sem("z_nb"); z_eb = sem("z_eb"); z_hps = sem("z_hps"); z_hc = sem("z_hc")
        z_s = sem("z_s"); z_p = sem("z_p"); z_o = sem("z_o"); z_f = sem("z_f"); z_y = sem("z_y"); z_acc = sem("z_acc")
        a_ld = sem("a_ld"); a_w = sem("a_w"); a_wo = sem("a_wo")
        a_pj = sem("a_pj"); a_hi = sem("a_hi"); a_pd = sem("a_pd")
        a_s = sem("a_s"); a_m = sem("a_m"); a_e = sem("a_e"); a_sm = sem("a_sm"); a_r = sem("a_r"); a_z = sem("a_z")
        a_t = sem("a_t"); a_ta = sem("a_ta"); a_td = sem("a_td"); a_pv = sem("a_pv"); a_o = sem("a_o")
        a_y = sem("a_y"); a_acc = sem("a_acc"); a_zero = sem("a_zero"); a_fin = sem("a_fin")
        f_lg = sem("f_lg"); f_d = sem("f_d"); f_e = sem("f_e"); f_oh = sem("f_oh"); f_rank = sem("f_rank")
        f_comb = sem("f_comb"); f_cps = sem("f_cps"); f_cf = sem("f_cf"); f_c = sem("f_c")
        f_ips = sem("f_ips"); f_init = sem("f_init")
        f_w = [sem("f_w0"), sem("f_w1")]
        f_ws = [sem("f_ws0"), sem("f_ws1")]
        f_wh = sem("f_wh"); f_sel = sem("f_sel"); f_xh = sem("f_xh"); f_xl = sem("f_xl"); f_hh = sem("f_hh"); f_hl = sem("f_hl")
        f_h = sem("f_h"); f_a = sem("f_a"); f_hd = sem("f_hd"); f_y = sem("f_y"); f_yd = sem("f_yd")
        l1_rep = sem("l1_rep"); f_init2 = sem("f_init2"); f_ym = sem("f_ym")
        out_sem = sem("out_sem")

        block = ctx.enter_context(nc.Block())

        def bsl(b):
            return slice(b * S, (b + 1) * S)

        def tiles(b):
            return slice(b * TB, (b + 1) * TB)

        x_d = t["x"].rearrange("b (n p) d -> b p n d", p=P)
        out_d = out.rearrange("b (n p) d -> b p n d", p=P)

        def col(name):
            return t[name].rearrange("(p a) -> p a", a=1)

        @block.sync
        def _(sp):
            for b in range(B):
                sp.dma_start(x_tok[:, tiles(b), :], x_d[b]).then_inc(in_x, 16)
            sp.dma_start(w_sim[:, :], t["L0_xattn_w_sim"].rearrange("(a p) -> p a", a=3), allow_slow_non_contiguous=True).then_inc(in_vec, 16)
            sp.dma_start(b_sim[:, :], t["L0_xattn_b_sim"].rearrange("(p a) -> p a", a=1).broadcast_to([P, 1])).then_inc(in_vec, 16)
            sp.dma_start(b_qv[:, :], col("L0_xattn_b_qv")).then_inc(in_vec, 16)
            sp.dma_start(bo1[:, :], col("L1_xattn_bo")).then_inc(in_vec, 16)
            sp.dma_start(gamma[:, :], col("L2_xattn_ln_gamma")).then_inc(in_vec, 16)
            sp.dma_start(beta[:, :], col("L2_xattn_ln_beta")).then_inc(in_vec, 16)
            sp.dma_start(bo2[:, :], col("L2_xattn_b_out")).then_inc(in_vec, 16)
            sp.dma_start(gate[:, :], t["L2_xattn_gate"].rearrange("(p a) -> p a", a=1).broadcast_to([P, 1])).then_inc(in_vec, 16)
            sp.dma_start(w_qv[:, :, :], t["L0_xattn_W_qv"].rearrange("(k p) d -> p k d", p=P)).then_inc(in_vec, 16)
            for l, f in enumerate(FFN):
                sp.dma_start(wg[:, l, :], t[f["wg"]]).then_inc(in_ffn, 16)
            for n, f in enumerate((FFN[0], FFN[3])):
                sp.dma_start(bg[:, n, :], t[f["bg"]].rearrange("(a e) -> a e", a=1).broadcast_to([P, E])).then_inc(in_ffn, 16)
            for n, l in enumerate((0, 1, 3)):
                sp.dma_start(b2[:, n, :], t[FFN[l]["b2"]]).then_inc(in_ffn, 16)
            for n, name in enumerate(("L0_ffn_b1", "L0_ffn_b0", "L1_ffn_b1", "L3_ffn_b1")):
                sp.dma_start(bias_rows[32 * n:32 * n + 32, :], t[name].rearrange("e (c p) -> (e c) p", p=P)).then_inc(in_ffn, 16)
            sp.dma_start(mask_i[:, :, :], t["mask_Bx1xSxS2_if1"].rearrange("b a (n p) s -> p (b a n) s", p=P)).then_inc(in_mask, 16)
            dh, rows = ATT[1]["dh"], ATT[1]["rows"]
            wait(sp, zeroed, 1)
            for n, name in enumerate(("L1_xattn_Wq", "L1_xattn_Wk", "L1_xattn_Wv")):
                for h in range(HEADS):
                    sp.dma_start(wP[n][dh * h:dh * h + dh, rows * h:rows * h + dh], t[name].rearrange("o d -> d o"), allow_slow_non_contiguous=True).then_inc(in_l1, 16)
            for j in range(4):
                for g in range(4):
                    h = 4 * g + j
                    sp.dma_start(woP[rows * j:rows * j + dh, g, :],
                                 t["L1_xattn_Wo"][:, dh * h:dh * h + dh].rearrange("e d -> d e"), allow_slow_non_contiguous=True).then_inc(in_l1, 16)

            def group_weights(l):
                a = ATT[l]
                if l == 1:
                    sp.wait_ge(in_l1, 16 * (3 * HEADS + 16))
                    sp.wait_ge(l1_rep, 1)
                    src = [w[:, :].rearrange("p (g c) -> p g c", g=4) for w in wP] + [woP[:, :, :]]
                elif l == 2:
                    kv = t["L2_xattn_w_kv"].rearrange("p (m g c) -> m p g c", m=2, c=P)
                    src = [t["L2_xattn_w_q"].rearrange("p (g c) -> p g c", c=P), kv[0], kv[1],
                           t["L2_xattn_w_out"].rearrange("(g p) e -> p g e", p=P)]
                else:
                    src = [t[f"L3_xattn_w_{m}"].rearrange("p (g c) -> p g c", c=P) for m in "qkv"] + \
                          [t["L3_xattn_w_o"].rearrange("(g p) e -> p g e", p=P)]

                def load(g):
                    sp.wait_ge(a_pj, g * len(a["jobs"]) + JB[l])
                    sp.sem_inc(a_ld, 1)
                    for n, dst in enumerate((wq_s, wk_s)):
                        if l == 1:
                            sp.dma_start(dst[:, :, :, :].rearrange("p (a j) r c -> p a (j r c)", a=1)[:, :, 0:P], src[n][:, one(g), :]).then_inc(a_w, 16)
                        else:
                            for r in range(2):
                                sp.dma_start(dst[:, :, r, :].rearrange("p (a j) c -> p a j c", a=1),
                                               src[n][:, one(g), :].rearrange("p a (j c) -> p a j c", j=2)).then_inc(a_w, 16)
                    sp.dma_start(wv_s[:, :].rearrange("p (a c) -> p a c", a=1), src[2][:, one(g), :]).then_inc(a_w, 16)
                    sp.wait_ge(a_y, g * B + OB[l])
                    sp.sem_inc(a_ld, 1)
                    sp.dma_start(wo_s[:, :].rearrange("p (a c) -> p a c", a=1), src[3][:, one(g), :]).then_inc(a_wo, 16)

                load(0)
                with sp.Fori(1, a["ng"]) as g:
                    load(g)

            def load_expert(f, u, e):
                n = f["nc"]
                for name, dst in (("w1", w1_s[u]), ("w0", w0_s[u])):
                    if f[name]:
                        sp.dma_start(dst[:, 0:n * P].rearrange("p (a f) -> p a f", a=1),
                                     t[f[name]].rearrange("e p f -> p e f")[:, one(e), :]).then_inc(f_w[u], 16)
                sp.dma_start(w2_s[u][:, 0:n, :].rearrange("p (a c) d -> p a c d", a=1),
                             t[f["w2"]].rearrange("e (c p) d -> p e c d", p=P)[:, one(e), :, :]).then_inc(f_w[u], 16)

            for l, f in enumerate(FFN[:NL_FFN]):
                if l == 0:
                    sp.wait_ge(z_s, B)
                for u in range(2):
                    wait(sp, f_ws[u], l * E // 2)
                    load_expert(f, u, u)
                with sp.Fori(0, E // 2 - 1) as i:
                    for u in range(2):
                        sp.wait_ge(f_ws[u], i + (l * E // 2 + 1))
                        load_expert(f, u, i * 2 + (2 + u))
                if 0 < 2 * (l + 1) < N_SUB:
                    group_weights(l + 1)
            for b in range(B):
                sp.wait_ge(x_new, B * (N_SUB - 1) + b + 1)
                sp.dma_start(out_d[b], x_tok[:, tiles(b), :]).then_inc(out_sem, 16)
            sp.wait_ge(out_sem, 16 * B)

        def start_at_one(eng, sems):
            for s_ in sems:
                eng.sem_inc(s_, 1)

        @block.gpsimd
        def _(pool):
            start_at_one(pool, (a_z,))
            for n in range(3):
                pool.memset(wP[n][:, :], 0.0)
            pool.memset(woP[:, :, :], 0.0).then_inc(zeroed, 1)
            pool.dma_start(ctx_tok[:, :, :], t["ctx_1024"].rearrange("b (c p) d -> p (b c) d", p=CK)).then_inc(in_ctx, 16)
            pool.memset(ident[:, :], 0.0).then_inc(const_g, 1)
            pool.memset(tri[:, :], 1.0).then_inc(const_g, 1)
            pool.memset(sel_src[:, :, :], 0.0).then_inc(const_g, 1)
            pool.memset(ones[:, :], 1.0)
            pool.memset(mhalf[:, :], -0.5)
            pool.iota(iota8[:, :], [[1, E]], base=0, channel_multiplier=0, allow_small_or_imprecise_dtypes=True)
            pool.wait_ge(const_g, 3)
            pool.affine_select(out=ident[:, :], in_=ident[:, :], compare_op=ALU.not_equal, fill=1.0, base=0,
                               pattern=[[-1, P]], channel_multiplier=1)
            pool.affine_select(out=tri[:, :], in_=tri[:, :], compare_op=ALU.is_ge, fill=0.0, base=0,
                               pattern=[[1, P]], channel_multiplier=-1)
            pool.affine_select(out=sel_src[:, :, :], in_=sel_src[:, :, :], compare_op=ALU.not_equal, fill=1.0, base=0,
                               pattern=[[-1, E], [0, P]], channel_multiplier=1).then_inc(const_g, 1)
            pool.wait_ge(const_g, 4)
            pool.affine_select(out=sel_src[:, :, :], in_=sel_src[:, :, :], compare_op=ALU.not_equal, fill=1.0, base=-LO,
                               pattern=[[-1, E], [0, P]], channel_multiplier=1).then_inc(const_g, 1)
            for n in range(3):
                pool.iota(rep_i[:, n:n + 1], [[1, 1]], base=0, channel_multiplier=1)
            pool.memset(acc[:, :], 0.0).then_inc(const_g, 1)

            def rstd(j):
                for b in range(B):
                    pool.wait_ge(ln_var, B * j + b + 1)
                    pool.tensor_tensor(ln_r[:, tiles(b)], ln_v[:, tiles(b)], mhalf[:, tiles(b)], ALU.pow).then_inc(ln_rstd, 1)

            def normalise(l):
                NM = B * TB * ATT[l]["nh"]
                with pool.Fori(0, ATT[l]["ng"]) as g:
                    for m in range(NM):
                        pool.wait_ge(a_r, g * NM + (MB[l] + m + 1))
                        u = m % NPT
                        pool.tensor_tensor(pt[u], pt[u], rc[:, u, :].rearrange("p (h a) -> p h a", a=1).broadcast_to([P, 2, SK]),
                                           ALU.mult).then_inc(a_z, 1)

            def split_weights(l):
                f = FFN[l]
                n = f["nc"]
                nd = 3 if f["w0"] else 2

                def split(i, u):
                    pool.wait_ge(f_w[u], i * (16 * nd) + (WB[l] + 16 * nd))
                    pairs = [(w1_s[u][:, 0:n * P], w1_p[u]), (w2_s[u][:, 0:n, :].rearrange("p c d -> p (c d)"), w2_p[u])]
                    if f["w0"]:
                        pairs.append((w0_s[u], w0_p[u]))
                    for w, (hi, lo) in pairs:
                        ins = pool.tensor_tensor(hi[:, 0:n * P], w, ones[:, 0:1].broadcast_to([P, n * P]), ALU.mult)
                    ins.then_inc(f_wh, 1)
                    pool.wait_ge(f_wh, i * 2 + (E * l + u + 1))
                    for w, (hi, lo) in pairs:
                        ins = pool.tensor_tensor(lo[:, 0:n * P], w, hi[:, 0:n * P].bitcast(F32), ALU.subtract)
                    ins.then_inc(f_ws[u], 1)

                split(0, 0)
                split(0, 1)
                with pool.Fori(1, E // 2) as i:
                    for u in range(2):
                        pool.wait_ge(f_y, i * (2 * B) + (KB[l] + B * (u + 1) - 2 * B))
                        split(i, u)

            j = 0
            for s in range(N_SUB):
                l = s // 2
                rstd(j)
                j += 1
                if s == 4:
                    rstd(j)
                    j += 1
                if s % 2:
                    split_weights(l)
                elif l:
                    normalise(l)

        @block.scalar
        def _(act):
            start_at_one(act, (f_a, f_hh, a_hi, a_e, a_ta, a_o))

            def copy_(out_, in_, sem_, **kw):
                return act.activation(out_, in_, ACT.Identity, **kw).then_inc(sem_, 1)

            for m in range(2):
                act.wait_ge(ctxT_ps, m + 1)
                copy_(ctxT[:, m * 2 * SK:(m + 1) * 2 * SK], ps[:, m, 0:2 * SK], ctxT_ok)
            act.wait_ge(bias_ps, 1)
            copy_(biasT[:, 0:P], ps[:, 2, 0:P], bias_ok)
            act.wait_ge(in_vec, 16 * 9)
            act.activation(tgate[:, :], gate[:, :], ACT.Tanh).then_inc(gate_ok, 1)
            def xT(s):
                if s == 4:
                    act.wait_ge(const_v, 1)
                for b in range(B):
                    act.wait_ge(xT_ps, B * s + b + 1)
                    if s == 4:
                        act.activation(xnT[:, bsl(b)], ps[:, b, :], ACT.Identity, bias=beta[:, 0:1], scale=gamma[:, 0:1]).then_inc(xT_ok, 1)
                    else:
                        copy_(xnT[:, bsl(b)], ps[:, b, :], xT_ok, **(dict(scale=ATT[s // 2]["scale"]) if s in (2, 6) else {}))
                if s % 2:
                    for b in range(B):
                        copy_(x_hi[:, bsl(b)], ps[:, b, :], f_xh)

            def attention0():
                act.wait_ge(z_cps, 1)
                copy_(cj[:, :], ps[0:CK, 4, 0:B * KC], z_c, bias=b_sim[0:CK, 0:1])
                for b in range(B):
                    act.wait_ge(z_mT, b + 1)
                    act.activation(nm0[:, bsl(b)], ps[0:1, 6, :], ACT.Copy, scale=-1.0).then_inc(z_nm, 1)
                    act.wait_ge(z_bps, b + 1)
                    act.activation(nbmax[:, b:b + 1], ps[:, 7, 0:1], ACT.Copy, scale=-1.0).then_inc(z_nb, 1)
                    act.wait_ge(z_nb, b + 1)
                    act.activation(eb[:, tiles(b)], mx0b[:, tiles(b)], ACT.Exp, bias=nbmax[:, b:b + 1]).then_inc(z_eb, 1)
                act.wait_ge(z_c, 1)
                for b in range(B):
                    act.wait_ge(z_s, b + 1)
                    if b >= 2:
                        act.wait_ge(z_o, b - 1)
                    for c in range(KC):
                        n = b * KC + c
                        act.activation(prob[b % 2][:, c, :], ps[0:CK, 2 * (b % 2) + c, :], ACT.Exp, bias=cj[:, n:n + 1]).then_inc(z_p, 1)
                    if b >= 1:
                        y_out(b - 1)
                y_out(B - 1)

            def y_out(b):
                act.wait_ge(z_y, b + 1)
                copy_(acc[:, bsl(b)], ps[:, 7, :], z_acc, bias=b_qv[:, 0:1])

            def attention(l):
                a = ATT[l]
                hg, nh, jobs = a["hg"], a["nh"], a["jobs"]
                NJ, NM, NP = len(jobs), B * TB * nh, B * nh

                def high(g, n):
                    kind, j, b = jobs[n]
                    act.wait_ge(a_pj, at(g, NJ, JB[l] + n + 1))
                    if kind == "q":
                        if n >= 2:
                            act.wait_ge(a_pd, at(g, NJ, JB[l] + n - 1))
                        dst, src = q_h[:, n % 2, :], ps[:, 2 + n % 4, :]
                    else:
                        if l == 1:
                            act.wait_ge(a_pd, at(g, NJ, JB[l] + n))
                        dst = kz_h[:, :] if l == 1 else k_hi[:, j, b * 2 * SK:(b + 1) * 2 * SK]
                        src = ps[:, 2 + n % 4, 0:2 * SK]
                    act.activation(dst, src, ACT.Identity).then_inc(a_hi, 1)

                def exps(g, m):
                    act.wait_ge(a_m, at(g, NM, MB[l] + m + 1))
                    for j in range(2):
                        ins = act.activation(pt[m % NPT][:, j, :], ps[:, m % 2, j * SK:(j + 1) * SK], ACT.Exp, bias=nmx[:, m % NPT, j:j + 1])
                    ins.then_inc(a_e, 1)

                def copy_first(g, p):
                    if p >= 0:
                        act.wait_ge(a_t, at(g, NP, PB[l] + p + 1))
                        act.activation(prob[(p // nh % 2) * hg + 2 * (p % nh)][:, :, :], ps[0:CK, 2:4, :], ACT.Identity).then_inc(a_ta, 1)

                def copy_out(g, b):
                    if b >= 0:
                        act.wait_ge(a_pv, at(g, B, OB[l] + b + 1))
                        act.wait_ge(a_y, at(g, B, OB[l] + b))
                        act.activation(oT[:, :], ps[:, 6, :], ACT.Identity).then_inc(a_o, 1)

                def heads(g):
                    for m in range(NM):
                        b, h, k = m // TB // nh, m // TB % nh, m % TB
                        exps(g, m)
                        if k == 0:
                            copy_first(g, m // TB - 1)
                        if h == 0 and k == TB - 1:
                            copy_out(g, b - 1)

                def between(g, following):
                    if g:
                        copy_first(g, NP - 1)
                    if following:
                        for n in range(4):
                            high(following, n)
                    if g:
                        copy_out(g, B - 1)
                    if following:
                        for n in range(4, NJ - 2):
                            high(following, n)

                between(None, (0, 0))
                act.preload_act_table(ACT.Exp)
                with act.Fori(0, a["ng"] - 1) as i:
                    heads((i, 0))
                    between((i, 0), (i, 1))
                last = (a["ng"] - 1, 0)
                heads(last)
                between(last, None)

            def ffn(l):
                f = FFN[l]
                n = f["nc"]
                act.wait_ge(f_d, l + 1)
                if l == 1:
                    act.activation(dexp[:, :, :], dexp[:, :, :], ACT.Exp).then_inc(f_e, 1)
                else:
                    act.activation(r_e[:, :], r_d[:, :], ACT.Exp).then_inc(f_e, 1)
                for b in range(B):
                    act.wait_ge(f_cps, B * l + b + 1)
                    copy_(cTf[:, bsl(b)], ps[0:E, 6 + b % 2, :], f_cf)
                if f["b2"]:
                    for b in range(B):
                        act.wait_ge(f_ips, B * IB[l] + b + 1)
                        copy_(acc[:, bsl(b)], ps[:, 4 + b % 2, :], f_init)
                act.preload_act_table(f["act"])
                with act.Fori(0, E // 2) as i:
                    def wait_unit(sem_, A):
                        act.wait_ge(sem_, i * (2 * B * n) + A)

                    for k in range(2 * B):
                        u = k // B
                        h_hi = h_p[k % 2][0]
                        for c in range(n):
                            A = AB[l] + n * k + c
                            bias = {} if l == 2 else dict(bias=b1_slot[u][:, c:c + 1])
                            wait_unit(f_h, A + 1)
                            if f["w0"]:
                                wait_unit(f_hd, A - c if k == 0 and c < 2 else A - 1)
                                act.activation(gS[c % 2][:, :], ps[:, c % 2, :], f["act"], **bias).then_inc(f_a, 1)
                                if c:
                                    wait_unit(f_hd, A)
                                    act.activation(h_hi[:, c - 1, :], h_f[:, (c - 1) % 2, :], ACT.Identity).then_inc(f_hh, 1)
                            else:
                                wait_unit(f_hl, A - c if k == 0 and c < 2 else A - 1)
                                act.activation(h_hi[:, c, :], ps[:, c, :], f["act"], **bias)
                                act.activation(h_f[:, c % 2, :], ps[:, c, :], f["act"], **bias).then_inc(f_a, 1)
                        if f["w0"]:
                            wait_unit(f_hd, A + 1)
                            act.activation(h_hi[:, n - 1, :], h_f[:, (n - 1) % 2, :], ACT.Identity).then_inc(f_hh, 1)

            for s in range(N_SUB):
                xT(s)
                if s % 2:
                    ffn(s // 2)
                elif s == 0:
                    attention0()
                else:
                    attention(s // 2)

        @block.vector
        def _(dve):
            start_at_one(dve, (f_yd, f_ym, f_hd, f_hl, a_pd, a_m, a_sm, a_r, a_td, a_acc))

            step = [0]

            def link(ins):
                step[0] += 1
                ins.then_inc(vec, 1)
                dve.wait_ge(vec, step[0])

            dve.wait_ge(const_g, 6)
            dve.tensor_copy(sel_all[:, 0:E, :], sel_src[:, :, :])
            dve.tensor_copy(sel_all[:, E, :], acc[0:LO + E, 0:P])
            dve.tensor_copy(biasT[:, P:P + 4], acc[:, 0:4])
            dve.tensor_copy(ones_r[:, :], ones[0:1, 0:CK])
            dve.tensor_copy(ident_bf[:, :], ident[:, :])
            for n, bit in enumerate((3, 4, 6)):
                link(dve.tensor_scalar(rep_i[:, n:n + 1], rep_i[:, n:n + 1], bit, 1, ALU.logical_shift_right, ALU.bitwise_and))
            link(dve.tensor_copy(neg_lo[:, :], rep_i[:, :]))
            link(dve.tensor_scalar(neg_lo[:, :], neg_lo[:, :], -1.0, None, ALU.mult))
            link(dve.tensor_copy(cT[:, :], acc[0:LO + E, :]))
            dve.wait_ge(in_vec, 16 * 9)
            link(dve.tensor_scalar(w2rep[:, :], ones[:, :], w_sim[:, 1:2], None, ALU.mult))
            for w in (gamma, beta):
                link(dve.tensor_scalar(w[:, :], w[:, :], ATT[2]["scale"], None, ALU.mult))
            dve.sem_inc(const_v, 1)
            dve.wait_ge(in_x, 16 * B)

            def layer_norm(j, src, scaled=False):
                for b in range(B):
                    tb = tiles(b)
                    link(dve.tensor_reduce(ln_s[:, tb], src[:, tb, :], AX.X, ALU.add))
                    link(dve.tensor_scalar(ln_s[:, tb], ln_s[:, tb], -1.0 / D, None, ALU.mult))
                    mean = ln_s[:, tb].rearrange("p (n a) -> p n a", a=1).broadcast_to([P, TB, D])
                    link(dve.tensor_tensor(xn_tok[:, tb, :], src[:, tb, :], mean, ALU.add))
                    link(dve.tensor_tensor(ln_sq, xn_tok[:, tb, :], xn_tok[:, tb, :], ALU.mult))
                    link(dve.tensor_reduce(ln_v[:, tb], ln_sq, AX.X, ALU.add))
                    dve.tensor_scalar(ln_v[:, tb], ln_v[:, tb], 1.0 / D, EPS, ALU.mult, ALU.add).then_inc(ln_var, 1)
                    dve.wait_ge(ln_rstd, B * j + b + 1)
                    if scaled:
                        link(dve.tensor_tensor(ln_r[:, tb], ln_r[:, tb], row_any[:, tb], ALU.mult))
                    r = ln_r[:, tb].rearrange("p (n a) -> p n a", a=1).broadcast_to([P, TB, D])
                    dve.tensor_tensor(xn_tok[:, tb, :], xn_tok[:, tb, :], r, ALU.mult).then_inc(ln_ok, 1)
                    dve.wait_ge(ln_ok, B * j + b + 1)

            def finish(s):
                for b in range(B):
                    dve.wait_ge(accT_ps, B * s + b + 1)
                    dve.tensor_tensor(x_tok[:, tiles(b), :], x_tok[:, tiles(b), :],
                                      ps[:, 6 + b % 2, :].rearrange("p (n d) -> p n d", n=TB), ALU.add).then_inc(x_new, 1)
                    dve.wait_ge(x_new, B * s + b + 1)

            def mask_bias():
                dve.wait_ge(in_mask, 16)
                for n in range(NT):
                    link(dve.tensor_scalar(mask_f[:, :], mask_i[:, n, :], 0.0, None, ALU.not_equal))
                    link(dve.tensor_reduce(row_any[:, n:n + 1], mask_f[:, :], AX.X, ALU.max))
                    link(dve.tensor_scalar(row_neg[:, n:n + 1], row_any[:, n:n + 1], -NEG, None, ALU.mult))
                    dve.tensor_scalar(mask_bf[:, n, :], mask_f[:, :], 1.0, row_neg[:, n:n + 1], ALU.subtract, ALU.mult).then_inc(mb_ok, 1)
                    dve.wait_ge(mb_ok, n + 1)

            def replicate_columns():
                dve.wait_ge(in_l1, 16 * (3 * HEADS + 16))
                for w in wP[0:2]:
                    cols = w[:, :].rearrange("p (h r o) -> p h r o", r=4, o=8)
                    for r in range(1, 4):
                        ins = dve.tensor_copy(cols[:, :, r, :], cols[:, :, 0, :])
                ins.then_inc(l1_rep, 1)

            def attention0():
                dve.wait_ge(ctxT_ok, 2)
                dve.tensor_scalar(keys0[:, :], ctxT[:, :], w_sim[:, 2:3], w_sim[:, 0:1], ALU.mult, ALU.add).then_inc(z_pre, 1)
                for b in range(B):
                    dve.wait_ge(z_sc, b + 1)
                    link(dve.tensor_reduce(mx0[:, tiles(b)], ps[:, 0:TB, 0:SK], AX.X, ALU.max))
                    dve.tensor_scalar(mx0b[:, tiles(b)], mx0[:, tiles(b)], b_sim[:, 0:1], None, ALU.add).then_inc(z_mx, 1)
                    dve.wait_ge(z_nm, b + 1)
                    dve.tensor_reduce(bmax[:, b:b + 1], ps[0:1, 6, :], AX.X, ALU.max).then_inc(z_bm, 1)
                    dve.wait_ge(z_hps, b + 1)
                    link(dve.reciprocal(hc_r[:, b:b + 1], ps[:, 7, 2:3]))
                    dve.tensor_tensor(hc[:, b:b + 1], ps[:, 7, 4:5], hc_r[:, b:b + 1], ALU.mult).then_inc(z_hc, 1)
                dve.wait_ge(z_hc, B)
                for b in range(B):
                    dve.wait_ge(z_o, b + 1)
                    wait(dve, z_y, b)
                    link(dve.reciprocal(rsum[:, :], ps[:, 5, :]))
                    link(dve.tensor_tensor(hqT, ps[:, 4, :], rsum[:, :], ALU.mult))
                    dve.tensor_tensor(xhq, hqT, xnT[:, bsl(b)], ALU.mult)
                    dve.tensor_scalar(xhc[:, :], xnT[:, bsl(b)], hc[:, b:b + 1], None, ALU.mult).then_inc(z_f, 1)

            def attention(l):
                a = ATT[l]
                hg, nh, rows, jobs = a["hg"], a["nh"], a["rows"], a["jobs"]
                dve.memset(acc[:, :], 0.0).then_inc(a_zero, 1)
                dve.wait_ge(a_zero, l)
                if l == 1:
                    for j in range(4):
                        ins = dve.tensor_copy(kz[:, j, :], acc[:, 0:B * SK])
                    link(ins)
                NJ, NM, NP = len(jobs), B * TB * nh, B * nh

                def low(g, n):
                    kind, j, b = jobs[n]
                    if kind == "v":
                        dve.wait_ge(a_pj, at(g, NJ, JB[l] + n + 1))
                        dve.tensor_copy(v[:, 4 * b:4 * b + 4, :], ps[0:CK, 2 + n % 4, :].rearrange("p (n c) -> p n c", n=4)).then_inc(a_pd, 1)
                        return
                    dve.wait_ge(a_hi, at(g, NJ - 2, HB[l] + n + 1))
                    ks = slice(b * 2 * SK, (b + 1) * 2 * SK)
                    if kind == "q":
                        m = 0 if l == 1 else 2
                        ins = dve.scalar_tensor_tensor(out=q_s[:, j, bsl(b)], in0=q_h[:, n % 2, :].bitcast(F32), scalar=neg_lo[:, m:m + 1],
                                                       in1=ps[:, 2 + n % 4, :], op0=ALU.mult, op1=ALU.add)
                    elif l == 1:
                        for i in range(hg):
                            r = slice(rows * i, rows * i + rows)
                            ins = dve.scalar_tensor_tensor(out=kz[r, i, ks], in0=kz_h[r, :].bitcast(F32), scalar=neg_lo[r, 1:2],
                                                           in1=ps[r, 2 + n % 4, 0:2 * SK], op0=ALU.mult, op1=ALU.add)
                    else:
                        ins = dve.tensor_tensor(k_lo[:, j, ks], ps[:, 2 + n % 4, 0:2 * SK], k_hi[:, j, ks].bitcast(F32), ALU.subtract)
                    ins.then_inc(a_pd, 1)

                def maxima(g, m):
                    if m < NM:
                        dve.wait_ge(a_s, at(g, NM, MB[l] + m + 1))
                        dve.tensor_reduce(nmx[:, m % NPT, :], ps[:, m % 2, 0:2 * SK].rearrange("p (h s) -> p h s", h=2),
                                          AX.X, ALU.max, negate=True).then_inc(a_m, 1)

                def inverses(g, m):
                    u = m % NPT
                    dve.wait_ge(a_e, at(g, NM, MB[l] + m + 1))
                    dve.tensor_reduce(sm[:, u, :], pt[u], AX.X, ALU.add).then_inc(a_sm, 1)
                    dve.wait_ge(a_sm, at(g, NM, MB[l] + m + 1))
                    dve.reciprocal(rc[:, u, :], sm[:, u, :]).then_inc(a_r, 1)

                def copy_second(g, p):
                    if p >= 0:
                        dve.wait_ge(a_t, at(g, NP, PB[l] + p + 1))
                        dve.tensor_copy(prob[(p // nh % 2) * hg + 2 * (p % nh) + 1][:, :, :], ps[0:CK, 4:6, :]).then_inc(a_td, 1)

                def add_up(g, b):
                    if b >= 0:
                        dve.wait_ge(a_y, at(g, B, OB[l] + b + 1))
                        dve.wait_ge(a_acc, at(g, B, OB[l] + b))
                        dve.tensor_tensor(acc[:, bsl(b)], acc[:, bsl(b)], ps[:, 7, :], ALU.add).then_inc(a_acc, 1)

                def heads(g):
                    for m in range(NM):
                        b, h, k = m // TB // nh, m // TB % nh, m % TB
                        inverses(g, m)
                        maxima(g, m + 2)
                        if k == 0:
                            copy_second(g, m // TB - 1)
                            if h == 0:
                                add_up(g, b - 2)

                def between(g, following):
                    if g:
                        copy_second(g, NP - 1)
                    if following:
                        for n in range(4):
                            low(following, n)
                    if g:
                        add_up(g, B - 2)
                    if following:
                        for n in range(4, NJ - 4 if l > 1 else NJ - 2):
                            low(following, n)
                    if g:
                        add_up(g, B - 1)
                    if following:
                        for n in range(NJ - 4 if l > 1 else NJ - 2, NJ):
                            low(following, n)
                        maxima(following, 0)
                        maxima(following, 1)

                between(None, (0, 0))
                with dve.Fori(0, a["ng"] - 1) as i:
                    heads((i, 0))
                    between((i, 0), (i, 1))
                last = (a["ng"] - 1, 0)
                heads(last)
                between(last, None)
                dve.wait_ge(a_acc, OB[l + 1])
                for b in range(B):
                    if l == 1:
                        dve.tensor_scalar(acc[:, bsl(b)], acc[:, bsl(b)], bo1[:, 0:1], None, ALU.add).then_inc(a_fin, 1)
                    elif l == 2:
                        dve.wait_ge(gate_ok, 1)
                        dve.tensor_scalar(acc[:, bsl(b)], acc[:, bsl(b)], bo2[:, 0:1], tgate[:, 0:1], ALU.add, ALU.mult).then_inc(a_fin, 1)

            def wide(ap):
                return ap.rearrange("p (n a) -> p n a", a=1).broadcast_to([P, NT, E])

            def routing(l):
                f = FFN[l]
                dve.wait_ge(f_lg, l + 1)
                logits = ps[:, 5, 0:NT * E].rearrange("p (n e) -> p n e", e=E)
                if f["bg"]:
                    row = bg[:, {0: 0, 3: 1}[l]:{0: 0, 3: 1}[l] + 1, :].broadcast_to([P, NT, E])
                    link(dve.tensor_tensor(lg[:, :, :], logits, row, ALU.add))
                else:
                    link(dve.tensor_copy(lg[:, :, :], logits))
                for n in range(NT):
                    ins = dve.max(m8[:, n, :], lg[:, n, :])
                link(ins)
                for n in range(NT):
                    ins = dve.max_index(ix8[:, n, :], m8[:, n, :], lg[:, n, :])
                link(ins)
                link(dve.tensor_copy(ixf[:, :, :], ix8[:, :, 0:2]))
                ex = iota8[:, :].rearrange("p (a e) -> p a e", a=1).broadcast_to([P, NT, E])
                for k in range(1 if l == 1 else 2):
                    link(dve.tensor_tensor(oh[:, k, :, :], ex, ixf[:, :, k:k + 1].broadcast_to([P, NT, E]), ALU.is_equal))
                if l == 1:
                    dve.tensor_tensor(dexp[:, :, :], lg[:, :, :], m8[:, :, 0:1].broadcast_to([P, NT, E]), ALU.subtract).then_inc(f_d, 1)
                    link(dve.memset(cum[0][:, 0:1, :], 0.0))
                    link(dve.tensor_copy(cum[0][:, 1:NT, :], oh[:, 0, 0:NT - 1, :]))
                    k, d = 0, 1
                    while d < NT:
                        dve.tensor_copy(cum[1 - k][:, 0:d, :], cum[k][:, 0:d, :])
                        link(dve.tensor_tensor(cum[1 - k][:, d:NT, :], cum[k][:, d:NT, :], cum[k][:, 0:NT - d, :], ALU.add))
                        k, d = 1 - k, 2 * d
                    dve.sem_inc(f_oh, 1)
                    dve.wait_ge(f_e, l + 1)
                    link(dve.tensor_reduce(r_s[:, :], dexp[:, :, :], AX.X, ALU.add))
                    link(dve.reciprocal(r_w[:, 0, :], r_s[:, :]))
                    dve.wait_ge(f_rank, 1)
                    link(dve.tensor_scalar(comb2[:, :, :], ps[:, 6, 0:NT * E].rearrange("p (n e) -> p n e", e=E),
                                           float(CAPACITY), None, ALU.is_le))
                    link(dve.tensor_tensor(comb2[:, :, :], comb2[:, :, :], oh[:, 0, :, :], ALU.mult))
                    dve.tensor_tensor(comb[:, :, :], comb2[:, :, :], wide(r_w[:, 0, :]), ALU.mult).then_inc(f_comb, 1)
                else:
                    dve.tensor_tensor(r_d[:, :].rearrange("p (n a) -> p n a", a=1), m8[:, :, 1:2], m8[:, :, 0:1], ALU.subtract).then_inc(f_d, 1)
                    dve.wait_ge(f_e, l + 1)
                    link(dve.tensor_scalar(r_s[:, :], r_e[:, :], 1.0, None, ALU.add))
                    link(dve.reciprocal(r_w[:, 0, :], r_s[:, :]))
                    link(dve.tensor_tensor(r_w[:, 1, :], r_w[:, 0, :], r_e[:, :], ALU.mult))
                    link(dve.tensor_tensor(comb[:, :, :], oh[:, 0, :, :], wide(r_w[:, 0, :]), ALU.mult))
                    link(dve.tensor_tensor(comb2[:, :, :], oh[:, 1, :, :], wide(r_w[:, 1, :]), ALU.mult))
                    dve.tensor_tensor(comb[:, :, :], comb[:, :, :], comb2[:, :, :], ALU.add).then_inc(f_comb, 1)
                if not f["b2"]:
                    dve.memset(acc[:, :], 0.0).then_inc(f_init2, 1)
                for b in range(B):
                    dve.wait_ge(f_xh, B * l + b + 1)
                    dve.tensor_tensor(x_lo[:, bsl(b)], xnT[:, bsl(b)], x_hi[:, bsl(b)].bitcast(F32), ALU.subtract).then_inc(f_xl, 1)
                for b in range(B):
                    dve.wait_ge(f_cf, B * l + b + 1)
                    link(dve.tensor_copy(cT[0:E, bsl(b)], cTf[:, bsl(b)]))
                    dve.tensor_tensor(cT[LO:LO + E, bsl(b)], cTf[:, bsl(b)], cT[0:E, bsl(b)].bitcast(F32), ALU.subtract).then_inc(f_c, 1)

            def ffn(l):
                f = FFN[l]
                n = f["nc"]
                routing(l)
                if f["b2"]:
                    dve.wait_ge(f_init, B * IB[l] + B)
                else:
                    dve.wait_ge(f_init2, 1)
                def slots(e, u):
                    for slot, base in ((b1_slot[u], {0: 0, 1: 64, 2: None, 3: 96}[l]), (b0_slot[u], 32 if f["w0"] else None)):
                        if base is not None:
                            dve.tensor_copy(slot[:, :].rearrange("p (a c) -> p a c", a=1),
                                            biasT[:, base:base + (E + 1) * n].rearrange("p (e c) -> p e c", c=n)[:, one(e), :])
                    dve.tensor_copy(sel_slot[u][:, :].rearrange("p (a c) -> p a c", a=1), sel_all[:, one(e), :]).then_inc(f_sel, 1)

                slots(0, 0)
                with dve.Fori(0, E // 2) as i:
                    def wait_unit(sem_, A):
                        dve.wait_ge(sem_, i * (2 * B * n) + A)

                    def y_acc(k):
                        K = KB[l] + k
                        dve.wait_ge(f_y, i * (2 * B) + (K + 1))
                        dve.wait_ge(f_yd, i * (2 * B) + K)
                        dve.tensor_copy(yw[:, :], ps[:, 6 + k % 2, :]).then_inc(f_ym, 1)
                        dve.wait_ge(f_ym, i * (4 * B) + 2 * K)
                        dve.tensor_tensor(yw[:, :], ps[:, 4 + k % 2, :], yw[:, :], ALU.mult).then_inc(f_ym, 1)
                        dve.wait_ge(f_ym, i * (4 * B) + (2 * K + 1))
                        dve.tensor_tensor(acc[:, bsl(k % B)], acc[:, bsl(k % B)], yw[:, :], ALU.add).then_inc(f_yd, 1)

                    def low(k, c):
                        hi, lo = h_p[k % 2]
                        wait_unit(f_hh if f["w0"] else f_a, AB[l] + n * k + c + 1)
                        dve.tensor_tensor(lo[:, c, :], h_f[:, c % 2, :], hi[:, c, :].bitcast(F32), ALU.subtract).then_inc(f_hl, 1)

                    slots(i * 2 + 1, 1)
                    for k in range(2 * B):
                        if f["w0"] and k % B == 0:
                            dve.wait_ge(f_sel, i * 2 + ((E + 1) * l + k // B + 1))
                        for c in range(n):
                            if f["w0"]:
                                A = AB[l] + n * k + c
                                wait_unit(f_a, A + 1)
                                wait_unit(f_hl, A - c if k == 0 and c < 2 else A - 1)
                                dve.scalar_tensor_tensor(out=h_f[:, c % 2, :], in0=ps[:, 2 + c % 2, :], scalar=b0_slot[k // B][:, c:c + 1],
                                                         in1=gS[c % 2][:, :], op0=ALU.add, op1=ALU.mult).then_inc(f_hd, 1)
                                if c:
                                    low(k, c - 1)
                            else:
                                low(k, c)
                        if f["w0"]:
                            low(k, n - 1)
                        if k:
                            y_acc(k - 1)
                        if k == B:
                            slots(i * 2 + 2, 0)
                    y_acc(2 * B - 1)

            j = 0
            for s in range(N_SUB):
                if s == 1:
                    mask_bias()
                    replicate_columns()
                layer_norm(j, x_tok, scaled=(s == 2))
                j += 1
                if s == 4:
                    layer_norm(j, xn_tok)
                    j += 1
                if s % 2:
                    ffn(s // 2)
                elif s == 0:
                    attention0()
                else:
                    attention(s // 2)
                finish(s)

        @block.tensor
        def _(pe):
            start_at_one(pe, (f_h, f_y, a_pj, a_s, a_t, a_pv, a_y))

            mm = pe.matmul
            pe.wait_ge(const_g, 6)
            pe.wait_ge(in_ctx, 16)
            for m in range(2):
                for n in range(4):
                    last = pe.transpose(ps[:, m, n * CK:(n + 1) * CK], ctx_tok[:, 4 * m + n, :], ident[0:CK, 0:CK])
                last.then_inc(ctxT_ps, 1)
            pe.wait_ge(in_ffn, 16 * 13)
            pe.transpose(ps[:, 2, 0:P], bias_rows[:, :], ident[:, :]).then_inc(bias_ps, 1)

            def xT(s):
                for b in range(B):
                    pe.wait_ge(ln_ok, B * (s + (1 if s >= 4 else 0)) + b + 1)
                    if b == 0 and s:
                        pe.wait_ge(xT_ok, B * s)
                    if s == 0:
                        pe.wait_ge(ctxT_ok, 2)
                        pe.wait_ge(bias_ok, 1)
                    for k in range(TB):
                        last = pe.transpose(ps[:, b, k * P:(k + 1) * P], xn_tok[:, b * TB + k, :], ident[:, :])
                    last.then_inc(xT_ps, 1)

            def finish(s, sem_, base):
                for b in range(B):
                    pe.wait_ge(sem_, base + (min(b + 3, B) if s % 2 else B))
                    if b >= 2:
                        pe.wait_ge(x_new, B * s + b - 1)
                    for k in range(TB):
                        last = pe.transpose(ps[:, 6 + b % 2, k * P:(k + 1) * P], acc[:, b * S + k * P:b * S + (k + 1) * P], ident[:, :])
                    last.then_inc(accT_ps, 1)

            def attention0():
                pe.wait_ge(z_pre, 1)
                pe.wait_ge(const_v, 1)
                for n in range(B * KC):
                    last = mm(ps[0:CK, 4, n:n + 1], ctxT[:, n * CK:(n + 1) * CK], w_sim[:, 1:2], start=True, stop=True)
                last.then_inc(z_cps, 1)
                for b in range(B):
                    keys = slice(b * SK, (b + 1) * SK)
                    pe.wait_ge(xT_ok, B)
                    wait(pe, z_mx, b)
                    for k in range(TB):
                        mm(ps[:, k, 0:SK], xnT[:, b * S + k * P:b * S + (k + 1) * P], keys0[:, keys], start=True, stop=False)
                        last = mm(ps[:, k, 0:SK], w2rep[:, :], ctxT[:, keys], start=False, stop=True)
                    last.then_inc(z_sc, 1)
                    pe.wait_ge(z_mx, b + 1)
                    wait(pe, z_bm, b)
                    for k in range(TB):
                        last = pe.transpose(ps[0:1, 6, k * P:(k + 1) * P], mx0b[:, b * TB + k:b * TB + k + 1], ident[:, :])
                    last.then_inc(z_mT, 1)
                    pe.wait_ge(z_bm, b + 1)
                    wait(pe, z_hc, b)
                    mm(ps[:, 7, 0:1], ones[0:1, :], bmax[:, b:b + 1], start=True, stop=True).then_inc(z_bps, 1)
                    pe.wait_ge(z_eb, b + 1)
                    for k in range(TB):
                        mm(ps[:, 7, 2:3], ones[:, :], eb[:, b * TB + k:b * TB + k + 1], start=(k == 0), stop=(k == TB - 1))
                    for k in range(TB):
                        last = mm(ps[:, 7, 4:5], xn_tok[:, b * TB + k, :], eb[:, b * TB + k:b * TB + k + 1], start=(k == 0), stop=(k == TB - 1))
                    last.then_inc(z_hps, 1)
                pe.wait_ge(z_nm, B)
                pe.wait_ge(z_c, 1)
                pe.wait_ge(z_hc, B)

                def scores(b):
                    if b >= 2:
                        pe.wait_ge(z_p, KC * (b - 1))
                    for c in range(KC):
                        n = b * KC + c
                        bank = ps[0:CK, 2 * (b % 2) + c, :]
                        mm(bank, keys0[:, n * CK:(n + 1) * CK], xnT[:, bsl(b)], start=True, stop=False)
                        last = mm(bank, ones_r[:, :], nm0[:, bsl(b)], start=False, stop=True)
                    last.then_inc(z_s, 1)

                scores(0)
                for b in range(B):
                    if b + 1 < B:
                        scores(b + 1)
                    pe.wait_ge(z_p, KC * (b + 1))
                    wait(pe, z_f, b)
                    for c in range(KC):
                        mm(ps[:, 4, :], ctx_tok[:, b * KC + c, :], prob[b % 2][:, c, :], start=(c == 0), stop=(c == KC - 1))
                    for c in range(KC):
                        last = mm(ps[:, 5, :], ones[0:CK, :], prob[b % 2][:, c, :], start=(c == 0), stop=(c == KC - 1))
                    last.then_inc(z_o, 1)
                    pe.wait_ge(z_f, b + 1)
                    wait(pe, z_acc, b)
                    for k, feat in enumerate((xnT[:, bsl(b)], hqT, xhq, xhc[:, :])):
                        last = mm(ps[:, 7, :], w_qv[:, k, :], feat, start=(k == 0), stop=(k == 3))
                    last.then_inc(z_y, 1)

            def attention(l):
                a = ATT[l]
                hg, rows, nh, jobs = a["hg"], a["rows"], a["nh"], a["jobs"]
                NM, NJ, NP = B * TB * nh, len(jobs), B * nh
                pe.wait_ge(xT_ok, B * (2 * l + 1))
                if l == 1:
                    pe.wait_ge(mb_ok, NT)
                nw = 3 if l == 1 else 5

                def proj(g, n):
                    kind, j, b = jobs[n]
                    if n == 0:
                        pe.wait_ge(a_w, at(g, 16 * nw, AW[l] + 16 * nw))
                    if n < 4:
                        pe.wait_ge(a_ta, at(g, NP, PB[l]))
                        pe.wait_ge(a_td, at(g, NP, PB[l]))
                    else:
                        pe.wait_ge(a_pd, at(g, NJ, JB[l] + n - 3))
                    wq, wk = (w[:, :, :, :].rearrange("p j r c -> p j (r c)")[:, j, :] for w in (wq_s, wk_s))
                    if kind == "q":
                        last = mm(ps[:, 2 + n % 4, :], wq, xnT[:, bsl(b)], start=True, stop=True)
                    elif kind == "k":
                        last = mm(ps[:, 2 + n % 4, 0:2 * SK], wk, ctxT[:, b * 2 * SK:(b + 1) * 2 * SK], start=True, stop=True)
                    else:
                        for i in range(4):
                            last = mm(ps[0:CK, 2 + n % 4, i * P:(i + 1) * P], ctxT[:, (4 * b + i) * CK:(4 * b + i + 1) * CK], wv_s[:, :], start=True, stop=True)
                    last.then_inc(a_pj, 1)

                def scores(g, m):
                    if m >= NM:
                        return
                    b, h, k = m // TB // nh, m // TB % nh, m % TB
                    tile, keys = b * TB + k, slice(b * SK, (b + 1) * SK)
                    if m == 0:
                        pe.wait_ge(a_pd, at(g, NJ, JB[l] + 2 * a["nj"]))
                    pe.wait_ge(a_e, at(g, NM, MB[l] + max(m - 1, 0)))
                    q = [q_s[:, j, tile * P:(tile + 1) * P] for j in range(2)]
                    if l == 1:
                        bank = ps[:, m % 2, 0:2 * SK].rearrange("p (h s) -> p h s", h=2)
                        mm(bank, q[0], kz[:, 2 * h:2 * h + 2, keys], start=True, stop=False)
                        last = mm(bank, ident_bf[:, :], mask_bf[:, tile:tile + 1, :].broadcast_to([P, 2, SK]), start=False, stop=True)
                    else:
                        for j in range(2):
                            bank = ps[:, m % 2, j * SK:(j + 1) * SK]
                            mm(bank, q[j], k_hi[:, j, keys], start=True, stop=False)
                            last = mm(bank, q[j], k_lo[:, j, keys], start=False, stop=True)
                    last.then_inc(a_s, 1)

                def transposes(g, m):
                    p, k = m // TB, m % TB
                    if m == 0:
                        pe.wait_ge(a_pd, at(g, NJ, JB[l] + NJ))
                    elif k == 0:
                        pe.wait_ge(a_ta, at(g, NP, PB[l] + p))
                        pe.wait_ge(a_td, at(g, NP, PB[l] + p))
                    pe.wait_ge(a_z, at(g, NM, MB[l] + m + 1))
                    for j in range(2):
                        for c in range(KC):
                            last = pe.transpose(ps[0:CK, 2 + 2 * j + c, k * P:(k + 1) * P], pt[m % NPT][:, j, c * CK:(c + 1) * CK], ident[:, :])
                    if k == TB - 1:
                        last.then_inc(a_t, 1)

                def values(g, b, c):
                    if b < 0:
                        return
                    if c == 0:
                        pe.wait_ge(a_ta, at(g, NP, PB[l] + (b + 1) * nh))
                        pe.wait_ge(a_td, at(g, NP, PB[l] + (b + 1) * nh))
                        pe.wait_ge(a_o, at(g, B, OB[l] + b))
                    for j in range(hg):
                        r = slice(rows * j, rows * j + rows)
                        last = mm(ps[r, 6, :], v[:, b * KC + c, r], prob[(b % 2) * hg + j][:, c, :], start=(c == 0), stop=(c == KC - 1))
                    if c == KC - 1:
                        last.then_inc(a_pv, 1)

                def project(g, b):
                    if b >= 0:
                        pe.wait_ge(a_o, at(g, B, OB[l] + b + 1))
                        pe.wait_ge(a_wo, at(g, 16, 16 * GB[l]))
                        pe.wait_ge(a_acc, at(g, B, OB[l] + b))
                        mm(ps[:, 7, :], wo_s[:, :], oT[:, :], start=True, stop=True).then_inc(a_y, 1)

                def heads(g):
                    for m in range(NM):
                        b, h, k = m // TB // nh, m // TB % nh, m % TB
                        if h == 0 and k == 0:
                            project(g, b - 2)
                        scores(g, m + 3)
                        transposes(g, m)
                        if h == 0 and k < KC:
                            values(g, b - 1, k)

                def between(g, following):
                    if g:
                        project(g, B - 2)
                    if following:
                        for n in range(4):
                            proj(following, n)
                    if g:
                        for c in range(KC):
                            values(g, B - 1, c)
                    if following:
                        for n in range(4, NJ - 4 if l > 1 else NJ - 2):
                            proj(following, n)
                    if g:
                        project(g, B - 1)
                    if following:
                        for n in range(NJ - 4 if l > 1 else NJ - 2, NJ):
                            proj(following, n)
                            if n >= NJ - 2:
                                scores(following, n - (NJ - 2))
                        scores(following, 2)

                between(None, (0, 0))
                with pe.Fori(0, a["ng"] - 1) as i:
                    heads((i, 0))
                    between((i, 0), (i, 1))
                last_g = (a["ng"] - 1, 0)
                heads(last_g)
                between(last_g, None)

            def ffn(l):
                f = FFN[l]
                n = f["nc"]
                pe.wait_ge(xT_ok, B * (2 * l + 2))
                for k in range(NT):
                    last = mm(ps[:, 5, k * E:(k + 1) * E], xnT[:, k * P:(k + 1) * P], wg[:, l, :], start=True, stop=True)
                last.then_inc(f_lg, 1)
                if l == 1:
                    pe.wait_ge(f_oh, 1)
                    pe.wait_ge(x_new, B * (2 * l + 1))
                    mm(ps[:, 6, 0:NT * E], tri[:, :], oh[:, 0, :, :], start=True, stop=False)
                    mm(ps[:, 6, 0:NT * E], ones[:, :], cum[0][:, :, :], start=False, stop=True).then_inc(f_rank, 1)
                pe.wait_ge(f_comb, l + 1)
                for b in range(B):
                    if b >= 2:
                        pe.wait_ge(f_cf, B * l + b - 1)
                    for k in range(TB):
                        last = pe.transpose(ps[0:E, 6 + b % 2, k * P:(k + 1) * P], comb[:, b * TB + k, :], ident[:, :])
                    last.then_inc(f_cps, 1)
                if f["b2"]:
                    for b in range(B):
                        pe.wait_ge(f_cf, B * l + b + 1)
                        if b >= 2:
                            pe.wait_ge(f_init, B * IB[l] + b - 1)
                        mm(ps[:, 4 + b % 2, :], b2[:, IB[l], :], cTf[:, bsl(b)], start=True, stop=True).then_inc(f_ips, 1)
                    pe.wait_ge(f_init, B * IB[l] + B)
                pe.wait_ge(f_cf, B * l + B)
                pe.wait_ge(f_c, B * l + B)
                pe.wait_ge(f_xl, B * l + B)

                def product(bank, w, x, first=True, last=True):
                    mm(bank, w[0], x[0], start=first, stop=False)
                    mm(bank, w[0], x[1], start=False, stop=False)
                    return mm(bank, w[1], x[0], start=False, stop=last)

                with pe.Fori(0, E // 2) as i:
                    def hidden(k):
                        u, b, K = k // B, k % B, KB[l] + k
                        if b == 0:
                            pe.wait_ge(f_ws[u], i + (l * E // 2 + 1))
                            pe.wait_ge(f_sel, i * 2 + ((E + 1) * l + u + 1))
                        x = (x_hi[:, bsl(b)], x_lo[:, bsl(b)])
                        for c in range(n):
                            A = AB[l] + n * k + c
                            cs = slice(c * P, (c + 1) * P)
                            w1 = [w[:, cs] for w in w1_p[u]]
                            if f["w0"]:
                                back = A - c if k == 0 and c < 2 else A - 1
                                wait(pe, f_a, i * (2 * B * n) + back)
                                product(ps[:, c % 2, :], w1, x)
                                wait(pe, f_hd, i * (2 * B * n) + back)
                                product(ps[:, 2 + c % 2, :], [w[:, cs] for w in w0_p[u]], x).then_inc(f_h, 1)
                            else:
                                wait(pe, f_a, i * (2 * B * n) + (A - c if k == 0 else A - n + 1))
                                product(ps[:, c, :], w1, x).then_inc(f_h, 1)

                    def down(k):
                        u, K = k // B, KB[l] + k
                        wait(pe, f_yd, i * (2 * B) + (K if k == 0 else K - 1))
                        mm(ps[:, 6 + k % 2, :], sel_slot[u][:, :], cT[:, bsl(k % B)], start=True, stop=True)
                        for c in range(n):
                            pe.wait_ge(f_hl, i * (2 * B * n) + (AB[l] + n * k + c + 1))
                            last = product(ps[:, 4 + k % 2, :], [w[:, c * P:(c + 1) * P] for w in w2_p[u]],
                                           [h[:, c, :] for h in h_p[k % 2]], first=(c == 0), last=(c == n - 1))
                        last.then_inc(f_y, 1)

                    for k in range(2 * B):
                        hidden(k)
                        if k:
                            down(k - 1)
                    down(2 * B - 1)

            for s in range(N_SUB):
                l = s // 2
                xT(s)
                if s % 2:
                    ffn(l)
                    finish(s, f_yd, KB[l + 1] - B)
                elif s == 0:
                    attention0()
                    finish(0, z_acc, 0)
                else:
                    attention(l)
                    finish(s, *((a_fin, B * (l - 1)) if l < 3 else (a_acc, OB[4] - B)))


NL_FFN = 4
N_SUB = 8
IB = {0: 0, 1: 1, 3: 2}


def kernel(**inputs):
    import numpy as _np
    import concourse.bacc as _bacc
    from concourse.bass_utils import run_bass_kernel_spmd as _run

    nc = _bacc.Bacc("TRN2", target_bir_lowering=False, num_devices=1)
    arrays, args = {}, {}
    for name, value in inputs.items():
        a = _np.ascontiguousarray(value)
        arrays[f"in_{name}"] = a
        args[name] = nc.dram_tensor(f"in_{name}", a.shape, mybir.dt.from_np(a.dtype), kind="ExternalInput").ap()
    shape = arrays["in_x"].shape
    out = nc.dram_tensor("out_0", shape, mybir.dt.float32, kind="ExternalOutput").ap()
    xattn_moe_stack(nc, args, out)
    r = _run(nc, [arrays], core_ids=[0])
    return r.results[0]["out_0"]
```

```python
import concourse.bass as bass
from concourse import mybir
from contextlib import ExitStack


def xattn_moe_stack(nc, t, out):
    F32, F32R, BF16 = mybir.dt.float32, mybir.dt.float32r, mybir.dt.bfloat16
    U32, I32 = mybir.dt.uint32, mybir.dt.int32
    ALU, ACT, AX = mybir.AluOpType, mybir.ActivationFunctionType, mybir.AxisListType

    B, S, D = t["x"].shape
    SK = t["ctx_1024"].shape[1]
    P = 128
    TB = S // P
    NT = B * TB
    KC = 2
    CK = SK // KC
    E = t["L0_ffn_Wg"].shape[1]
    HEADS = 16
    EPS = 1e-5
    CAPACITY = int(B * S / E * 1.25) + 1
    NEG = -1e20
    NPT = 4
    LO = 32
    NLN = 9

    FFN = [
        dict(w1="L0_ffn_W1", w0="L0_ffn_W0", w2="L0_ffn_W2", wg="L0_ffn_Wg", bg="L0_ffn_bg", b2="L0_ffn_b2", act=ACT.Silu),
        dict(w1="L1_ffn_W1", w0=None, w2="L1_ffn_W2", wg="L1_ffn_wg", bg=None, b2="L1_ffn_b2", act=ACT.Gelu),
        dict(w1="L2_ffn_w1", w0=None, w2="L2_ffn_w2", wg="L2_ffn_wg", bg=None, b2=None, act=ACT.Gelu),
        dict(w1="L3_ffn_W1", w0=None, w2="L3_ffn_W2", wg="L3_ffn_W_router", bg="L3_ffn_b_router", b2="L3_ffn_b2", act=ACT.Relu),
    ]
    for f in FFN:
        f["nc"] = t[f["w1"]].shape[2] // P
    KB = [1 + l * E * B for l in range(5)]
    AB = [1 + sum(f["nc"] for f in FFN[:l]) * E * B for l in range(5)]
    WB = [sum(3 if f["w0"] else 2 for f in FFN[:l]) * 16 * (E // 2) for l in range(5)]

    ATT = [None, dict(hg=4, dh=8, scale=D ** -0.5), dict(hg=2, dh=64, scale=64 ** -0.5), dict(hg=2, dh=64, scale=64 ** -0.5)]
    for a in ATT[1:]:
        a["ng"] = HEADS // a["hg"]
        a["rows"] = P // a["hg"]
        a["nh"] = a["hg"] // 2
    JOBS = [("q", 0), ("k", 0), ("q", 1), ("q", 2), ("q", 3), ("k", 1), ("v", 0), ("v", 1)]
    NJ = len(JOBS)

    def before(count):
        out_, n = [0, 1], 1
        for a in ATT[1:]:
            n += count(a) * a["ng"]
            out_.append(n)
        return out_

    GB = before(lambda a: 1)
    OB = before(lambda a: B)
    PB = before(lambda a: B * a["nh"])
    MB = before(lambda a: B * TB * a["nh"])
    JB = before(lambda a: NJ)
    HB = before(lambda a: NJ - 2)

    def wait(eng, sem, value):
        if not isinstance(value, int) or value > 0:
            eng.wait_ge(sem, value)

    def at(g, k, c):
        return g[0] * k + (g[1] * k + c)

    def one(i):
        return slice(i, i + 1) if isinstance(i, int) else bass.ds(i, 1)

    with ExitStack() as ctx:
        def sb(name, shape, dt=F32):
            return ctx.enter_context(nc.sbuf_tensor(name, shape, dt))

        def sb_two(name, shape):
            offset = -(-nc.sbuf_base // 32) * 32
            room = sb(name, shape)
            return room, nc.alloc_sbuf_tensor_at(name + "_r", shape, F32R, offset=offset)

        def sem(name):
            return ctx.enter_context(nc.semaphore(name))

        x_tok = sb("x_tok", [P, NT, D])
        xn_tok = sb("xn_tok", [P, NT, D])
        xnT = sb("xnT", [P, B * S])
        acc = sb("acc", [P, B * S])
        ln_st = sb("ln_st", [P, NT, 6])
        ln_mv = sb("ln_mv", [P, NT, 2])
        ln_v = sb("ln_v", [P, NT])
        ln_r = sb("ln_r", [P, NT])
        mhalf = sb("mhalf", [P, NT])
        ident = sb("ident", [P, P])
        ones = sb("ones", [P, P])
        tri = sb("tri", [P, P])
        iota8 = sb("iota8", [P, E])
        ident_bf = sb("ident_bf", [P, P], BF16)
        sel_all = sb("sel_all", [LO + E, E + 1, P], F32R)
        sel_slot = [sb(f"sel_slot{u}", [LO + E, P], F32R) for u in range(2)]
        rep_i = sb("rep_i", [P, 2], I32)
        neg_lo = sb("neg_lo", [P, 2])
        ones_r = sb("ones_r", [1, CK], F32R)
        ctx_tok = sb("ctx_tok", [CK, B * KC, D])
        ctxT = sb("ctxT", [P, B * SK])
        mask_f = sb("mask_f", [P, TB, SK])
        mask_bf = sb("mask_bf", [P, NT, SK], BF16)
        row_any = sb("row_any", [P, NT])
        row_neg = sb("row_neg", [P, NT])
        w_sim = sb("w_sim", [P, 3])
        b_sim = sb("b_sim", [P, 1])
        b_qv = sb("b_qv", [P, 1])
        bo1 = sb("bo1", [P, 1])
        gamma = sb("gamma", [P, 1])
        beta = sb("beta", [P, 1])
        bo2 = sb("bo2", [P, 1])
        gate = sb("gate", [P, 1])
        tgate = sb("tgate", [P, 1])
        bias_rows = sb("bias_rows", [P, P])
        biasT = sb("biasT", [P, P + 4])
        b1_slot = [sb(f"b1_slot{u}", [P, 4]) for u in range(2)]
        b0_slot = [sb(f"b0_slot{u}", [P, 4]) for u in range(2)]
        w_qv = sb("w_qv", [P, 4, D])
        keys0 = sb("keys0", [P, B * SK])
        w2rep = sb("w2rep", [P, P])
        cj = sb("cj", [CK, B * KC])
        mx0 = sb("mx0", [P, NT])
        mx0b = sb("mx0b", [P, NT])
        nm0 = sb("nm0", [1, B * S], F32R)
        bmax = sb("bmax", [1, B])
        nbmax = sb("nbmax", [P, B])
        eb = sb("eb", [P, NT])
        hc_r = sb("hc_r", [P, B])
        hc = sb("hc", [P, B])
        xhc = sb("xhc", [P, S])
        wP = [sb(f"wP{n}", [P, 4 * P]) for n in range(3)]
        woP = sb("woP", [P, 4, P])
        wq_s = sb("wq_s", [P, P])
        wk_s = sb("wk_s", [P, P])
        wv_s = sb("wv_s", [P, P])
        wo_s = sb("wo_s", [P, P])
        q_s = sb("q_s", [P, 2, B * S], F32R)
        q_h = sb("q_h", [P, 2, S], F32R)
        kz_h = sb("kz_h", [P, 2 * SK], F32R)
        kz = sb("kz", [P, 4, B * SK], F32R)
        k_hi = sb("k_hi", [P, 2, B * SK], F32R)
        k_lo = sb("k_lo", [P, 2, B * SK], F32R)
        v_room, v_room_r = sb_two("v_room", [P, B * KC * P])
        v = v_room[0:CK, :].rearrange("p (n c) -> p n c", c=P)
        nmx = sb("nmx", [P, NPT, 2])
        sm = sb("sm", [P, NPT, 2])
        rc = sb("rc", [P, NPT, 2])
        h_room, h_room_r = sb_two("h_room", [P, 2 * 4 * S])
        p_room, p_room_r = sb_two("p_room", [P, 4 * KC * S])
        prob = [r[0:CK, n * KC * S:(n + 1) * KC * S].rearrange("p (c s) -> p c s", c=KC) for r in (p_room, h_room) for n in range(4)]
        rsum = sb("rsum", [P, S])
        oT = sb("oT", [P, S])
        wg = sb("wg", [P, 4, E])
        bg = sb("bg", [P, 2, E])
        b2 = sb("b2", [E, 3, D])
        lg = sb("lg", [P, NT, E])
        m8 = sb("m8", [P, NT, 8])
        ix8 = sb("ix8", [P, NT, 8], U32)
        ixf = sb("ixf", [P, NT, 2])
        oh = sb("oh", [P, 2, NT, E])
        dexp = sb("dexp", [P, NT, E])
        r_d = sb("r_d", [P, NT])
        r_e = sb("r_e", [P, NT])
        r_s = sb("r_s", [P, NT])
        r_w = sb("r_w", [P, 2, NT])
        cum = [sb(f"cum{n}", [P, NT, E]) for n in range(2)]
        comb = sb("comb", [P, NT, E])
        comb2 = sb("comb2", [P, NT, E])
        cTf = xn_tok[0:E, :, :].rearrange("p n d -> p (n d)")
        cT = sb("cT", [LO + E, B * S], F32R)
        w1_s = [sb(f"w1_s{u}", [P, 4 * P]) for u in range(2)]
        w0_s = [v_room[:, 0:4 * P], keys0[:, 0:4 * P]]
        w2_s = [sb(f"w2_s{u}", [P, 4, D]) for u in range(2)]
        w0_lo = sb("w0_lo", [P, 4 * P], F32R)
        x_hi, x_lo = q_s[:, 0, :], q_s[:, 1, :]
        kz_flat = kz[:, :, :].rearrange("p j s -> p (j s)")
        k_flat = [k[:, :, :].rearrange("p j s -> p (j s)") for k in (k_hi, k_lo)]
        w1_p = [[kz_flat[:, (2 * u + n) * 4 * P:(2 * u + n + 1) * 4 * P] for n in range(2)] for u in range(2)]
        w0_p = [[q_h[:, 0, :], v_room_r[:, 4 * P:8 * P]], [q_h[:, 1, :], w0_lo[:, :]]]
        w2_p = [[k[:, u * 4 * P:(u + 1) * 4 * P] for k in k_flat] for u in range(2)]
        h_p = [[r[:, n * 4 * S:(n + 1) * 4 * S].rearrange("p (c s) -> p c s", c=4) for r in (h_room_r, p_room_r)] for n in range(2)]
        mask_i = h_room[:, 0:NT * SK].bitcast(I32).rearrange("p (n s) -> p n s", n=NT)
        gS = [xhc, oT]
        hqT = [p_room[:, (4 + u) * S:(5 + u) * S] for u in range(2)]
        xhq = [p_room[:, (6 + u) * S:(7 + u) * S] for u in range(2)]
        xhcs = [xhc[:, :], h_room[:, 5 * S:6 * S]]
        h_f = sb("h_f", [P, 2, S])
        sel_src = h_f[0:LO + E, :, :].rearrange("p a s -> p (a s)").rearrange("p (e c) -> p e c", e=E)
        yw = rsum
        h_flat = h_f[:, :, :].rearrange("p u s -> p (u s)")
        pt = [w.rearrange("p (h s) -> p h s", h=2) for w in [h_flat[:, 2 * SK * u:2 * SK * (u + 1)] for u in range(3)] + [rsum[:, 0:2 * SK]]]

        ps = ctx.enter_context(nc.psum_tensor("ps", [P, 8, 512], F32))

        in_x = sem("in_x")
        in_ctx = sem("in_ctx")
        in_vec = sem("in_vec")
        in_mask = sem("in_mask")
        in_ffn = sem("in_ffn")
        in_l1 = sem("in_l1")
        zeroed = sem("zeroed")
        const_g = sem("const_g")
        const_v = sem("const_v")
        vec = sem("vec")
        ctxT_ps = sem("ctxT_ps"); ctxT_ok = sem("ctxT_ok")
        bias_ps = sem("bias_ps"); bias_ok = sem("bias_ok")
        mb_ok = sem("mb_ok")
        gate_ok = sem("gate_ok")
        ln_var = sem("ln_var"); ln_rstd = sem("ln_rstd"); ln_ok = sem("ln_ok")
        xT_ps = sem("xT_ps"); xT_ok = sem("xT_ok")
        x_new = sem("x_new"); accT_ps = sem("accT_ps")
        z_pre = sem("z_pre"); z_cps = sem("z_cps"); z_c = sem("z_c")
        z_sc = sem("z_sc"); z_mx = sem("z_mx"); z_mT = sem("z_mT"); z_nm = sem("z_nm"); z_bm = sem("z_bm")
        z_bps = sem("z_bps"); z_nb = sem("z_nb"); z_eb = sem("z_eb"); z_hps = sem("z_hps"); z_hc = sem("z_hc")
        z_s = sem("z_s"); z_p = sem("z_p"); z_o = sem("z_o"); z_f = sem("z_f"); z_y = sem("z_y"); z_acc = sem("z_acc")
        a_ld = sem("a_ld"); a_kz = sem("a_kz"); a_w = sem("a_w"); a_wo = sem("a_wo")
        a_pj = sem("a_pj"); a_hi = sem("a_hi"); a_pd = sem("a_pd")
        a_s = sem("a_s"); a_m = sem("a_m"); a_e = sem("a_e"); a_sm = sem("a_sm"); a_r = sem("a_r"); a_z = sem("a_z")
        a_t = sem("a_t"); a_ta = sem("a_ta"); a_td = sem("a_td"); a_pv = sem("a_pv"); a_o = sem("a_o")
        a_y = sem("a_y"); a_acc = sem("a_acc"); a_zero = sem("a_zero"); a_fin = sem("a_fin")
        f_lg = sem("f_lg"); f_d = sem("f_d"); f_e = sem("f_e"); f_oh = sem("f_oh"); f_rank = sem("f_rank")
        f_comb = sem("f_comb"); f_cps = sem("f_cps"); f_cf = sem("f_cf"); f_c = sem("f_c")
        f_ips = sem("f_ips"); f_init = sem("f_init")
        f_w = [sem("f_w0"), sem("f_w1")]
        f_ws = [sem("f_ws0"), sem("f_ws1")]
        f_wh = sem("f_wh"); f_sel = sem("f_sel"); f_xh = sem("f_xh"); f_xl = sem("f_xl"); f_hh = sem("f_hh"); f_hl = sem("f_hl")
        f_h = sem("f_h"); f_a = sem("f_a"); f_hd = sem("f_hd"); f_y = sem("f_y"); f_yd = sem("f_yd")
        l1_rep = sem("l1_rep"); f_init2 = sem("f_init2"); f_ym = sem("f_ym")
        out_sem = sem("out_sem")

        block = ctx.enter_context(nc.Block())

        def bsl(b):
            return slice(b * S, (b + 1) * S)

        def tiles(b):
            return slice(b * TB, (b + 1) * TB)

        x_d = t["x"].rearrange("b (n p) d -> b p n d", p=P)
        out_d = out.rearrange("b (n p) d -> b p n d", p=P)

        def col(name):
            return t[name].rearrange("(p a) -> p a", a=1)

        @block.sync
        def _(sp):
            for b in range(B):
                sp.dma_start(x_tok[:, tiles(b), :], x_d[b]).then_inc(in_x, 16)
            sp.dma_start(w_sim[:, :], t["L0_xattn_w_sim"].rearrange("(a p) -> p a", a=3), allow_slow_non_contiguous=True).then_inc(in_vec, 16)
            sp.dma_start(b_sim[:, :], t["L0_xattn_b_sim"].rearrange("(p a) -> p a", a=1).broadcast_to([P, 1])).then_inc(in_vec, 16)
            sp.dma_start(b_qv[:, :], col("L0_xattn_b_qv")).then_inc(in_vec, 16)
            sp.dma_start(bo1[:, :], col("L1_xattn_bo")).then_inc(in_vec, 16)
            sp.dma_start(gamma[:, :], col("L2_xattn_ln_gamma")).then_inc(in_vec, 16)
            sp.dma_start(beta[:, :], col("L2_xattn_ln_beta")).then_inc(in_vec, 16)
            sp.dma_start(bo2[:, :], col("L2_xattn_b_out")).then_inc(in_vec, 16)
            sp.dma_start(gate[:, :], t["L2_xattn_gate"].rearrange("(p a) -> p a", a=1).broadcast_to([P, 1])).then_inc(in_vec, 16)
            sp.dma_start(w_qv[:, :, :], t["L0_xattn_W_qv"].rearrange("(k p) d -> p k d", p=P)).then_inc(in_vec, 16)
            for l, f in enumerate(FFN):
                sp.dma_start(wg[:, l, :], t[f["wg"]]).then_inc(in_ffn, 16)
            for n, f in enumerate((FFN[0], FFN[3])):
                sp.dma_start(bg[:, n, :], t[f["bg"]].rearrange("(a e) -> a e", a=1).broadcast_to([P, E])).then_inc(in_ffn, 16)
            for n, l in enumerate((0, 1, 3)):
                sp.dma_start(b2[:, n, :], t[FFN[l]["b2"]]).then_inc(in_ffn, 16)
            for n, name in enumerate(("L0_ffn_b1", "L0_ffn_b0", "L1_ffn_b1", "L3_ffn_b1")):
                sp.dma_start(bias_rows[32 * n:32 * n + 32, :], t[name].rearrange("e (c p) -> (e c) p", p=P)).then_inc(in_ffn, 16)
            sp.dma_start(mask_i[:, :, :], t["mask_Bx1xSxS2_if1"].rearrange("b a (n p) s -> p (b a n) s", p=P)).then_inc(in_mask, 16)
            dh, rows = ATT[1]["dh"], ATT[1]["rows"]
            wait(sp, zeroed, 1)
            for n, name in enumerate(("L1_xattn_Wq", "L1_xattn_Wk", "L1_xattn_Wv")):
                for h in range(HEADS):
                    sp.dma_start(wP[n][dh * h:dh * h + dh, rows * h:rows * h + dh], t[name].rearrange("o d -> d o"), allow_slow_non_contiguous=True).then_inc(in_l1, 16)
            for j in range(4):
                for g in range(4):
                    h = 4 * g + j
                    sp.dma_start(woP[rows * j:rows * j + dh, g, :],
                                 t["L1_xattn_Wo"][:, dh * h:dh * h + dh].rearrange("e d -> d e"), allow_slow_non_contiguous=True).then_inc(in_l1, 16)

            def group_weights(l):
                a = ATT[l]
                if l == 1:
                    sp.wait_ge(in_l1, 16 * (3 * HEADS + 16))
                    sp.wait_ge(l1_rep, 1)
                    src = [w[:, :].rearrange("p (g c) -> p g c", g=4) for w in wP] + [woP[:, :, :]]
                elif l == 2:
                    kv = t["L2_xattn_w_kv"].rearrange("p (m g c) -> m p g c", m=2, c=P)
                    src = [t["L2_xattn_w_q"].rearrange("p (g c) -> p g c", c=P), kv[0], kv[1],
                           t["L2_xattn_w_out"].rearrange("(g p) e -> p g e", p=P)]
                else:
                    src = [t[f"L3_xattn_w_{m}"].rearrange("p (g c) -> p g c", c=P) for m in "qkv"] + \
                          [t["L3_xattn_w_o"].rearrange("(g p) e -> p g e", p=P)]

                def load(g):
                    sp.wait_ge(a_pj, g * NJ + JB[l])
                    sp.sem_inc(a_ld, 1)
                    for n, dst in enumerate((wq_s, wk_s, wv_s)):
                        sp.dma_start(dst[:, :].rearrange("p (a c) -> p a c", a=1), src[n][:, one(g), :]).then_inc(a_w, 16)
                    sp.wait_ge(a_y, g * B + OB[l])
                    sp.sem_inc(a_ld, 1)
                    sp.dma_start(wo_s[:, :].rearrange("p (a c) -> p a c", a=1), src[3][:, one(g), :]).then_inc(a_wo, 16)

                load(0)
                with sp.Fori(1, a["ng"]) as g:
                    load(g)

            def load_expert(f, u, e):
                n = f["nc"]
                for name, dst in (("w1", w1_s[u]), ("w0", w0_s[u])):
                    if f[name]:
                        sp.dma_start(dst[:, 0:n * P].rearrange("p (a f) -> p a f", a=1),
                                     t[f[name]].rearrange("e p f -> p e f")[:, one(e), :]).then_inc(f_w[u], 16)
                sp.dma_start(w2_s[u][:, 0:n, :].rearrange("p (a c) d -> p a c d", a=1),
                             t[f["w2"]].rearrange("e (c p) d -> p e c d", p=P)[:, one(e), :, :]).then_inc(f_w[u], 16)

            for l, f in enumerate(FFN[:NL_FFN]):
                if l == 0:
                    sp.wait_ge(z_s, B)
                for u in range(2):
                    wait(sp, f_ws[u], l * E // 2)
                    load_expert(f, u, u)
                with sp.Fori(0, E // 2 - 1) as i:
                    for u in range(2):
                        sp.wait_ge(f_ws[u], i + (l * E // 2 + 1))
                        load_expert(f, u, i * 2 + (2 + u))
                if 0 < 2 * (l + 1) < N_SUB:
                    group_weights(l + 1)
            for b in range(B):
                sp.wait_ge(x_new, B * (N_SUB - 1) + b + 1)
                sp.dma_start(out_d[b], x_tok[:, tiles(b), :]).then_inc(out_sem, 16)
            sp.wait_ge(out_sem, 16 * B)

        def start_at_one(eng, sems):
            for s_ in sems:
                eng.sem_inc(s_, 1)

        @block.gpsimd
        def _(pool):
            start_at_one(pool, (a_z,))
            for n in range(3):
                pool.memset(wP[n][:, :], 0.0)
            pool.memset(woP[:, :, :], 0.0).then_inc(zeroed, 1)
            pool.dma_start(ctx_tok[:, :, :], t["ctx_1024"].rearrange("b (c p) d -> p (b c) d", p=CK)).then_inc(in_ctx, 16)
            pool.memset(ident[:, :], 0.0).then_inc(const_g, 1)
            pool.memset(tri[:, :], 1.0).then_inc(const_g, 1)
            pool.memset(sel_src[:, :, :], 0.0).then_inc(const_g, 1)
            pool.memset(ones[:, :], 1.0)
            pool.memset(mhalf[:, :], -0.5)
            pool.iota(iota8[:, :], [[1, E]], base=0, channel_multiplier=0, allow_small_or_imprecise_dtypes=True)
            pool.wait_ge(const_g, 3)
            pool.affine_select(out=ident[:, :], in_=ident[:, :], compare_op=ALU.not_equal, fill=1.0, base=0,
                               pattern=[[-1, P]], channel_multiplier=1)
            pool.affine_select(out=tri[:, :], in_=tri[:, :], compare_op=ALU.is_ge, fill=0.0, base=0,
                               pattern=[[1, P]], channel_multiplier=-1)
            pool.affine_select(out=sel_src[:, :, :], in_=sel_src[:, :, :], compare_op=ALU.not_equal, fill=1.0, base=0,
                               pattern=[[-1, E], [0, P]], channel_multiplier=1).then_inc(const_g, 1)
            pool.wait_ge(const_g, 4)
            pool.affine_select(out=sel_src[:, :, :], in_=sel_src[:, :, :], compare_op=ALU.not_equal, fill=1.0, base=-LO,
                               pattern=[[-1, E], [0, P]], channel_multiplier=1).then_inc(const_g, 1)
            for n in range(2):
                pool.iota(rep_i[:, n:n + 1], [[1, 1]], base=0, channel_multiplier=1)
            pool.memset(acc[:, :], 0.0).then_inc(const_g, 1)

            def rstd(j):
                for b in range(B):
                    pool.wait_ge(ln_var, B * j + b + 1)
                    pool.tensor_tensor(ln_r[:, tiles(b)], ln_v[:, tiles(b)], mhalf[:, tiles(b)], ALU.pow).then_inc(ln_rstd, 1)

            def normalise(l):
                NM = B * TB * ATT[l]["nh"]
                with pool.Fori(0, ATT[l]["ng"]) as g:
                    for m in range(NM):
                        pool.wait_ge(a_r, g * NM + (MB[l] + m + 1))
                        u = m % NPT
                        pool.tensor_tensor(pt[u], pt[u], rc[:, u, :].rearrange("p (h a) -> p h a", a=1).broadcast_to([P, 2, SK]),
                                           ALU.mult).then_inc(a_z, 1)

            def split_weights(l):
                f = FFN[l]
                n = f["nc"]
                nd = 3 if f["w0"] else 2

                def split(i, u):
                    pool.wait_ge(f_w[u], i * (16 * nd) + (WB[l] + 16 * nd))
                    pairs = [(w1_s[u][:, 0:n * P], w1_p[u]), (w2_s[u][:, 0:n, :].rearrange("p c d -> p (c d)"), w2_p[u])]
                    if f["w0"]:
                        pairs.append((w0_s[u], w0_p[u]))
                    for w, (hi, lo) in pairs:
                        ins = pool.tensor_tensor(hi[:, 0:n * P], w, ones[:, 0:1].broadcast_to([P, n * P]), ALU.mult)
                    ins.then_inc(f_wh, 1)
                    pool.wait_ge(f_wh, i * 2 + (E * l + u + 1))
                    for w, (hi, lo) in pairs:
                        ins = pool.tensor_tensor(lo[:, 0:n * P], w, hi[:, 0:n * P].bitcast(F32), ALU.subtract)
                    ins.then_inc(f_ws[u], 1)

                split(0, 0)
                split(0, 1)
                with pool.Fori(1, E // 2) as i:
                    for u in range(2):
                        pool.wait_ge(f_y, i * (2 * B) + (KB[l] + B * (u + 1) - 2 * B))
                        split(i, u)

            j = 0
            for s in range(N_SUB):
                l = s // 2
                rstd(j)
                j += 1
                if s == 4:
                    rstd(j)
                    j += 1
                if s % 2:
                    split_weights(l)
                elif l:
                    normalise(l)

        @block.scalar
        def _(act):
            start_at_one(act, (f_a, f_hh, a_hi, a_e, a_ta, a_o))

            def copy_(out_, in_, sem_, **kw):
                return act.activation(out_, in_, ACT.Identity, **kw).then_inc(sem_, 1)

            for m in range(2):
                act.wait_ge(ctxT_ps, m + 1)
                copy_(ctxT[:, m * 2 * SK:(m + 1) * 2 * SK], ps[:, m, 0:2 * SK], ctxT_ok)
            act.wait_ge(bias_ps, 1)
            copy_(biasT[:, 0:P], ps[:, 2, 0:P], bias_ok)
            act.wait_ge(in_vec, 16 * 9)
            act.activation(tgate[:, :], gate[:, :], ACT.Tanh).then_inc(gate_ok, 1)
            def xT(s):
                if s == 4:
                    act.wait_ge(const_v, 1)
                for b in range(B):
                    act.wait_ge(xT_ps, B * s + b + 1)
                    if s == 4:
                        act.activation(xnT[:, bsl(b)], ps[:, b, :], ACT.Identity, bias=beta[:, 0:1], scale=gamma[:, 0:1]).then_inc(xT_ok, 1)
                    else:
                        copy_(xnT[:, bsl(b)], ps[:, b, :], xT_ok, **(dict(scale=ATT[s // 2]["scale"]) if s in (2, 6) else {}))
                if s % 2:
                    for b in range(B):
                        copy_(x_hi[:, bsl(b)], ps[:, b, :], f_xh)

            def attention0():
                act.wait_ge(z_cps, 1)
                copy_(cj[:, :], ps[0:CK, 4, 0:B * KC], z_c, bias=b_sim[0:CK, 0:1])
                for b in range(B):
                    act.wait_ge(z_mT, b + 1)
                    act.activation(nm0[:, bsl(b)], ps[0:1, 6, :], ACT.Copy, scale=-1.0).then_inc(z_nm, 1)
                act.wait_ge(z_bps, 1)
                act.activation(nbmax[:, :], ps[:, 7, 0:B], ACT.Copy, scale=-1.0).then_inc(z_nb, 1)
                act.wait_ge(z_nb, 1)
                for b in range(B):
                    act.activation(eb[:, tiles(b)], mx0b[:, tiles(b)], ACT.Exp, bias=nbmax[:, b:b + 1]).then_inc(z_eb, 1)
                act.wait_ge(z_c, 1)
                for b in range(B):
                    act.wait_ge(z_s, b + 1)
                    if b >= 2:
                        act.wait_ge(z_o, b - 1)
                    for c in range(KC):
                        n = b * KC + c
                        act.activation(prob[b % 2][:, c, :], ps[0:CK, c, :], ACT.Exp, bias=cj[:, n:n + 1]).then_inc(z_p, 1)
                    if b >= 2:
                        y_out(b - 2)
                y_out(B - 2)
                y_out(B - 1)

            def y_out(b):
                act.wait_ge(z_y, b + 1)
                copy_(acc[:, bsl(b)], ps[:, 6 + b % 2, :], z_acc, bias=b_qv[:, 0:1])

            def attention(l):
                a = ATT[l]
                hg, nh, rows = a["hg"], a["nh"], a["rows"]
                NM, NP = B * TB * nh, B * nh

                def high(g, n):
                    kind, b = JOBS[n]
                    act.wait_ge(a_pj, at(g, NJ, JB[l] + n + 1))
                    ks = slice(b * 2 * SK, (b + 1) * 2 * SK)
                    if l == 1:
                        if kind == "k" or n >= 2:
                            act.wait_ge(a_pd, at(g, NJ, JB[l] + n - (0 if kind == "k" else 1)))
                        if kind == "q":
                            ins = act.activation(q_h[:, n % 2, :], ps[:, 2 + n % 4, :], ACT.Identity)
                        else:
                            ins = act.activation(kz_h[:, :], ps[:, 2 + n % 4, 0:2 * SK], ACT.Identity)
                    elif kind == "q":
                        ins = act.activation(q_s[:, 0, bsl(b)], ps[:, 2 + n % 4, :], ACT.Identity)
                    else:
                        for i in range(hg):
                            r = slice(rows * i, rows * i + rows)
                            ins = act.activation(k_hi[r, i, ks], ps[r, 2 + n % 4, 0:2 * SK], ACT.Identity)
                    ins.then_inc(a_hi, 1)

                def exps(g, m):
                    act.wait_ge(a_m, at(g, NM, MB[l] + m + 1))
                    for j in range(2):
                        ins = act.activation(pt[m % NPT][:, j, :], ps[:, m % 2, j * SK:(j + 1) * SK], ACT.Exp, bias=nmx[:, m % NPT, j:j + 1])
                    ins.then_inc(a_e, 1)

                def copy_first(g, p):
                    if p >= 0:
                        act.wait_ge(a_t, at(g, NP, PB[l] + p + 1))
                        act.activation(prob[(p // nh % 2) * hg + 2 * (p % nh)][:, :, :], ps[0:CK, 2:4, :], ACT.Identity).then_inc(a_ta, 1)

                def copy_out(g, b):
                    if b >= 0:
                        act.wait_ge(a_pv, at(g, B, OB[l] + b + 1))
                        act.wait_ge(a_y, at(g, B, OB[l] + b))
                        act.activation(oT[:, :], ps[:, 6, :], ACT.Identity).then_inc(a_o, 1)

                def heads(g):
                    for m in range(NM):
                        b, h, k = m // TB // nh, m // TB % nh, m % TB
                        exps(g, m)
                        if k == 0:
                            copy_first(g, m // TB - 1)
                        if h == 0 and k == TB - 1:
                            copy_out(g, b - 1)

                def between(g, following):
                    if g:
                        copy_first(g, NP - 1)
                    if following:
                        for n in range(4):
                            high(following, n)
                    if g:
                        copy_out(g, B - 1)
                    if following:
                        for n in range(4, NJ - 2):
                            high(following, n)

                act.wait_ge(a_kz, l)
                between(None, (0, 0))
                act.preload_act_table(ACT.Exp)
                with act.Fori(0, a["ng"] - 1) as i:
                    heads((i, 0))
                    between((i, 0), (i, 1))
                last = (a["ng"] - 1, 0)
                heads(last)
                between(last, None)

            def ffn(l):
                f = FFN[l]
                n = f["nc"]
                act.wait_ge(f_d, l + 1)
                if l == 1:
                    act.activation(dexp[:, :, :], dexp[:, :, :], ACT.Exp).then_inc(f_e, 1)
                else:
                    act.activation(r_e[:, :], r_d[:, :], ACT.Exp).then_inc(f_e, 1)
                for b in range(B):
                    act.wait_ge(f_cps, B * l + b + 1)
                    copy_(cTf[:, bsl(b)], ps[0:E, 6 + b % 2, :], f_cf)
                if f["b2"]:
                    for b in range(B):
                        act.wait_ge(f_ips, B * IB[l] + b + 1)
                        copy_(acc[:, bsl(b)], ps[:, 4 + b % 2, :], f_init)
                act.preload_act_table(f["act"])
                with act.Fori(0, E // 2) as i:
                    def wait_unit(sem_, A):
                        act.wait_ge(sem_, i * (2 * B * n) + A)

                    for k in range(2 * B):
                        u = k // B
                        h_hi = h_p[k % 2][0]
                        for c in range(n):
                            A = AB[l] + n * k + c
                            bias = {} if l == 2 else dict(bias=b1_slot[u][:, c:c + 1])
                            wait_unit(f_h, A + 1)
                            if f["w0"]:
                                wait_unit(f_hd, A - c if k == 0 and c < 2 else A - 1)
                                act.activation(gS[c % 2][:, :], ps[:, c % 2, :], f["act"], **bias).then_inc(f_a, 1)
                                if c:
                                    wait_unit(f_hd, A)
                                    act.activation(h_hi[:, c - 1, :], h_f[:, (c - 1) % 2, :], ACT.Identity).then_inc(f_hh, 1)
                            else:
                                wait_unit(f_hl, A - c if k == 0 and c < 2 else A - 1)
                                act.activation(h_hi[:, c, :], ps[:, c, :], f["act"], **bias)
                                act.activation(h_f[:, c % 2, :], ps[:, c, :], f["act"], **bias).then_inc(f_a, 1)
                        if f["w0"]:
                            wait_unit(f_hd, A + 1)
                            act.activation(h_hi[:, n - 1, :], h_f[:, (n - 1) % 2, :], ACT.Identity).then_inc(f_hh, 1)

            for s in range(N_SUB):
                xT(s)
                if s % 2:
                    ffn(s // 2)
                elif s == 0:
                    attention0()
                else:
                    attention(s // 2)

        @block.vector
        def _(dve):
            start_at_one(dve, (f_yd, f_ym, f_hd, f_hl, a_pd, a_m, a_sm, a_r, a_td, a_acc))

            step = [0]

            def link(ins):
                step[0] += 1
                ins.then_inc(vec, 1)
                dve.wait_ge(vec, step[0])

            dve.wait_ge(const_g, 6)
            dve.tensor_copy(sel_all[:, 0:E, :], sel_src[:, :, :])
            dve.tensor_copy(sel_all[:, E, :], acc[0:LO + E, 0:P])
            dve.tensor_copy(biasT[:, P:P + 4], acc[:, 0:4])
            dve.tensor_copy(ones_r[:, :], ones[0:1, 0:CK])
            dve.tensor_copy(ident_bf[:, :], ident[:, :])
            for n, bit in enumerate((3, 4)):
                link(dve.tensor_scalar(rep_i[:, n:n + 1], rep_i[:, n:n + 1], bit, 1, ALU.logical_shift_right, ALU.bitwise_and))
            link(dve.tensor_copy(neg_lo[:, :], rep_i[:, :]))
            link(dve.tensor_scalar(neg_lo[:, :], neg_lo[:, :], -1.0, None, ALU.mult))
            link(dve.tensor_copy(cT[:, :], acc[0:LO + E, :]))
            dve.wait_ge(in_vec, 16 * 9)
            link(dve.tensor_scalar(w2rep[:, :], ones[:, :], w_sim[:, 1:2], None, ALU.mult))
            for w in (gamma, beta):
                link(dve.tensor_scalar(w[:, :], w[:, :], ATT[2]["scale"], None, ALU.mult))
            dve.sem_inc(const_v, 1)
            dve.wait_ge(in_x, 16 * B)

            def layer_norm(j, src, scaled=False, refresh=None):
                def statistics(b):
                    if refresh is not None:
                        finish(refresh, b)
                    for n in range(b * TB, (b + 1) * TB):
                        ins = dve.bn_stats(ln_st[:, n, :], src[:, n, :])
                    link(ins)
                    for n in range(b * TB, (b + 1) * TB):
                        ins = dve.bn_aggr(ln_mv[:, n, :], ln_st[:, n, :])
                    link(ins)
                    dve.tensor_scalar(ln_v[:, tiles(b)], ln_mv[:, tiles(b), 1], EPS, None, ALU.add).then_inc(ln_var, 1)

                def scale(b):
                    dve.wait_ge(ln_rstd, B * j + b + 1)
                    if scaled:
                        link(dve.tensor_tensor(ln_r[:, tiles(b)], ln_r[:, tiles(b)], row_any[:, tiles(b)], ALU.mult))
                    for n in range(b * TB, (b + 1) * TB):
                        ins = dve.tensor_scalar(xn_tok[:, n, :], src[:, n, :], ln_mv[:, n, 0:1], ln_r[:, n:n + 1], ALU.subtract, ALU.mult)
                    ins.then_inc(ln_ok, 1)
                    dve.wait_ge(ln_ok, B * j + b + 1)

                statistics(0)
                for b in range(1, B):
                    statistics(b)
                    scale(b - 1)
                scale(B - 1)

            def finish(s, b):
                dve.wait_ge(accT_ps, B * s + b + 1)
                dve.tensor_tensor(x_tok[:, tiles(b), :], x_tok[:, tiles(b), :],
                                  ps[:, 6 + b % 2, :].rearrange("p (n d) -> p n d", n=TB), ALU.add).then_inc(x_new, 1)
                dve.wait_ge(x_new, B * s + b + 1)

            def mask_bias(b):
                dve.wait_ge(in_mask, 16)
                link(dve.tensor_scalar(mask_f[:, :, :], mask_i[:, tiles(b), :], 0.0, 1.0, ALU.not_equal, ALU.subtract))
                link(dve.tensor_reduce(row_neg[:, tiles(b)], mask_f[:, :, :], AX.X, ALU.max))
                link(dve.tensor_scalar(row_any[:, tiles(b)], row_neg[:, tiles(b)], 1.0, None, ALU.add))
                link(dve.tensor_scalar(row_neg[:, tiles(b)], row_any[:, tiles(b)], -NEG, None, ALU.mult))
                dve.tensor_tensor(mask_bf[:, tiles(b), :], mask_f[:, :, :],
                                  row_neg[:, tiles(b)].rearrange("p (n a) -> p n a", a=1).broadcast_to([P, TB, SK]), ALU.mult).then_inc(mb_ok, 1)
                dve.wait_ge(mb_ok, b + 1)

            def replicate_columns():
                dve.wait_ge(in_l1, 16 * (3 * HEADS + 16))
                for w in wP[0:2]:
                    cols = w[:, :].rearrange("p (h r o) -> p h r o", r=4, o=8)
                    for r in range(1, 4):
                        ins = dve.tensor_copy(cols[:, :, r, :], cols[:, :, 0, :])
                ins.then_inc(l1_rep, 1)

            def attention0():
                dve.wait_ge(ctxT_ok, 2)
                dve.tensor_scalar(keys0[:, :], ctxT[:, :], w_sim[:, 2:3], w_sim[:, 0:1], ALU.mult, ALU.add).then_inc(z_pre, 1)
                def query_maxima(b):
                    dve.wait_ge(z_sc, b + 1)
                    link(dve.tensor_reduce(mx0[:, tiles(b)], ps[:, 0:TB, 0:SK], AX.X, ALU.max))
                    dve.tensor_scalar(mx0b[:, tiles(b)], mx0[:, tiles(b)], b_sim[:, 0:1], None, ALU.add).then_inc(z_mx, 1)

                def batch_maximum(b):
                    dve.wait_ge(z_nm, b + 1)
                    dve.tensor_reduce(bmax[:, b:b + 1], ps[0:1, 6, :], AX.X, ALU.max).then_inc(z_bm, 1)

                query_maxima(0)
                for b in range(1, B):
                    query_maxima(b)
                    batch_maximum(b - 1)
                batch_maximum(B - 1)
                replicate_columns()
                dve.wait_ge(z_hps, 1)
                link(dve.reciprocal(hc_r[:, :], ps[:, 7, 8:8 + B]))
                dve.tensor_tensor(hc[:, :], ps[:, 7, 16:16 + B], hc_r[:, :], ALU.mult).then_inc(z_hc, 1)
                dve.wait_ge(z_hc, 1)
                for b in range(B):
                    u = b % 2
                    dve.wait_ge(z_o, b + 1)
                    if b >= 2:
                        dve.wait_ge(z_y, b - 1)
                    link(dve.reciprocal(rsum[:, :], ps[:, 3 + 2 * u, :]))
                    link(dve.tensor_tensor(hqT[u], ps[:, 2 + 2 * u, :], rsum[:, :], ALU.mult))
                    dve.tensor_tensor(xhq[u], hqT[u], xnT[:, bsl(b)], ALU.mult)
                    dve.tensor_scalar(xhcs[u], xnT[:, bsl(b)], hc[:, b:b + 1], None, ALU.mult).then_inc(z_f, 1)
                    mask_bias(b)

            def attention(l):
                a = ATT[l]
                hg, nh, rows = a["hg"], a["nh"], a["rows"]
                dve.memset(acc[:, :], 0.0).then_inc(a_zero, 1)
                dve.wait_ge(a_zero, l)
                for k in [kz[:, j, :] for j in range(hg)] if l == 1 else [w[:, j, :] for w in (k_hi, k_lo) for j in range(hg)]:
                    ins = dve.tensor_copy(k, acc[:, 0:B * SK])
                ins.then_inc(a_kz, 1)
                dve.wait_ge(a_kz, l)
                NM, NP = B * TB * nh, B * nh

                def low(g, n):
                    kind, b = JOBS[n]
                    if kind == "v":
                        dve.wait_ge(a_pj, at(g, NJ, JB[l] + n + 1))
                        dve.tensor_copy(v[:, 4 * b:4 * b + 4, :], ps[0:CK, 2 + n % 4, :].rearrange("p (n c) -> p n c", n=4)).then_inc(a_pd, 1)
                        return
                    dve.wait_ge(a_hi, at(g, NJ - 2, HB[l] + n + 1))
                    ks = slice(b * 2 * SK, (b + 1) * 2 * SK)
                    if l == 1 and kind == "q":
                        ins = dve.scalar_tensor_tensor(out=q_s[:, 0, bsl(b)], in0=q_h[:, n % 2, :].bitcast(F32), scalar=neg_lo[:, 0:1],
                                                       in1=ps[:, 2 + n % 4, :], op0=ALU.mult, op1=ALU.add)
                    elif kind == "q":
                        ins = dve.tensor_tensor(q_s[:, 1, bsl(b)], ps[:, 2 + n % 4, :], q_s[:, 0, bsl(b)].bitcast(F32), ALU.subtract)
                    else:
                        for i in range(hg):
                            r = slice(rows * i, rows * i + rows)
                            src = ps[r, 2 + n % 4, 0:2 * SK]
                            if l == 1:
                                ins = dve.scalar_tensor_tensor(out=kz[r, i, ks], in0=kz_h[r, :].bitcast(F32), scalar=neg_lo[r, 1:2],
                                                               in1=src, op0=ALU.mult, op1=ALU.add)
                            else:
                                ins = dve.tensor_tensor(k_lo[r, i, ks], src, k_hi[r, i, ks].bitcast(F32), ALU.subtract)
                    ins.then_inc(a_pd, 1)

                def maxima(g, m):
                    if m < NM:
                        dve.wait_ge(a_s, at(g, NM, MB[l] + m + 1))
                        dve.tensor_reduce(nmx[:, m % NPT, :], ps[:, m % 2, 0:2 * SK].rearrange("p (h s) -> p h s", h=2),
                                          AX.X, ALU.max, negate=True).then_inc(a_m, 1)

                def inverses(g, m):
                    u = m % NPT
                    dve.wait_ge(a_e, at(g, NM, MB[l] + m + 1))
                    dve.tensor_reduce(sm[:, u, :], pt[u], AX.X, ALU.add).then_inc(a_sm, 1)
                    dve.wait_ge(a_sm, at(g, NM, MB[l] + m + 1))
                    dve.reciprocal(rc[:, u, :], sm[:, u, :]).then_inc(a_r, 1)

                def copy_second(g, p):
                    if p >= 0:
                        dve.wait_ge(a_t, at(g, NP, PB[l] + p + 1))
                        dve.tensor_copy(prob[(p // nh % 2) * hg + 2 * (p % nh) + 1][:, :, :], ps[0:CK, 4:6, :]).then_inc(a_td, 1)

                def add_up(g, b):
                    if b >= 0:
                        dve.wait_ge(a_y, at(g, B, OB[l] + b + 1))
                        dve.wait_ge(a_acc, at(g, B, OB[l] + b))
                        dve.tensor_tensor(acc[:, bsl(b)], acc[:, bsl(b)], ps[:, 7, :], ALU.add).then_inc(a_acc, 1)

                def heads(g):
                    for m in range(NM):
                        b, h, k = m // TB // nh, m // TB % nh, m % TB
                        inverses(g, m)
                        maxima(g, m + 2)
                        if k == 0:
                            copy_second(g, m // TB - 1)
                            if h == 0:
                                add_up(g, b - 2)

                def between(g, following):
                    if g:
                        copy_second(g, NP - 1)
                    if following:
                        for n in range(4):
                            low(following, n)
                    if g:
                        add_up(g, B - 2)
                    if following:
                        for n in range(4, NJ - 2):
                            low(following, n)
                    if g:
                        add_up(g, B - 1)
                    if following:
                        for n in range(NJ - 2, NJ):
                            low(following, n)
                        maxima(following, 0)
                        maxima(following, 1)

                between(None, (0, 0))
                with dve.Fori(0, a["ng"] - 1) as i:
                    heads((i, 0))
                    between((i, 0), (i, 1))
                last = (a["ng"] - 1, 0)
                heads(last)
                between(last, None)
                dve.wait_ge(a_acc, OB[l + 1])
                for b in range(B):
                    if l == 1:
                        dve.tensor_scalar(acc[:, bsl(b)], acc[:, bsl(b)], bo1[:, 0:1], None, ALU.add).then_inc(a_fin, 1)
                    elif l == 2:
                        dve.wait_ge(gate_ok, 1)
                        dve.tensor_scalar(acc[:, bsl(b)], acc[:, bsl(b)], bo2[:, 0:1], tgate[:, 0:1], ALU.add, ALU.mult).then_inc(a_fin, 1)

            def wide(ap):
                return ap.rearrange("p (n a) -> p n a", a=1).broadcast_to([P, NT, E])

            def routing(l):
                f = FFN[l]
                dve.wait_ge(f_lg, l + 1)
                logits = ps[:, 5, 0:NT * E].rearrange("p (n e) -> p n e", e=E)
                if f["bg"]:
                    row = bg[:, {0: 0, 3: 1}[l]:{0: 0, 3: 1}[l] + 1, :].broadcast_to([P, NT, E])
                    link(dve.tensor_tensor(lg[:, :, :], logits, row, ALU.add))
                else:
                    link(dve.tensor_copy(lg[:, :, :], logits))
                for n in range(NT):
                    ins = dve.max(m8[:, n, :], lg[:, n, :])
                link(ins)
                for n in range(NT):
                    ins = dve.max_index(ix8[:, n, :], m8[:, n, :], lg[:, n, :])
                link(ins)
                link(dve.tensor_copy(ixf[:, :, :], ix8[:, :, 0:2]))
                ex = iota8[:, :].rearrange("p (a e) -> p a e", a=1).broadcast_to([P, NT, E])
                for k in range(1 if l == 1 else 2):
                    link(dve.tensor_tensor(oh[:, k, :, :], ex, ixf[:, :, k:k + 1].broadcast_to([P, NT, E]), ALU.is_equal))
                if l == 1:
                    dve.tensor_tensor(dexp[:, :, :], lg[:, :, :], m8[:, :, 0:1].broadcast_to([P, NT, E]), ALU.subtract).then_inc(f_d, 1)
                    link(dve.memset(cum[0][:, 0:1, :], 0.0))
                    link(dve.tensor_copy(cum[0][:, 1:NT, :], oh[:, 0, 0:NT - 1, :]))
                    k, d = 0, 1
                    while d < NT:
                        dve.tensor_copy(cum[1 - k][:, 0:d, :], cum[k][:, 0:d, :])
                        link(dve.tensor_tensor(cum[1 - k][:, d:NT, :], cum[k][:, d:NT, :], cum[k][:, 0:NT - d, :], ALU.add))
                        k, d = 1 - k, 2 * d
                    dve.sem_inc(f_oh, 1)
                    dve.wait_ge(f_e, l + 1)
                    link(dve.tensor_reduce(r_s[:, :], dexp[:, :, :], AX.X, ALU.add))
                    link(dve.reciprocal(r_w[:, 0, :], r_s[:, :]))
                    dve.wait_ge(f_rank, 1)
                    link(dve.tensor_scalar(comb2[:, :, :], ps[:, 6, 0:NT * E].rearrange("p (n e) -> p n e", e=E),
                                           float(CAPACITY), None, ALU.is_le))
                    link(dve.tensor_tensor(comb2[:, :, :], comb2[:, :, :], oh[:, 0, :, :], ALU.mult))
                    dve.tensor_tensor(comb[:, :, :], comb2[:, :, :], wide(r_w[:, 0, :]), ALU.mult).then_inc(f_comb, 1)
                else:
                    dve.tensor_tensor(r_d[:, :].rearrange("p (n a) -> p n a", a=1), m8[:, :, 1:2], m8[:, :, 0:1], ALU.subtract).then_inc(f_d, 1)
                    dve.wait_ge(f_e, l + 1)
                    link(dve.tensor_scalar(r_s[:, :], r_e[:, :], 1.0, None, ALU.add))
                    link(dve.reciprocal(r_w[:, 0, :], r_s[:, :]))
                    link(dve.tensor_tensor(r_w[:, 1, :], r_w[:, 0, :], r_e[:, :], ALU.mult))
                    link(dve.tensor_tensor(comb[:, :, :], oh[:, 0, :, :], wide(r_w[:, 0, :]), ALU.mult))
                    link(dve.tensor_tensor(comb2[:, :, :], oh[:, 1, :, :], wide(r_w[:, 1, :]), ALU.mult))
                    dve.tensor_tensor(comb[:, :, :], comb[:, :, :], comb2[:, :, :], ALU.add).then_inc(f_comb, 1)
                if not f["b2"]:
                    dve.memset(acc[:, :], 0.0).then_inc(f_init2, 1)
                for b in range(B):
                    dve.wait_ge(f_xh, B * l + b + 1)
                    dve.tensor_tensor(x_lo[:, bsl(b)], xnT[:, bsl(b)], x_hi[:, bsl(b)].bitcast(F32), ALU.subtract).then_inc(f_xl, 1)
                for b in range(B):
                    dve.wait_ge(f_cf, B * l + b + 1)
                    link(dve.tensor_copy(cT[0:E, bsl(b)], cTf[:, bsl(b)]))
                    dve.tensor_tensor(cT[LO:LO + E, bsl(b)], cTf[:, bsl(b)], cT[0:E, bsl(b)].bitcast(F32), ALU.subtract).then_inc(f_c, 1)

            def ffn(l):
                f = FFN[l]
                n = f["nc"]
                routing(l)
                if f["b2"]:
                    dve.wait_ge(f_init, B * IB[l] + B)
                else:
                    dve.wait_ge(f_init2, 1)
                def slots(e, u):
                    for slot, base in ((b1_slot[u], {0: 0, 1: 64, 2: None, 3: 96}[l]), (b0_slot[u], 32 if f["w0"] else None)):
                        if base is not None:
                            dve.tensor_copy(slot[:, :].rearrange("p (a c) -> p a c", a=1),
                                            biasT[:, base:base + (E + 1) * n].rearrange("p (e c) -> p e c", c=n)[:, one(e), :])
                    dve.tensor_copy(sel_slot[u][:, :].rearrange("p (a c) -> p a c", a=1), sel_all[:, one(e), :]).then_inc(f_sel, 1)

                slots(0, 0)
                with dve.Fori(0, E // 2) as i:
                    def wait_unit(sem_, A):
                        dve.wait_ge(sem_, i * (2 * B * n) + A)

                    def y_acc(k):
                        K = KB[l] + k
                        dve.wait_ge(f_y, i * (2 * B) + (K + 1))
                        dve.wait_ge(f_yd, i * (2 * B) + K)
                        dve.tensor_copy(yw[:, :], ps[:, 6 + k % 2, :]).then_inc(f_ym, 1)
                        dve.wait_ge(f_ym, i * (4 * B) + 2 * K)
                        dve.tensor_tensor(yw[:, :], ps[:, 4 + k % 2, :], yw[:, :], ALU.mult).then_inc(f_ym, 1)
                        dve.wait_ge(f_ym, i * (4 * B) + (2 * K + 1))
                        dve.tensor_tensor(acc[:, bsl(k % B)], acc[:, bsl(k % B)], yw[:, :], ALU.add).then_inc(f_yd, 1)

                    def low(k, c):
                        hi, lo = h_p[k % 2]
                        wait_unit(f_hh if f["w0"] else f_a, AB[l] + n * k + c + 1)
                        dve.tensor_tensor(lo[:, c, :], h_f[:, c % 2, :], hi[:, c, :].bitcast(F32), ALU.subtract).then_inc(f_hl, 1)

                    slots(i * 2 + 1, 1)
                    for k in range(2 * B):
                        if f["w0"] and k % B == 0:
                            dve.wait_ge(f_sel, i * 2 + ((E + 1) * l + k // B + 1))
                        for c in range(n):
                            if f["w0"]:
                                A = AB[l] + n * k + c
                                wait_unit(f_a, A + 1)
                                wait_unit(f_hl, A - c if k == 0 and c < 2 else A - 1)
                                dve.scalar_tensor_tensor(out=h_f[:, c % 2, :], in0=ps[:, 2 + c % 2, :], scalar=b0_slot[k // B][:, c:c + 1],
                                                         in1=gS[c % 2][:, :], op0=ALU.add, op1=ALU.mult).then_inc(f_hd, 1)
                                if c:
                                    low(k, c - 1)
                            else:
                                low(k, c)
                        if f["w0"]:
                            low(k, n - 1)
                        if k:
                            y_acc(k - 1)
                        if k == B:
                            slots(i * 2 + 2, 0)
                    y_acc(2 * B - 1)

            j = 0
            for s in range(N_SUB):
                layer_norm(j, x_tok, scaled=(s == 2), refresh=s - 1 if s else None)
                j += 1
                if s == 4:
                    layer_norm(j, xn_tok)
                    j += 1
                if s % 2:
                    ffn(s // 2)
                elif s == 0:
                    attention0()
                else:
                    attention(s // 2)
            for b in range(B):
                finish(N_SUB - 1, b)

        @block.tensor
        def _(pe):
            start_at_one(pe, (f_h, f_y, a_pj, a_s, a_t, a_pv, a_y))

            mm = pe.matmul
            pe.wait_ge(const_g, 6)
            pe.wait_ge(in_ctx, 16)
            for m in range(2):
                for n in range(4):
                    last = pe.transpose(ps[:, m, n * CK:(n + 1) * CK], ctx_tok[:, 4 * m + n, :], ident[0:CK, 0:CK])
                last.then_inc(ctxT_ps, 1)
            pe.wait_ge(in_ffn, 16 * 13)
            pe.transpose(ps[:, 2, 0:P], bias_rows[:, :], ident[:, :]).then_inc(bias_ps, 1)

            def xT(s):
                for b in range(B):
                    pe.wait_ge(ln_ok, B * (s + (1 if s >= 4 else 0)) + b + 1)
                    if b == 0 and s:
                        pe.wait_ge(xT_ok, B * s)
                    if s == 0:
                        pe.wait_ge(ctxT_ok, 2)
                        pe.wait_ge(bias_ok, 1)
                    for k in range(TB):
                        last = pe.transpose(ps[:, b, k * P:(k + 1) * P], xn_tok[:, b * TB + k, :], ident[:, :])
                    last.then_inc(xT_ps, 1)

            def finish(s, sem_, base):
                for b in range(B):
                    pe.wait_ge(sem_, base + (min(b + 3, B) if s % 2 else B))
                    if b >= 2:
                        pe.wait_ge(x_new, B * s + b - 1)
                    for k in range(TB):
                        last = pe.transpose(ps[:, 6 + b % 2, k * P:(k + 1) * P], acc[:, b * S + k * P:b * S + (k + 1) * P], ident[:, :])
                    last.then_inc(accT_ps, 1)

            def attention0():
                pe.wait_ge(z_pre, 1)
                pe.wait_ge(const_v, 1)
                for n in range(B * KC):
                    last = mm(ps[0:CK, 4, n:n + 1], ctxT[:, n * CK:(n + 1) * CK], w_sim[:, 1:2], start=True, stop=True)
                last.then_inc(z_cps, 1)
                pe.wait_ge(xT_ok, B)

                def similarities(b):
                    keys = slice(b * SK, (b + 1) * SK)
                    wait(pe, z_mx, b)
                    for k in range(TB):
                        mm(ps[:, k, 0:SK], xnT[:, b * S + k * P:b * S + (k + 1) * P], keys0[:, keys], start=True, stop=False)
                        last = mm(ps[:, k, 0:SK], w2rep[:, :], ctxT[:, keys], start=False, stop=True)
                    last.then_inc(z_sc, 1)

                def maxima_row(b):
                    pe.wait_ge(z_mx, b + 1)
                    wait(pe, z_bm, b)
                    for k in range(TB):
                        last = pe.transpose(ps[0:1, 6, k * P:(k + 1) * P], mx0b[:, b * TB + k:b * TB + k + 1], ident[:, :])
                    last.then_inc(z_mT, 1)

                similarities(0)
                for b in range(B):
                    if b + 1 < B:
                        similarities(b + 1)
                    maxima_row(b)
                pe.wait_ge(z_bm, B)
                mm(ps[:, 7, 0:B], ones[0:1, :], bmax[:, :], start=True, stop=True).then_inc(z_bps, 1)
                pe.wait_ge(z_eb, B)
                for b in range(B):
                    for k in range(TB):
                        mm(ps[:, 7, 8 + b:9 + b], ones[:, :], eb[:, b * TB + k:b * TB + k + 1], start=(k == 0), stop=(k == TB - 1))
                    for k in range(TB):
                        last = mm(ps[:, 7, 16 + b:17 + b], xn_tok[:, b * TB + k, :], eb[:, b * TB + k:b * TB + k + 1], start=(k == 0), stop=(k == TB - 1))
                last.then_inc(z_hps, 1)

                def scores(b):
                    wait(pe, z_p, KC * b)
                    for c in range(KC):
                        n = b * KC + c
                        bank = ps[0:CK, c, :]
                        mm(bank, keys0[:, n * CK:(n + 1) * CK], xnT[:, bsl(b)], start=True, stop=False)
                        last = mm(bank, ones_r[:, :], nm0[:, bsl(b)], start=False, stop=True)
                    last.then_inc(z_s, 1)

                def features_out(b):
                    pe.wait_ge(z_f, b + 1)
                    if b >= 2:
                        pe.wait_ge(z_acc, b - 1)
                    for k, feat in enumerate((xnT[:, bsl(b)], hqT[b % 2], xhq[b % 2], xhcs[b % 2])):
                        last = mm(ps[:, 6 + b % 2, :], w_qv[:, k, :], feat, start=(k == 0), stop=(k == 3))
                    last.then_inc(z_y, 1)

                pe.wait_ge(z_nm, B)
                pe.wait_ge(z_c, 1)
                pe.wait_ge(z_mx, B)
                scores(0)
                pe.wait_ge(z_hc, 1)
                for b in range(B):
                    u = b % 2
                    pe.wait_ge(z_p, KC * (b + 1))
                    if b >= 2:
                        pe.wait_ge(z_f, b - 1)
                    for c in range(KC):
                        mm(ps[:, 2 + 2 * u, :], ctx_tok[:, b * KC + c, :], prob[u][:, c, :], start=(c == 0), stop=(c == KC - 1))
                    for c in range(KC):
                        last = mm(ps[:, 3 + 2 * u, :], ones[0:CK, :], prob[u][:, c, :], start=(c == 0), stop=(c == KC - 1))
                    last.then_inc(z_o, 1)
                    if b + 1 < B:
                        scores(b + 1)
                    if b:
                        features_out(b - 1)
                features_out(B - 1)

            def attention(l):
                a = ATT[l]
                hg, rows, nh = a["hg"], a["rows"], a["nh"]
                NM, NP = B * TB * nh, B * nh
                pe.wait_ge(xT_ok, B * (2 * l + 1))
                if l == 1:
                    pe.wait_ge(mb_ok, B)

                def proj(g, n):
                    kind, b = JOBS[n]
                    if n == 0:
                        pe.wait_ge(a_w, at(g, 3 * 16, 3 * 16 * GB[l]))
                    if n < 4:
                        pe.wait_ge(a_ta, at(g, NP, PB[l]))
                        pe.wait_ge(a_td, at(g, NP, PB[l]))
                    else:
                        pe.wait_ge(a_pd, at(g, NJ, JB[l] + n - 3))
                    if kind == "q":
                        last = mm(ps[:, 2 + n % 4, :], wq_s[:, :], xnT[:, bsl(b)], start=True, stop=True)
                    elif kind == "k":
                        last = mm(ps[:, 2 + n % 4, 0:2 * SK], wk_s[:, :], ctxT[:, b * 2 * SK:(b + 1) * 2 * SK], start=True, stop=True)
                    else:
                        for i in range(4):
                            last = mm(ps[0:CK, 2 + n % 4, i * P:(i + 1) * P], ctxT[:, (4 * b + i) * CK:(4 * b + i + 1) * CK], wv_s[:, :], start=True, stop=True)
                    last.then_inc(a_pj, 1)

                def scores(g, m):
                    if m >= NM:
                        return
                    b, h, k = m // TB // nh, m // TB % nh, m % TB
                    tile, keys = b * TB + k, slice(b * SK, (b + 1) * SK)
                    if m == 0:
                        pe.wait_ge(a_pd, at(g, NJ, JB[l] + 2))
                    pe.wait_ge(a_e, at(g, NM, MB[l] + max(m - 1, 0)))
                    q = [q_s[:, j, tile * P:(tile + 1) * P] for j in range(2)]
                    bank = ps[:, m % 2, 0:2 * SK].rearrange("p (h s) -> p h s", h=2)
                    if l == 1:
                        mm(bank, q[0], kz[:, 2 * h:2 * h + 2, keys], start=True, stop=False)
                        last = mm(bank, ident_bf[:, :], mask_bf[:, tile:tile + 1, :].broadcast_to([P, 2, SK]), start=False, stop=True)
                    else:
                        mm(bank, q[0], k_hi[:, :, keys], start=True, stop=False)
                        mm(bank, q[0], k_lo[:, :, keys], start=False, stop=False)
                        last = mm(bank, q[1], k_hi[:, :, keys], start=False, stop=True)
                    last.then_inc(a_s, 1)

                def transposes(g, m):
                    p, k = m // TB, m % TB
                    if m == 0:
                        pe.wait_ge(a_pd, at(g, NJ, JB[l] + NJ))
                    elif k == 0:
                        pe.wait_ge(a_ta, at(g, NP, PB[l] + p))
                        pe.wait_ge(a_td, at(g, NP, PB[l] + p))
                    pe.wait_ge(a_z, at(g, NM, MB[l] + m + 1))
                    for j in range(2):
                        for c in range(KC):
                            last = pe.transpose(ps[0:CK, 2 + 2 * j + c, k * P:(k + 1) * P], pt[m % NPT][:, j, c * CK:(c + 1) * CK], ident[:, :])
                    if k == TB - 1:
                        last.then_inc(a_t, 1)

                def values(g, b, c):
                    if b < 0:
                        return
                    if c == 0:
                        pe.wait_ge(a_ta, at(g, NP, PB[l] + (b + 1) * nh))
                        pe.wait_ge(a_td, at(g, NP, PB[l] + (b + 1) * nh))
                        pe.wait_ge(a_o, at(g, B, OB[l] + b))
                    for j in range(hg):
                        r = slice(rows * j, rows * j + rows)
                        last = mm(ps[r, 6, :], v[:, b * KC + c, r], prob[(b % 2) * hg + j][:, c, :], start=(c == 0), stop=(c == KC - 1))
                    if c == KC - 1:
                        last.then_inc(a_pv, 1)

                def project(g, b):
                    if b >= 0:
                        pe.wait_ge(a_o, at(g, B, OB[l] + b + 1))
                        pe.wait_ge(a_wo, at(g, 16, 16 * GB[l]))
                        pe.wait_ge(a_acc, at(g, B, OB[l] + b))
                        mm(ps[:, 7, :], wo_s[:, :], oT[:, :], start=True, stop=True).then_inc(a_y, 1)

                def heads(g):
                    for m in range(NM):
                        b, h, k = m // TB // nh, m // TB % nh, m % TB
                        if h == 0 and k == 0:
                            project(g, b - 2)
                        scores(g, m + 3)
                        transposes(g, m)
                        if h == 0 and k < KC:
                            values(g, b - 1, k)

                def between(g, following):
                    if g:
                        project(g, B - 2)
                    if following:
                        for n in range(4):
                            proj(following, n)
                    if g:
                        for c in range(KC):
                            values(g, B - 1, c)
                    if following:
                        for n in range(4, NJ - 2):
                            proj(following, n)
                    if g:
                        project(g, B - 1)
                    if following:
                        for n in range(NJ - 2, NJ):
                            proj(following, n)
                            if n >= NJ - 2:
                                scores(following, n - (NJ - 2))
                        scores(following, 2)

                between(None, (0, 0))
                with pe.Fori(0, a["ng"] - 1) as i:
                    heads((i, 0))
                    between((i, 0), (i, 1))
                last_g = (a["ng"] - 1, 0)
                heads(last_g)
                between(last_g, None)

            def ffn(l):
                f = FFN[l]
                n = f["nc"]
                pe.wait_ge(xT_ok, B * (2 * l + 2))
                for k in range(NT):
                    last = mm(ps[:, 5, k * E:(k + 1) * E], xnT[:, k * P:(k + 1) * P], wg[:, l, :], start=True, stop=True)
                last.then_inc(f_lg, 1)
                if l == 1:
                    pe.wait_ge(f_oh, 1)
                    pe.wait_ge(x_new, B * (2 * l + 1))
                    mm(ps[:, 6, 0:NT * E], tri[:, :], oh[:, 0, :, :], start=True, stop=False)
                    mm(ps[:, 6, 0:NT * E], ones[:, :], cum[0][:, :, :], start=False, stop=True).then_inc(f_rank, 1)
                pe.wait_ge(f_comb, l + 1)
                for b in range(B):
                    if b >= 2:
                        pe.wait_ge(f_cf, B * l + b - 1)
                    for k in range(TB):
                        last = pe.transpose(ps[0:E, 6 + b % 2, k * P:(k + 1) * P], comb[:, b * TB + k, :], ident[:, :])
                    last.then_inc(f_cps, 1)
                if f["b2"]:
                    for b in range(B):
                        pe.wait_ge(f_cf, B * l + b + 1)
                        if b >= 2:
                            pe.wait_ge(f_init, B * IB[l] + b - 1)
                        mm(ps[:, 4 + b % 2, :], b2[:, IB[l], :], cTf[:, bsl(b)], start=True, stop=True).then_inc(f_ips, 1)
                    pe.wait_ge(f_init, B * IB[l] + B)
                pe.wait_ge(f_cf, B * l + B)
                pe.wait_ge(f_c, B * l + B)
                pe.wait_ge(f_xl, B * l + B)

                def product(bank, w, x, first=True, last=True):
                    mm(bank, w[0], x[0], start=first, stop=False)
                    mm(bank, w[0], x[1], start=False, stop=False)
                    return mm(bank, w[1], x[0], start=False, stop=last)

                with pe.Fori(0, E // 2) as i:
                    def hidden(k):
                        u, b, K = k // B, k % B, KB[l] + k
                        if b == 0:
                            pe.wait_ge(f_ws[u], i + (l * E // 2 + 1))
                            pe.wait_ge(f_sel, i * 2 + ((E + 1) * l + u + 1))
                        x = (x_hi[:, bsl(b)], x_lo[:, bsl(b)])
                        for c in range(n):
                            A = AB[l] + n * k + c
                            cs = slice(c * P, (c + 1) * P)
                            w1 = [w[:, cs] for w in w1_p[u]]
                            if f["w0"]:
                                back = A - c if k == 0 and c < 2 else A - 1
                                wait(pe, f_a, i * (2 * B * n) + back)
                                product(ps[:, c % 2, :], w1, x)
                                wait(pe, f_hd, i * (2 * B * n) + back)
                                product(ps[:, 2 + c % 2, :], [w[:, cs] for w in w0_p[u]], x).then_inc(f_h, 1)
                            else:
                                wait(pe, f_a, i * (2 * B * n) + (A - c if k == 0 else A - n + 1))
                                product(ps[:, c, :], w1, x).then_inc(f_h, 1)

                    def down(k):
                        u, K = k // B, KB[l] + k
                        wait(pe, f_yd, i * (2 * B) + (K if k == 0 else K - 1))
                        mm(ps[:, 6 + k % 2, :], sel_slot[u][:, :], cT[:, bsl(k % B)], start=True, stop=True)
                        for c in range(n):
                            pe.wait_ge(f_hl, i * (2 * B * n) + (AB[l] + n * k + c + 1))
                            last = product(ps[:, 4 + k % 2, :], [w[:, c * P:(c + 1) * P] for w in w2_p[u]],
                                           [h[:, c, :] for h in h_p[k % 2]], first=(c == 0), last=(c == n - 1))
                        last.then_inc(f_y, 1)

                    for k in range(2 * B):
                        hidden(k)
                        if k:
                            down(k - 1)
                    down(2 * B - 1)

            for s in range(N_SUB):
                l = s // 2
                xT(s)
                if s % 2:
                    ffn(l)
                    finish(s, f_yd, KB[l + 1] - B)
                elif s == 0:
                    attention0()
                    finish(0, z_acc, 0)
                else:
                    attention(l)
                    finish(s, *((a_fin, B * (l - 1)) if l < 3 else (a_acc, OB[4] - B)))


NL_FFN = 4
N_SUB = 8
IB = {0: 0, 1: 1, 3: 2}


def kernel(**inputs):
    import numpy as _np
    import concourse.bacc as _bacc
    from concourse.bass_utils import run_bass_kernel_spmd as _run

    nc = _bacc.Bacc("TRN2", target_bir_lowering=False, num_devices=1)
    arrays, args = {}, {}
    for name, value in inputs.items():
        a = _np.ascontiguousarray(value)
        arrays[f"in_{name}"] = a
        args[name] = nc.dram_tensor(f"in_{name}", a.shape, mybir.dt.from_np(a.dtype), kind="ExternalInput").ap()
    shape = arrays["in_x"].shape
    out = nc.dram_tensor("out_0", shape, mybir.dt.float32, kind="ExternalOutput").ap()
    xattn_moe_stack(nc, args, out)
    r = _run(nc, [arrays], core_ids=[0])
    return r.results[0]["out_0"]
```
